# Optimizing a Trainium2 kernel written in Bass

```python
import numpy as np
import jax
import jax.numpy as jnp

def _softmax(x, axis=-1):
    return jax.nn.softmax(x, axis=axis)

def _gelu(x):
    return jax.nn.gelu(x, approximate=True)

def _silu(x):
    return jax.nn.silu(x)

def _sigmoid(x):
    return jax.nn.sigmoid(x)

def _layernorm(x, axis=-1, eps=1e-05):
    m = jnp.mean(x, axis=axis, keepdims=True)
    v = jnp.var(x, axis=axis, keepdims=True)
    return (x - m) / jnp.sqrt(v + eps)

def _scatter_add(tgt, idx, src, axis=0):
    return tgt.at[idx].add(src)

def _segment_sum(src, seg, n):
    return jax.ops.segment_sum(src, seg, n)
kernel_name = 'mk_recurrent_d4_jaxref_r8_542663'

def setup_inputs(seed: int=0):
    np.random.seed(seed)
    _w = jnp.asarray

    def _L0_attn_setup():
        import jax, jax.numpy as jnp
        import numpy as np
        D_MODEL = 128
        N_HEADS = 16
        D_HEAD = D_MODEL // N_HEADS
        key = jax.random.key(seed)
        ks = jax.random.split(key, 5)
        B, S = (1, 256)
        x = jax.random.normal(ks[0], (B, S, D_MODEL), dtype=jnp.float32)
        lim = float(np.sqrt(6.0 / (2 * D_MODEL)))

        def w(k):
            return jax.random.uniform(k, (D_MODEL, D_MODEL), jnp.float32, -lim, lim)
        return {'x': x, 'Wq': w(ks[1]), 'bq': jnp.zeros((D_MODEL,), jnp.float32), 'Wk': w(ks[2]), 'bk': jnp.zeros((D_MODEL,), jnp.float32), 'Wv': w(ks[3]), 'bv': jnp.zeros((D_MODEL,), jnp.float32), 'Wo': w(ks[4]), 'bo': jnp.zeros((D_MODEL,), jnp.float32)}
    _L0_attn_in = _L0_attn_setup()

    def _L0_ffn_setup():
        import jax, jax.numpy as jnp
        import numpy as np
        DIM = 128
        HIDDEN = 384
        SCALE = 1.0 / 127.0

        def _dequant(w_int, dtype):
            return w_int.astype(dtype) * jnp.asarray(SCALE, dtype)
        key = jax.random.key(seed)
        k_x, k_g, k_u, k_d = jax.random.split(key, 4)
        x = jax.random.normal(k_x, (4, 256, DIM), dtype=jnp.float32)
        w_gate = jax.random.randint(k_g, (HIDDEN, DIM), -127, 128, dtype=jnp.int32)
        w_up = jax.random.randint(k_u, (HIDDEN, DIM), -127, 128, dtype=jnp.int32)
        w_down = jax.random.randint(k_d, (DIM, HIDDEN), -127, 128, dtype=jnp.int32)
        return {'x': x, 'w_gate': w_gate, 'w_up': w_up, 'w_down': w_down}
    _L0_ffn_in = _L0_ffn_setup()

    def _L1_attn_setup():
        import math
        import jax, jax.numpy as jnp
        import numpy as np
        DIM = 128
        N_HEADS = 16
        HEAD_DIM = DIM // N_HEADS
        SEQ_LEN = 256
        BASE = 10000.0
        EPS = 1e-05

        def rope_cache(seq_len, dim):
            pos = jnp.arange(seq_len, dtype=jnp.float32)[:, None]
            di = jnp.arange(0, dim, 2, dtype=jnp.float32) / dim
            theta = pos * jnp.exp(-di * math.log(BASE))
            cos = jnp.repeat(jnp.cos(theta), 2, axis=1)
            sin = jnp.repeat(jnp.sin(theta), 2, axis=1)
            return (cos, sin)

        def rotate_half(x):
            x1 = x[..., ::2]
            x2 = x[..., 1::2]
            return jnp.concatenate((-x2, x1), axis=-1)

        def layernorm(x, gamma, beta):
            mu = jnp.mean(x, axis=-1, keepdims=True)
            var = jnp.var(x, axis=-1, keepdims=True)
            return (x - mu) * jax.lax.rsqrt(var + EPS) * gamma + beta
        key = jax.random.key(seed)
        ks = jax.random.split(key, 7)
        s = 1.0 / math.sqrt(DIM)
        return {'x': jax.random.normal(ks[0], (2, SEQ_LEN, DIM), dtype=jnp.float32), 'Wq': jax.random.normal(ks[1], (DIM, DIM), dtype=jnp.float32) * s, 'Wk': jax.random.normal(ks[2], (DIM, DIM), dtype=jnp.float32) * s, 'Wv': jax.random.normal(ks[3], (DIM, DIM), dtype=jnp.float32) * s, 'q_gamma': jnp.ones((HEAD_DIM,), jnp.float32), 'q_beta': jnp.zeros((HEAD_DIM,), jnp.float32), 'k_gamma': jnp.ones((HEAD_DIM,), jnp.float32), 'k_beta': jnp.zeros((HEAD_DIM,), jnp.float32), 'Wo': jax.random.normal(ks[4], (DIM, DIM), dtype=jnp.float32) * s, 'bo': jnp.zeros((DIM,), jnp.float32)}
    _L1_attn_in = _L1_attn_setup()

    def _L1_ffn_setup():
        import jax, jax.numpy as jnp
        import numpy as np
        B, S, D, F, E = (8, 128, 128, 512, 8)
        EPS = 1e-05
        key = jax.random.key(seed)
        ks = jax.random.split(key, 4)
        s = 0.02
        return {'input_features': jax.random.normal(ks[0], (B, S, D), jnp.float32), 'centroids': jax.random.normal(ks[1], (E, D), jnp.float32) * 0.1, 'ln_g': jnp.ones((E, D), jnp.float32), 'ln_b': jnp.zeros((E, D), jnp.float32), 'w1': jax.random.normal(ks[2], (E, D, F), jnp.float32) * s, 'b1': jnp.zeros((E, F), jnp.float32), 'w2': jax.random.normal(ks[3], (E, F, D), jnp.float32) * s, 'b2': jnp.zeros((E, D), jnp.float32)}
    _L1_ffn_in = _L1_ffn_setup()

    def _L2_attn_setup():
        import jax, jax.numpy as jnp
        import numpy as np
        D_MODEL, N_HEADS, N_KV, HEAD_DIM, D_LAT = (128, 8, 2, 128, 32)
        N_REP = N_HEADS // N_KV
        B, T = (2, 256)
        key = jax.random.key(seed)
        ks = jax.random.split(key, 8)
        s = lambda fan_in: 1.0 / np.sqrt(fan_in)
        return {'x': jax.random.normal(ks[0], (B, T, D_MODEL), jnp.float32), 'wq': jax.random.normal(ks[1], (D_MODEL, N_HEADS * HEAD_DIM), jnp.float32) * s(D_MODEL), 'wk_down': jax.random.normal(ks[2], (D_MODEL, N_KV * D_LAT), jnp.float32) * s(D_MODEL), 'wv_down': jax.random.normal(ks[3], (D_MODEL, N_KV * D_LAT), jnp.float32) * s(D_MODEL), 'wk_up': jax.random.normal(ks[4], (D_LAT, HEAD_DIM), jnp.float32) * s(D_LAT), 'wv_up': jax.random.normal(ks[5], (D_LAT, HEAD_DIM), jnp.float32) * s(D_LAT), 'wo': jax.random.normal(ks[6], (N_HEADS * HEAD_DIM, D_MODEL), jnp.float32) * s(N_HEADS * HEAD_DIM)}
    _L2_attn_in = _L2_attn_setup()

    def _L2_ffn_setup():
        import jax, jax.numpy as jnp
        import numpy as np
        H = 128
        E = 32
        I = 64
        TOP_K = 6
        IS = 128
        NORM_MIN = 1e-12
        B, S = (2, 128)
        key = jax.random.key(seed)
        ks = jax.random.split(key, 8)
        sc = 0.02
        return {'hidden_states': jax.random.normal(ks[0], (B, S, H), jnp.float32), 'router_weight': jax.random.normal(ks[1], (E, H), jnp.float32) * sc, 'e_score_bias': jnp.zeros((E,), jnp.float32), 'gate_up_proj': jax.random.normal(ks[2], (E, 2 * I, H), jnp.float32) * sc, 'down_proj': jax.random.normal(ks[3], (E, H, I), jnp.float32) * sc, 'shared_gate_w': jax.random.normal(ks[4], (IS, H), jnp.float32) * sc, 'shared_up_w': jax.random.normal(ks[5], (IS, H), jnp.float32) * sc, 'shared_down_w': jax.random.normal(ks[6], (H, IS), jnp.float32) * sc}
    _L2_ffn_in = _L2_ffn_setup()

    def _L3_attn_setup():
        import jax, jax.numpy as jnp
        import numpy as np
        EPS = 1e-12
        ATTEND_SCALE = 8.0

        def _l2norm(t, axis=-1):
            n = jnp.sqrt(jnp.sum(t * t, axis=axis, keepdims=True))
            return t / jnp.maximum(n, EPS)

        def _reference_tuple_inner(x, gamma, w_qkv, temperature, w_out):
            b, n, dim = x.shape
            heads = temperature.shape[0]
            dim_head = w_qkv.shape[1] // (3 * heads)
            xn = _l2norm(x) * dim ** 0.5 * gamma
            qkv = xn @ w_qkv
            qkv = qkv.reshape(b, n, 3, heads, dim_head).transpose(2, 0, 3, 4, 1)
            q, k, v = (qkv[0], qkv[1], qkv[2])
            orig_v = v
            q = _l2norm(q) * jnp.exp(temperature)
            k = _l2norm(k)
            sim = jnp.einsum('bhdn,bhen->bhde', q, k) * ATTEND_SCALE
            attn = jax.nn.softmax(sim, axis=-1)
            out = jnp.einsum('bhde,bhen->bhdn', attn, v)
            out = out.transpose(0, 3, 1, 2).reshape(b, n, heads * dim_head) @ w_out
            return (out, orig_v)
        key = jax.random.key(seed)
        k1, k2, k3, k4 = jax.random.split(key, 4)
        b, n, dim = (4, 1024, 128)
        heads, dim_head = (16, 64)
        dim_inner = heads * dim_head
        x = jax.random.normal(k1, (b, n, dim), dtype=jnp.float32)
        gamma = jnp.ones((dim,), dtype=jnp.float32)
        w_qkv = jax.random.normal(k2, (dim, 3 * dim_inner), dtype=jnp.float32) * dim ** (-0.5)
        temperature = jnp.zeros((heads, 1, 1), dtype=jnp.float32)
        w_out = jax.random.normal(k3, (dim_inner, dim), dtype=jnp.float32) * dim_inner ** (-0.5)
        return {'x': x, 'gamma': gamma, 'w_qkv': w_qkv, 'temperature': temperature, 'w_out': w_out}
    _L3_attn_in = _L3_attn_setup()

    def _L3_ffn_setup():
        import jax, jax.numpy as jnp
        import numpy as np
        import math
        E = 16
        TOP_K = 2
        D = 128
        F = 512
        SH = 256
        key = jax.random.key(seed)
        ks = jax.random.split(key, 10)
        s = lambda k, shape, fan: jax.random.normal(k, shape, jnp.float32) / np.sqrt(fan)
        return {'x': jax.random.normal(ks[0], (32, 32, D), jnp.float32), 'gate_w': s(ks[1], (E, D), D), 'up_w': s(ks[2], (E, F, D), D), 'up_b': s(ks[3], (E, F), D), 'gw': s(ks[4], (E, F, D), D), 'gb': s(ks[5], (E, F), D), 'down_w': s(ks[6], (E, D, F), F), 'down_b': s(ks[7], (E, D), F), 'sh_gate_w': s(ks[8], (SH, D), D), 'sh_up_w': s(ks[9], (SH, D), D), 'sh_down_w': s(jax.random.fold_in(key, 11), (D, SH), SH)}
    _L3_ffn_in = _L3_ffn_setup()
    _d = {'L0_attn_x': _L0_attn_in['x'], 'L0_attn_Wq': _L0_attn_in['Wq'], 'L0_attn_bq': _L0_attn_in['bq'], 'L0_attn_Wk': _L0_attn_in['Wk'], 'L0_attn_bk': _L0_attn_in['bk'], 'L0_attn_Wv': _L0_attn_in['Wv'], 'L0_attn_bv': _L0_attn_in['bv'], 'L0_attn_Wo': _L0_attn_in['Wo'], 'L0_attn_bo': _L0_attn_in['bo'], 'L0_ffn_w_gate': _L0_ffn_in['w_gate'], 'L0_ffn_w_up': _L0_ffn_in['w_up'], 'L0_ffn_w_down': _L0_ffn_in['w_down'], 'L1_attn_Wq': _L1_attn_in['Wq'], 'L1_attn_Wk': _L1_attn_in['Wk'], 'L1_attn_Wv': _L1_attn_in['Wv'], 'L1_attn_q_gamma': _L1_attn_in['q_gamma'], 'L1_attn_q_beta': _L1_attn_in['q_beta'], 'L1_attn_k_gamma': _L1_attn_in['k_gamma'], 'L1_attn_k_beta': _L1_attn_in['k_beta'], 'L1_attn_Wo': _L1_attn_in['Wo'], 'L1_attn_bo': _L1_attn_in['bo'], 'L1_ffn_centroids': _L1_ffn_in['centroids'], 'L1_ffn_ln_g': _L1_ffn_in['ln_g'], 'L1_ffn_ln_b': _L1_ffn_in['ln_b'], 'L1_ffn_w1': _L1_ffn_in['w1'], 'L1_ffn_b1': _L1_ffn_in['b1'], 'L1_ffn_w2': _L1_ffn_in['w2'], 'L1_ffn_b2': _L1_ffn_in['b2'], 'L2_attn_wq': _L2_attn_in['wq'], 'L2_attn_wk_down': _L2_attn_in['wk_down'], 'L2_attn_wv_down': _L2_attn_in['wv_down'], 'L2_attn_wk_up': _L2_attn_in['wk_up'], 'L2_attn_wv_up': _L2_attn_in['wv_up'], 'L2_attn_wo': _L2_attn_in['wo'], 'L2_ffn_router_weight': _L2_ffn_in['router_weight'], 'L2_ffn_e_score_bias': _L2_ffn_in['e_score_bias'], 'L2_ffn_gate_up_proj': _L2_ffn_in['gate_up_proj'], 'L2_ffn_down_proj': _L2_ffn_in['down_proj'], 'L2_ffn_shared_gate_w': _L2_ffn_in['shared_gate_w'], 'L2_ffn_shared_up_w': _L2_ffn_in['shared_up_w'], 'L2_ffn_shared_down_w': _L2_ffn_in['shared_down_w'], 'L3_attn_gamma': _L3_attn_in['gamma'], 'L3_attn_w_qkv': _L3_attn_in['w_qkv'], 'L3_attn_temperature': _L3_attn_in['temperature'], 'L3_attn_w_out': _L3_attn_in['w_out'], 'L3_ffn_gate_w': _L3_ffn_in['gate_w'], 'L3_ffn_up_w': _L3_ffn_in['up_w'], 'L3_ffn_up_b': _L3_ffn_in['up_b'], 'L3_ffn_gw': _L3_ffn_in['gw'], 'L3_ffn_gb': _L3_ffn_in['gb'], 'L3_ffn_down_w': _L3_ffn_in['down_w'], 'L3_ffn_down_b': _L3_ffn_in['down_b'], 'L3_ffn_sh_gate_w': _L3_ffn_in['sh_gate_w'], 'L3_ffn_sh_up_w': _L3_ffn_in['sh_up_w'], 'L3_ffn_sh_down_w': _L3_ffn_in['sh_down_w']}
    _x0 = _d['L0_attn_x']
    _d['L0_attn_x'] = jax.random.normal(jax.random.fold_in(jax.random.key(seed), 1), (16, 256, 128), dtype=_x0.dtype)
    del _x0
    return _d

def reference(L0_attn_x, L0_attn_Wq, L0_attn_bq, L0_attn_Wk, L0_attn_bk, L0_attn_Wv, L0_attn_bv, L0_attn_Wo, L0_attn_bo, L0_ffn_w_gate, L0_ffn_w_up, L0_ffn_w_down, L1_attn_Wq, L1_attn_Wk, L1_attn_Wv, L1_attn_q_gamma, L1_attn_q_beta, L1_attn_k_gamma, L1_attn_k_beta, L1_attn_Wo, L1_attn_bo, L1_ffn_centroids, L1_ffn_ln_g, L1_ffn_ln_b, L1_ffn_w1, L1_ffn_b1, L1_ffn_w2, L1_ffn_b2, L2_attn_wq, L2_attn_wk_down, L2_attn_wv_down, L2_attn_wk_up, L2_attn_wv_up, L2_attn_wo, L2_ffn_router_weight, L2_ffn_e_score_bias, L2_ffn_gate_up_proj, L2_ffn_down_proj, L2_ffn_shared_gate_w, L2_ffn_shared_up_w, L2_ffn_shared_down_w, L3_attn_gamma, L3_attn_w_qkv, L3_attn_temperature, L3_attn_w_out, L3_ffn_gate_w, L3_ffn_up_w, L3_ffn_up_b, L3_ffn_gw, L3_ffn_gb, L3_ffn_down_w, L3_ffn_down_b, L3_ffn_sh_gate_w, L3_ffn_sh_up_w, L3_ffn_sh_down_w):

    def _L0_attn_ref(x, Wq, bq, Wk, bk, Wv, bv, Wo, bo):
        import jax, jax.numpy as jnp
        import numpy as np
        D_MODEL = 128
        N_HEADS = 16
        D_HEAD = D_MODEL // N_HEADS
        B, S, _ = x.shape
        H, d = (N_HEADS, D_HEAD)
        q = x @ Wq.T + bq
        k = x @ Wk.T + bk
        v = x @ Wv.T + bv

        def to_z(t):
            return t.reshape(B, S, H, d).transpose(0, 2, 1, 3).reshape(B * H, S, d)
        q = jax.nn.softplus(to_z(q))
        k = jax.nn.softplus(to_z(k))
        v = to_z(v)
        kv = jnp.cumsum(k[:, :, :, None] * v[:, :, None, :], axis=1)
        k1 = jnp.cumsum(k, axis=1)
        num = jnp.einsum('zsD,zsDe->zse', q, kv)
        den = jnp.sum(q * k1, axis=-1, keepdims=True)
        out = num / den
        out = out.reshape(B, H, S, d).transpose(0, 2, 1, 3).reshape(B, S, H * d)
        return out @ Wo.T + bo

    def _L0_ffn_ref(x, w_gate, w_up, w_down):
        import jax, jax.numpy as jnp
        import numpy as np
        DIM = 128
        HIDDEN = 384
        SCALE = 1.0 / 127.0

        def _dequant(w_int, dtype):
            return w_int.astype(dtype) * jnp.asarray(SCALE, dtype)
        wg = _dequant(w_gate, x.dtype)
        wu = _dequant(w_up, x.dtype)
        wd = _dequant(w_down, x.dtype)
        gate = jnp.einsum('bsd,hd->bsh', x, wg)
        up = jnp.einsum('bsd,hd->bsh', x, wu)
        h = jax.nn.silu(gate) * up
        return jnp.einsum('bsh,dh->bsd', h, wd)

    def _L1_attn_ref(x, Wq, Wk, Wv, q_gamma, q_beta, k_gamma, k_beta, Wo, bo):
        import math
        import jax, jax.numpy as jnp
        import numpy as np
        DIM = 128
        N_HEADS = 16
        HEAD_DIM = DIM // N_HEADS
        SEQ_LEN = 256
        BASE = 10000.0
        EPS = 1e-05

        def rope_cache(seq_len, dim):
            pos = jnp.arange(seq_len, dtype=jnp.float32)[:, None]
            di = jnp.arange(0, dim, 2, dtype=jnp.float32) / dim
            theta = pos * jnp.exp(-di * math.log(BASE))
            cos = jnp.repeat(jnp.cos(theta), 2, axis=1)
            sin = jnp.repeat(jnp.sin(theta), 2, axis=1)
            return (cos, sin)

        def rotate_half(x):
            x1 = x[..., ::2]
            x2 = x[..., 1::2]
            return jnp.concatenate((-x2, x1), axis=-1)

        def layernorm(x, gamma, beta):
            mu = jnp.mean(x, axis=-1, keepdims=True)
            var = jnp.var(x, axis=-1, keepdims=True)
            return (x - mu) * jax.lax.rsqrt(var + EPS) * gamma + beta
        B, S, D = x.shape
        H, hd = (N_HEADS, HEAD_DIM)
        q = (x @ Wq.T).reshape(B, S, H, hd).transpose(0, 2, 1, 3)
        k = (x @ Wk.T).reshape(B, S, H, hd).transpose(0, 2, 1, 3)
        v = (x @ Wv.T).reshape(B, S, H, hd).transpose(0, 2, 1, 3)
        q = layernorm(q, q_gamma, q_beta)
        k = layernorm(k, k_gamma, k_beta)
        cos, sin = rope_cache(S, hd)
        cos = cos[None, None]
        sin = sin[None, None]
        q = q * cos + rotate_half(q) * sin
        k = k * cos + rotate_half(k) * sin
        scale = 1.0 / math.sqrt(hd)
        scores = scale * jnp.einsum('bhqd,bhkd->bhqk', q, k)
        mask = jnp.tril(jnp.ones((S, S), dtype=bool))
        scores = jnp.where(mask, scores, -jnp.inf)
        attn = jax.nn.softmax(scores, axis=-1)
        out = jnp.einsum('bhqk,bhkd->bhqd', attn, v)
        out = out.transpose(0, 2, 1, 3).reshape(B, S, D)
        return out @ Wo.T + bo

    def _L1_ffn_ref(input_features, centroids, ln_g, ln_b, w1, b1, w2, b2):
        import jax, jax.numpy as jnp
        import numpy as np
        B, S, D, F, E = (8, 128, 128, 512, 8)
        EPS = 1e-05
        x = input_features.reshape(-1, D)
        aff = jax.lax.stop_gradient(x @ centroids.T)
        eid = jnp.argmax(aff, axis=-1)
        alpha = jax.nn.sigmoid(jnp.sum(x * centroids[eid], axis=-1, keepdims=True))
        mu = jnp.mean(x, axis=-1, keepdims=True)
        var = jnp.mean((x - mu) ** 2, axis=-1, keepdims=True)
        xn = (x - mu) * jax.lax.rsqrt(var + EPS)
        xln = xn * ln_g[eid] + ln_b[eid]
        onehot = jax.nn.one_hot(eid, E, dtype=x.dtype)
        ffn = jnp.zeros_like(x)
        for e in range(E):
            h = jax.nn.relu(xln @ w1[e] + b1[e])
            ffn = ffn + onehot[:, e:e + 1] * (h @ w2[e] + b2[e])
        out = x + alpha * ffn
        return out.reshape(input_features.shape)

    def _L2_attn_ref(x, wq, wk_down, wv_down, wk_up, wv_up, wo):
        import jax, jax.numpy as jnp
        import numpy as np
        D_MODEL, N_HEADS, N_KV, HEAD_DIM, D_LAT = (128, 8, 2, 128, 32)
        N_REP = N_HEADS // N_KV
        B, T = (2, 256)
        Bq, Tq, _ = x.shape
        scale = HEAD_DIM ** (-0.5)
        q = (x @ wq).reshape(Bq, Tq, N_KV, N_REP, HEAD_DIM)
        k_lat = (x @ wk_down).reshape(Bq, Tq, N_KV, D_LAT)
        v_lat = (x @ wv_down).reshape(Bq, Tq, N_KV, D_LAT)
        k = jnp.einsum('bkhl,ld->bkhd', k_lat, wk_up)
        v = jnp.einsum('bkhl,ld->bkhd', v_lat, wv_up)
        scores = jnp.einsum('bqhrd,bkhd->bhrqk', q, k) * scale
        causal = jnp.tril(jnp.ones((Tq, Tq), dtype=bool))
        scores = jnp.where(causal, scores, jnp.finfo(scores.dtype).min)
        probs = jax.nn.softmax(scores, axis=-1)
        y = jnp.einsum('bhrqk,bkhd->bqhrd', probs, v)
        y = y.reshape(Bq, Tq, N_HEADS * HEAD_DIM)
        return y @ wo

    def _L2_ffn_ref(hidden_states, router_weight, e_score_bias, gate_up_proj, down_proj, shared_gate_w, shared_up_w, shared_down_w):
        import jax, jax.numpy as jnp
        import numpy as np
        H = 128
        E = 32
        I = 64
        TOP_K = 6
        IS = 128
        NORM_MIN = 1e-12
        B, S = (2, 128)
        b, s, h = hidden_states.shape
        x = hidden_states.reshape(-1, h)
        T = x.shape[0]
        shared_out = jax.nn.silu(x @ shared_gate_w.T) * (x @ shared_up_w.T) @ shared_down_w.T
        xf = x.astype(jnp.float32)
        router_logits = xf @ router_weight.T
        routing_weights = jax.nn.softmax(router_logits, axis=-1)
        corrected = routing_weights + e_score_bias
        _, top_idx = jax.lax.top_k(corrected, TOP_K)
        top_w = jnp.take_along_axis(routing_weights, top_idx, axis=-1)
        top_w = top_w / jnp.clip(top_w.sum(axis=-1, keepdims=True), NORM_MIN)
        top_w = top_w.astype(x.dtype)
        combine = jnp.zeros((T, E), x.dtype).at[jnp.arange(T)[:, None], top_idx].add(top_w)
        gu = jnp.einsum('th,eih->tei', x, gate_up_proj)
        gate, up = jnp.split(gu, 2, axis=-1)
        hmid = jax.nn.silu(gate) * up
        y = jnp.einsum('tei,ehi->teh', hmid, down_proj)
        out = jnp.einsum('teh,te->th', y, combine) + shared_out
        return out.reshape(b, s, h)

    def _L3_attn_ref(x, gamma, w_qkv, temperature, w_out):
        import jax, jax.numpy as jnp
        import numpy as np
        EPS = 1e-12
        ATTEND_SCALE = 8.0

        def _l2norm(t, axis=-1):
            n = jnp.sqrt(jnp.sum(t * t, axis=axis, keepdims=True))
            return t / jnp.maximum(n, EPS)

        def _reference_tuple_inner(x, gamma, w_qkv, temperature, w_out):
            b, n, dim = x.shape
            heads = temperature.shape[0]
            dim_head = w_qkv.shape[1] // (3 * heads)
            xn = _l2norm(x) * dim ** 0.5 * gamma
            qkv = xn @ w_qkv
            qkv = qkv.reshape(b, n, 3, heads, dim_head).transpose(2, 0, 3, 4, 1)
            q, k, v = (qkv[0], qkv[1], qkv[2])
            orig_v = v
            q = _l2norm(q) * jnp.exp(temperature)
            k = _l2norm(k)
            sim = jnp.einsum('bhdn,bhen->bhde', q, k) * ATTEND_SCALE
            attn = jax.nn.softmax(sim, axis=-1)
            out = jnp.einsum('bhde,bhen->bhdn', attn, v)
            out = out.transpose(0, 3, 1, 2).reshape(b, n, heads * dim_head) @ w_out
            return (out, orig_v)
        return _reference_tuple_inner(x, gamma, w_qkv, temperature, w_out)[0]

    def _L3_ffn_ref(x, gate_w, up_w, up_b, gw, gb, down_w, down_b, sh_gate_w, sh_up_w, sh_down_w):
        import jax, jax.numpy as jnp
        import numpy as np
        import math
        E = 16
        TOP_K = 2
        D = 128
        F = 512
        SH = 256
        B, S, Dm = x.shape
        h = x.reshape(-1, Dm)
        T = h.shape[0]
        scores = jax.nn.sigmoid(h @ gate_w.T)
        cap = math.ceil(T / E * TOP_K)
        topk_score, topk_ids = jax.lax.top_k(scores.T, cap)
        xin = h[topk_ids]
        up = jnp.einsum('ecd,efd->ecf', xin, up_w) + up_b[:, None, :]
        g = jnp.einsum('ecd,efd->ecf', xin, gw) + gb[:, None, :]
        eo = jax.nn.silu(g) * up
        eo = jnp.einsum('ecf,edf->ecd', eo, down_w) + down_b[:, None, :]
        flat = (eo * topk_score[..., None]).reshape(-1, Dm)
        out = jnp.zeros_like(h).at[topk_ids.reshape(-1)].add(flat)
        out = out.reshape(B, S, Dm)
        shared = jax.nn.silu(jnp.einsum('bsd,fd->bsf', x, sh_gate_w)) * jnp.einsum('bsd,fd->bsf', x, sh_up_w)
        shared = jnp.einsum('bsf,df->bsd', shared, sh_down_w)
        return out + shared
    x = L0_attn_x
    xn = _layernorm(x, axis=-1)
    s = _L0_attn_ref(xn, L0_attn_Wq, L0_attn_bq, L0_attn_Wk, L0_attn_bk, L0_attn_Wv, L0_attn_bv, L0_attn_Wo, L0_attn_bo)
    g = _silu(_L0_ffn_ref(xn, L0_ffn_w_gate, L0_ffn_w_up, L0_ffn_w_down))
    x = x + s * g
    xn = _layernorm(x, axis=-1)
    s = _L1_attn_ref(xn, L1_attn_Wq, L1_attn_Wk, L1_attn_Wv, L1_attn_q_gamma, L1_attn_q_beta, L1_attn_k_gamma, L1_attn_k_beta, L1_attn_Wo, L1_attn_bo)
    g = _silu(_L1_ffn_ref(xn, L1_ffn_centroids, L1_ffn_ln_g, L1_ffn_ln_b, L1_ffn_w1, L1_ffn_b1, L1_ffn_w2, L1_ffn_b2))
    x = x + s * g
    xn = _layernorm(x, axis=-1)
    s = _L2_attn_ref(xn, L2_attn_wq, L2_attn_wk_down, L2_attn_wv_down, L2_attn_wk_up, L2_attn_wv_up, L2_attn_wo)
    g = _silu(_L2_ffn_ref(xn, L2_ffn_router_weight, L2_ffn_e_score_bias, L2_ffn_gate_up_proj, L2_ffn_down_proj, L2_ffn_shared_gate_w, L2_ffn_shared_up_w, L2_ffn_shared_down_w))
    x = x + s * g
    xn = _layernorm(x, axis=-1)
    s = _L3_attn_ref(xn, L3_attn_gamma, L3_attn_w_qkv, L3_attn_temperature, L3_attn_w_out)
    g = _silu(_L3_ffn_ref(xn, L3_ffn_gate_w, L3_ffn_up_w, L3_ffn_up_b, L3_ffn_gw, L3_ffn_gb, L3_ffn_down_w, L3_ffn_down_b, L3_ffn_sh_gate_w, L3_ffn_sh_up_w, L3_ffn_sh_down_w))
    x = x + s * g
    return x

_drawn_inputs = setup_inputs


def setup_inputs(seed=0):
    import zlib

    import numpy as np

    out = dict(_drawn_inputs(seed))
    spreads = {'L0_attn_bq': (0.0, 0.8),
     'L0_attn_bk': (0.0, 0.8),
     'L0_attn_bv': (0.0, 0.1),
     'L0_attn_bo': (0.0, 0.1),
     'L1_attn_q_gamma': (1.0, 0.6),
     'L1_attn_q_beta': (0.0, 0.8),
     'L1_attn_k_gamma': (1.0, 0.6),
     'L1_attn_k_beta': (0.0, 0.8),
     'L1_attn_bo': (0.0, 0.8),
     'L1_ffn_ln_g': (1.0, 0.6),
     'L1_ffn_ln_b': (0.0, 0.8),
     'L1_ffn_b1': (0.0, 0.8),
     'L1_ffn_b2': (0.0, 0.8),
     'L2_ffn_e_score_bias': (0.0, 0.8),
     'L3_attn_gamma': (1.0, 0.6),
     'L3_attn_temperature': (0.0, 0.8)}
    factors = {'L1_attn_Wq': 8.0,
     'L1_attn_Wk': 8.0,
     'L1_attn_Wv': 8.0,
     'L1_attn_Wo': 7.46,
     'L1_ffn_centroids': 8.0,
     'L1_ffn_w1': 8.0,
     'L1_ffn_w2': 8.0,
     'L2_attn_wq': 8.0,
     'L2_attn_wk_down': 8.0,
     'L2_attn_wv_down': 8.0,
     'L2_attn_wk_up': 8.0,
     'L2_attn_wv_up': 8.0,
     'L2_attn_wo': 8.0,
     'L2_ffn_router_weight': 8.0,
     'L2_ffn_gate_up_proj': 8.0,
     'L2_ffn_down_proj': 8.0,
     'L2_ffn_shared_gate_w': 8.0,
     'L2_ffn_shared_up_w': 8.0,
     'L2_ffn_shared_down_w': 8.0,
     'L3_attn_w_qkv': 8.0,
     'L3_attn_w_out': 8.0,
     'L3_ffn_gate_w': 8.0,
     'L3_ffn_up_w': 8.0,
     'L3_ffn_up_b': 8.0,
     'L3_ffn_gw': 8.0,
     'L3_ffn_gb': 8.0,
     'L3_ffn_down_w': 8.0,
     'L3_ffn_down_b': 8.0,
     'L3_ffn_sh_gate_w': 8.0,
     'L3_ffn_sh_up_w': 8.0,
     'L3_ffn_sh_down_w': 8.0}
    for name, (base, spread) in spreads.items():
        noise = np.random.default_rng([zlib.crc32(name.encode()), seed]).standard_normal(out[name].shape)
        drawn = base * np.exp(spread * noise) if base else spread * noise
        out[name] = jnp.asarray(drawn.astype(out[name].dtype))
    for name, factor in factors.items():
        out[name] = (out[name] * factor).astype(out[name].dtype)
    return out
```

```python
from contextlib import ExitStack

import concourse.bass as bass
import numpy as np
from concourse import mybir

F32 = mybir.dt.float32
BF16 = mybir.dt.bfloat16
I32 = mybir.dt.int32
U32 = mybir.dt.uint32
ALU = mybir.AluOpType
ACT = mybir.ActivationFunctionType
AX = mybir.AxisListType

P = 128
BATCH, SEQ, D = 16, 256, 128
TOKENS = BATCH * SEQ
TILES = TOKENS // P
QT = SEQ // P
COLS = 512
BLOCKS = TOKENS // COLS
TPB = COLS // P
LN_EPS = 1e-5
BIG_NEG = -1e30


def software_pipeline(fori, steps, n):
    lags = [lag for _, lag in steps]
    first, last = max(lags) + (max(lags) > 0), n + min(lags)
    last -= (last - first) % 2

    def turn(t, parity):
        for fn, lag in steps:
            if not isinstance(t, int) or 0 <= t - lag < n:
                fn(t - lag, (parity - lag) % 2)

    if last - first < 4:
        first = last = 0
    for t in range(first):
        turn(t, t % 2)
    if last > first:
        with fori(0, (last - first) // 2) as r:
            for k in range(2):
                turn(r * 2 + (first + k), (first + k) % 2)
    for t in range(last, n + max(lags)):
        turn(t, t % 2)


def scope(nc):
    ctx = ExitStack()
    sems = []

    def clear():
        nc.clear_and_free_semaphores(sems)
        nc.all_engine_barrier()

    ctx.callback(clear)

    def sb(name, shape, dt=F32):
        return ctx.enter_context(nc.sbuf_tensor(name, shape, dt))

    def pb(name, shape, dt=F32):
        return ctx.enter_context(nc.psum_tensor(name, shape, dt))

    def sem(name):
        sems.append(nc.alloc_semaphore(name))
        return sems[-1]

    return ctx, sb, pb, sem


def constants_stage(nc, on, dram):
    ctx, sb, pb, sem = scope(nc)
    with ctx:
        filled, shaped, loaded = sem("c_filled"), sem("c_shaped"), sem("c_loaded")
        block = ctx.enter_context(nc.Block())

        @block.sync
        def _(sp):
            sp.dma_start(on.x[:, :, :], dram["x"].rearrange("(t p) d -> p t d", p=P)).then_inc(loaded, 16)
            sp.wait_ge(loaded, 16)

        @block.gpsimd
        def _(pool):
            nc.gpsimd.memset(on.ident[:, :], 0.0)
            nc.gpsimd.memset(on.ident_bf[:, :], 0.0)
            nc.gpsimd.memset(on.ones[:, :], 1.0)
            nc.gpsimd.memset(on.causal[:, :], 1.0)
            nc.gpsimd.memset(on.mask_kq[:, :, :], 0.0)
            nc.gpsimd.memset(on.mask_qk[:, :, :], 0.0).then_inc(filled, 1)
            pool.wait_ge(filled, 1)
            for m in (on.ident, on.ident_bf):
                nc.gpsimd.affine_select(out=m[:, :], in_=m[:, :], compare_op=ALU.not_equal, fill=1.0, base=0,
                                        pattern=[[-1, P]], channel_multiplier=1)
            nc.gpsimd.affine_select(out=on.causal[:, :], in_=on.causal[:, :], compare_op=ALU.is_ge, fill=0.0, base=0,
                                    pattern=[[1, P]], channel_multiplier=-1)
            nc.gpsimd.affine_select(out=on.mask_kq[:, :, :], in_=on.mask_kq[:, :, :], compare_op=ALU.is_ge,
                                    fill=BIG_NEG, base=0, pattern=[[0, 4], [1, P]], channel_multiplier=-1)
            nc.gpsimd.affine_select(out=on.mask_qk[:, :, :], in_=on.mask_qk[:, :, :], compare_op=ALU.is_ge,
                                    fill=BIG_NEG, base=0, pattern=[[0, 4], [-1, P]], channel_multiplier=1)\
                .then_inc(shaped, 1)
            pool.wait_ge(shaped, 1)


def layernorm_stage(nc, on, name, src, dst, dst_t, gated):
    ctx, sb, pb, sem = scope(nc)
    with ctx:
        gate = [sb(f"{name}_gate{k}", [P, COLS]) for k in range(2)]
        stats = sb(f"{name}_stats", [P, TILES, 6])
        mean_var = sb(f"{name}_mv", [P, TILES, 2])
        rstd = sb(f"{name}_rstd", [P, TILES])
        std = sb(f"{name}_std", [P, TILES])
        turned = [pb(f"{name}_turned{k}", [P, COLS]) for k in range(2)]
        s_gate, s_gate_free, s_prod, s_added = (sem(f"{name}_{w}") for w in ("silu", "silufree", "prod", "added"))
        s_stats, s_aggr, s_eps, s_std, s_rstd = (sem(f"{name}_{w}") for w in ("stats", "aggr", "eps", "std", "rstd"))
        s_norm, s_turned, s_turned_free = (sem(f"{name}_{w}") for w in ("norm", "turned", "turnedfree"))
        block = ctx.enter_context(nc.Block())

        def block_of(t, i):
            return t[:, bass.ds(i * TPB, TPB), :].rearrange("p t d -> p (t d)")

        @block.scalar
        def _(act):
            act.sem_inc(s_turned_free, 2)
            if gated:
                def silu(i, k):
                    act.wait_ge(s_gate_free, i + 1)
                    nc.scalar.activation(gate[k][:, :], block_of(on.g, i), ACT.Silu).then_inc(s_gate, 1)

                software_pipeline(nc.scalar.Fori, [(silu, 0)], BLOCKS)
            act.wait_ge(s_eps, 1)
            nc.scalar.activation(std[:, :], rstd[:, :], ACT.Sqrt).then_inc(s_std, 1)

            def copy_out(i, k):
                act.wait_ge(s_turned, i + 1)
                nc.scalar.activation(dst_t[:, bass.ts(i, COLS)], turned[k][:, :], ACT.Copy).then_inc(s_turned_free, 1)

            software_pipeline(nc.scalar.Fori, [(copy_out, 0)], BLOCKS)

        @block.gpsimd
        def _(pool):
            if gated:
                def add(i, k):
                    pool.wait_ge(s_prod, i + 1)
                    nc.gpsimd.tensor_tensor(block_of(on.x, i), block_of(on.x, i), gate[k][:, :], ALU.add)\
                        .then_inc(s_added, 1)

                pool.sem_inc(s_gate_free, 2)
                software_pipeline(nc.gpsimd.Fori, [(add, 0)], BLOCKS)

        @block.vector
        def _(dve):
            if gated:
                def product(i, k):
                    dve.wait_ge(s_gate, i + 1)
                    nc.vector.tensor_tensor(gate[k][:, :], gate[k][:, :], block_of(on.s, i), ALU.mult)\
                        .then_inc(s_prod, 1)

                def block_stats(i, k):
                    dve.wait_ge(s_added, i + 1)
                    dve.sem_inc(s_gate_free, 1)
                    for t in range(TPB):
                        nc.vector.bn_stats(stats[:, bass.ds(i * TPB + t, 1), :], src[:, bass.ds(i * TPB + t, 1), :])\
                            .then_inc(s_stats, 1)

                software_pipeline(nc.vector.Fori, [(product, 0), (block_stats, 1)], BLOCKS)
            else:
                with nc.vector.Fori(0, TILES) as t:
                    nc.vector.bn_stats(stats[:, bass.ds(t, 1), :], src[:, bass.ds(t, 1), :]).then_inc(s_stats, 1)
            dve.wait_ge(s_stats, TILES)
            for t in range(TILES):
                nc.vector.bn_aggr(mean_var[:, t, :], stats[:, t, :]).then_inc(s_aggr, 1)
            dve.wait_ge(s_aggr, TILES)
            nc.vector.tensor_scalar(rstd[:, :], mean_var[:, :, 1], LN_EPS, None, ALU.add).then_inc(s_eps, 1)
            dve.wait_ge(s_std, 1)
            nc.vector.reciprocal(rstd[:, :], std[:, :]).then_inc(s_rstd, 1)
            dve.wait_ge(s_rstd, 1)
            with nc.vector.Fori(0, TILES) as t:
                nc.vector.tensor_scalar(dst[:, bass.ds(t, 1), :], src[:, bass.ds(t, 1), :],
                                        mean_var[:, bass.ds(t, 1), 0], rstd[:, bass.ds(t, 1)],
                                        ALU.subtract, ALU.mult).then_inc(s_norm, 1)

        @block.tensor
        def _(pe):
            for i in range(BLOCKS):
                pe.wait_ge(s_norm, (i + 1) * TPB)
                pe.wait_ge(s_turned_free, i + 1)
                for t in range(TPB):
                    ins = nc.tensor.transpose(turned[i % 2][:, t * P:(t + 1) * P], dst[:, i * TPB + t, :],
                                              on.ident[:, :])
                ins.then_inc(s_turned, 1)


def ffn_stage(nc, on, name, src_t, acc, experts, chunks, down_outs, weights, gated, combine=None):
    ctx, sb, pb, sem = scope(nc)
    with ctx:
        kinds = [w for w in ("gate", "up", "down", "bias") if w in weights]
        biased = "bias" in weights
        w_sb = {w: [sb(f"{name}_w_{w}{k}", [P, 1, (1 + gated) * chunks] if w == "bias" else [P, chunks, P])
                    for k in range(min(2, experts))] for w in kinds}
        h = [[sb(f"{name}_h{k}_{c}", [P, COLS]) for c in range(chunks)] for k in range(2)]
        silu = [sb(f"{name}_silu{k}", [P, COLS]) for k in range(2)] if gated else None
        gate_ps = [pb(f"{name}_gate{k}", [P, COLS]) for k in range(2)]
        up_ps = [pb(f"{name}_up{k}", [P, COLS]) for k in range(2)] if gated else None
        down_ps = [[pb(f"{name}_down{k}_{o}", [P, TPB, P]) for o in range(down_outs)] for k in range(2)]
        w_loaded = [sem(f"{name}_w_loaded{k}") for k in range(2)]
        s_proj, s_gate_free, s_silu, s_up_free, s_acc, s_down, s_down_free = (
            sem(f"{name}_{w}") for w in ("proj", "gatefree", "silu", "upfree", "acc", "down", "downfree"))
        block = ctx.enter_context(nc.Block())

        def each_expert(fori, body):
            if experts == 1:
                body(0, 0)
            else:
                with fori(0, experts // 2) as r:
                    for k in range(2):
                        body(r * 2 + k, k)

        @block.sync
        def _(sp):
            def load(e, k):
                for w in kinds:
                    sp.dma_start(w_sb[w][k][:, :, :], weights[w](e)).then_inc(w_loaded[k], 16)

            for e in range(min(2, experts)):
                load(e, e)
            if experts > 2:
                with nc.sync.Fori(0, experts // 2 - 1) as r:
                    for k in range(2):
                        sp.wait_ge(s_down, r * (2 * BLOCKS) + ((k + 1) * BLOCKS + 2))
                        load(r * 2 + (2 + k), k)

        @block.tensor
        def _(pe):
            pe.sem_inc(s_down, 2)

            def project(e, k, i, par):
                u = e * BLOCKS + i
                cols = src_t[:, bass.ts(i, COLS)]
                for c in range(chunks):
                    n, b = u * chunks + c, (par * chunks + c) % 2
                    pe.wait_ge(s_gate_free, n + 1)
                    ins = nc.tensor.matmul(gate_ps[b][:, :], w_sb["gate"][k][:, c, :], cols, start=True, stop=True)
                    if gated:
                        pe.wait_ge(s_up_free, n + 1)
                        ins = nc.tensor.matmul(up_ps[b][:, :], w_sb["up"][k][:, c, :], cols, start=True, stop=True)
                    ins.then_inc(s_proj, 1)

            def down(e, k, i, par):
                u = e * BLOCKS + i
                pe.wait_ge(s_up_free if gated else s_gate_free, (u + 1) * chunks + 2)
                pe.wait_ge(s_down_free, u + 1)
                rows = P // down_outs
                for t in range(TPB):
                    for o in range(down_outs):
                        r = slice(o * rows, (o + 1) * rows)
                        for c in range(chunks):
                            ins = nc.tensor.matmul(down_ps[par][o][:, t, :], h[par][c][r, t * P:(t + 1) * P],
                                                   w_sb["down"][k][r, c, :], start=(c == 0), stop=(c == chunks - 1))
                ins.then_inc(s_down, 1)

            def expert(e, k):
                pe.wait_ge(w_loaded[k], (e // 2 + 1) * 16 * len(kinds) if isinstance(e, int)
                           else (e - k) * (8 * len(kinds)) + 16 * len(kinds))
                software_pipeline(nc.tensor.Fori, [(lambda i, par: project(e, k, i, par), 0),
                                                   (lambda i, par: down(e, k, i, par), 1)], BLOCKS)

            each_expert(nc.tensor.Fori, expert)

        @block.scalar
        def _(act):
            act.sem_inc(s_gate_free, 2)

            def unit(e, k, i, par):
                u = e * BLOCKS + i
                if not gated:
                    act.wait_ge(s_down, u + 1)
                for c in range(chunks):
                    n, b = u * chunks + c, (par * chunks + c) % 2
                    act.wait_ge(s_proj, n + 1)
                    if gated:
                        act.wait_ge(s_up_free, n + 1)
                        if biased:
                            nc.scalar.activation(silu[b][:, :], gate_ps[b][:, :], ACT.Silu,
                                                 bias=w_sb["bias"][k][:, 0, c:c + 1]).then_inc(s_gate_free, 1)
                        else:
                            nc.scalar.activation(silu[b][:, :], gate_ps[b][:, :], ACT.Silu).then_inc(s_gate_free, 1)
                    else:
                        nc.scalar.activation(h[par][c][:, :], gate_ps[b][:, :], ACT.Relu,
                                             bias=w_sb["bias"][k][:, 0, c:c + 1]).then_inc(s_gate_free, 1)

            each_expert(nc.scalar.Fori, lambda e, k: software_pipeline(
                nc.scalar.Fori, [(lambda i, par: unit(e, k, i, par), 0)], BLOCKS))

        @block.vector
        def _(dve):
            dve.sem_inc(s_up_free, 2)
            dve.sem_inc(s_down_free, 2)

            def hidden(e, k, i, par):
                u = e * BLOCKS + i
                dve.wait_ge(s_down, u + 1)
                for c in range(chunks):
                    n, b = u * chunks + c, (par * chunks + c) % 2
                    dve.wait_ge(s_gate_free, n + 3)
                    if biased:
                        nc.vector.scalar_tensor_tensor(h[par][c][:, :], up_ps[b][:, :],
                                                       w_sb["bias"][k][:, 0, chunks + c:chunks + c + 1],
                                                       silu[b][:, :], ALU.add, ALU.mult).then_inc(s_up_free, 1)
                    else:
                        nc.vector.tensor_tensor(h[par][c][:, :], up_ps[b][:, :], silu[b][:, :], ALU.mult)\
                            .then_inc(s_up_free, 1)

            def take(e, k, i, par):
                u = e * BLOCKS + i
                dve.wait_ge(s_down, u + 3)
                if combine is None:
                    nc.vector.tensor_copy(acc[:, bass.ts(i, TPB), :], down_ps[par][0][:, :, :]).then_inc(s_down_free, 1)
                    return
                for o in range(down_outs):
                    if o:
                        dve.wait_ge(s_acc, u * (down_outs - 1) + 1)
                    for t in range(TPB):
                        tile = i * TPB + t
                        ins = nc.vector.scalar_tensor_tensor(
                            acc[:, bass.ds(tile, 1), :], down_ps[par][o][:, t:t + 1, :],
                            combine[:, bass.ds(tile, 1), bass.ds(e * down_outs + o, 1)],
                            acc[:, bass.ds(tile, 1), :], ALU.mult, ALU.add)
                    ins.then_inc(s_down_free if o == down_outs - 1 else s_acc, 1)

            steps = [(hidden, 0)] * gated + [(take, 1)]
            each_expert(nc.vector.Fori, lambda e, k: software_pipeline(
                nc.vector.Fori, [((lambda i, par, fn=fn: fn(e, k, i, par)), lag) for fn, lag in steps], BLOCKS))


def upto(value, limit):
    return min(value, limit) if isinstance(value, int) else value


def project_stage(nc, on, name, dram, heads, finish):
    hd = D // heads
    GROUPS = TILES // 2
    ctx, sb, pb, sem = scope(nc)
    with ctx:
        w = dram["w_sb"] if finish == "latent" else sb(f"{name}_w", [P, 3 * D])
        xb = [sb(f"{name}_xb{k}", [P, 2 * P]) for k in range(2)]
        prod = [[pb(f"{name}_prod{k}{t}", [P, 3, D]) for t in range(2)] for k in range(2)]
        loaded, s_xb, s_prod, s_taken, s_chain, s_act = (
            sem(f"{name}_{n}") for n in ("loaded", "xb", "prod", "taken", "chain", "act"))
        loads = [] if finish == "latent" else [(w[:, :], dram["w"])]
        if finish == "latent":
            pass
        elif finish == "softplus":
            bias = sb(f"{name}_bias", [P, 3, D])
            loads.append((bias[:, :, :], dram["bias"]))
            terms = [sb(f"{name}_terms{j}", [P, TILES, D]) for j in range(2)]
        else:
            cos_sin = sb(f"{name}_cos_sin", [P, 2, QT, hd])
            gamma_beta = sb(f"{name}_gamma_beta", [P, 2, 2, hd])
            loads += [(cos_sin[:, :, :, :], dram["cos_sin"]), (gamma_beta[:, :, :, :], dram["gamma_beta"])]
            mean = sb(f"{name}_mean", [P, TILES, heads])
            var = sb(f"{name}_var", [P, TILES, heads])
            square = sb(f"{name}_square", [P, TILES, D])
            turned = sb(f"{name}_turned", [P, TILES, D])
        block = ctx.enter_context(nc.Block())

        @block.sync
        def _(sp):
            for dst, src in loads:
                sp.dma_start(dst, src).then_inc(loaded, 16)

        @block.gpsimd
        def _(pool):
            def copy_x(i, k):
                pool.wait_ge(s_prod, i + 1)
                nc.gpsimd.tensor_copy(xb[k][:, :], on.xnT[:, bass.ts(i, 2 * P)]).then_inc(s_xb, 1)

            software_pipeline(nc.gpsimd.Fori, [(copy_x, 0)], GROUPS)

        @block.tensor
        def _(pe):
            pe.sem_inc(s_prod, 2)
            pe.wait_ge(loaded, 16 * len(loads))

            def product(i, k):
                pe.wait_ge(s_xb, i + 1)
                pe.wait_ge(s_taken, i + 1)
                for t in range(2):
                    ins = nc.tensor.matmul(prod[k][t][:, :, :].rearrange("p j d -> p (j d)"),
                                           xb[k][:, t * P:(t + 1) * P], w[:, :], start=True, stop=True)
                ins.then_inc(s_prod, 1)

            software_pipeline(nc.tensor.Fori, [(product, 0)], GROUPS)

        @block.vector
        def _(dve):
            dve.sem_inc(s_taken, 2)
            dve.wait_ge(loaded, 16 * len(loads))

            def take(i, k):
                dve.wait_ge(s_prod, i + 3)
                for t in range(2):
                    if finish == "latent":
                        tile = bass.ds(i * 2 + t, 1)
                        nc.vector.tensor_copy(on.q2[:, tile, :], prod[k][t][:, 0:2, :].rearrange("p j d -> p (j d)"))
                        ins = nc.vector.tensor_copy(on.kv[:, tile, :], prod[k][t][:, 2:3, :])
                        continue
                    for j, dst in enumerate((on.q, on.k, on.v)):
                        out = dst[:, bass.ds(i * 2 + t, 1), :]
                        if finish == "softplus":
                            ins = nc.vector.tensor_tensor(out, prod[k][t][:, j:j + 1, :], bias[:, j:j + 1, :], ALU.add)
                        else:
                            ins = nc.vector.tensor_copy(out, prod[k][t][:, j:j + 1, :])
                ins.then_inc(s_taken, 1)

            software_pipeline(nc.vector.Fori, [(take, 0)], GROUPS)
            done = [0]

            def link(ins):
                done[0] += 1
                ins.then_inc(s_chain, 1)
                dve.wait_ge(s_chain, done[0])

            dve.wait_ge(s_taken, GROUPS + 2)
            if finish == "latent":
                return
            if finish == "softplus":
                for j, z in enumerate((on.q, on.k)):
                    dve.wait_ge(s_act, 5 + j)
                    nc.vector.scalar_tensor_tensor(z[:, :, :], z[:, :, :], 0.0, terms[j][:, :, :], ALU.max, ALU.add)\
                        .then_inc(s_chain, 1)
                dve.wait_ge(s_chain, 2)
                return
            for j, z in enumerate((on.q, on.k)):
                by_head = z[:, :, :].rearrange("p t (h d) -> p t h d", d=hd)
                flat = z[:, :, :].rearrange("p t (h d) -> p (t h) d", d=hd)
                sq = square[:, :, :].rearrange("p t (h d) -> p (t h) d", d=hd)

                def wide(a):
                    return a.unsqueeze(2).broadcast_to([P, TILES * heads, hd])

                m, v = (a[:, :, :].rearrange("p t h -> p (t h)") for a in (mean, var))
                link(nc.vector.tensor_reduce(m, flat, AX.X, ALU.add))
                link(nc.vector.tensor_scalar(m, m, 1.0 / hd, None, ALU.mult))
                link(nc.vector.tensor_tensor(flat, flat, wide(m), ALU.subtract))
                link(nc.vector.tensor_tensor(sq, flat, flat, ALU.mult))
                link(nc.vector.tensor_reduce(v, sq, AX.X, ALU.add))
                link(nc.vector.tensor_scalar(v, v, 1.0 / hd, LN_EPS, ALU.mult, ALU.add))
                dve.wait_ge(s_act, j + 1)
                link(nc.vector.reciprocal(v, v))
                link(nc.vector.tensor_tensor(flat, flat, wide(v), ALU.mult))
                for op, row in ((ALU.mult, 0), (ALU.add, 1)):
                    gb = gamma_beta[:, row, j, :].unsqueeze(1).broadcast_to([P, TILES * heads, hd])
                    link(nc.vector.tensor_tensor(flat, flat, gb, op))
                half = hd // 2
                rot = turned[:, :, :].rearrange("p t (h d) -> p (t h) d", d=hd)
                nc.vector.tensor_scalar(rot[:, :, 0:half], flat[:, :, 1:hd:2], -1.0, None, ALU.mult)
                link(nc.vector.tensor_copy(rot[:, :, half:hd], flat[:, :, 0:hd:2]))
                for t in range(QT):
                    for src, row in ((z, 0), (turned, 1)):
                        part = src[:, t:TILES:QT, :].rearrange("p t (h d) -> p t h d", d=hd)
                        table = cos_sin[:, row, t, :].unsqueeze(1).unsqueeze(1).broadcast_to([P, TILES // QT, heads, hd])
                        ins = nc.vector.tensor_tensor(part, part, table, ALU.mult)
                link(ins)
                link(nc.vector.tensor_tensor(z[:, :, :], z[:, :, :], turned[:, :, :], ALU.add))

        @block.scalar
        def _(act):
            if finish == "softplus":
                act.wait_ge(s_taken, GROUPS + 2)
                for n, (func, scale, plus) in enumerate(((ACT.Abs, 1.0, 0.0), (ACT.Exp, -1.0, 0.0), (ACT.Ln, 1.0, 1.0))):
                    for j, z in enumerate((on.q, on.k)):
                        if n:
                            act.wait_ge(s_act, 2 * (n - 1) + j + 1)
                        nc.scalar.activation(terms[j][:, :, :], (terms[j] if n else z)[:, :, :], func, scale=scale,
                                             bias=plus).then_inc(s_act, 1)
            elif finish == "rope":
                for j in range(2):
                    act.wait_ge(s_chain, 13 * j + 6)
                    nc.scalar.activation(var[:, :, :], var[:, :, :], ACT.Sqrt).then_inc(s_act, 1)


def latent_fold_stage(nc, on, name, dram, w_sb, wo_sb, heads, kvh):
    lat = 32
    ctx, sb, pb, sem = scope(nc)
    with ctx:
        wqT, wo = sb(f"{name}_wqT", [P, heads, D]), sb(f"{name}_wo", [P, heads, D])
        up = sb(f"{name}_up", [P, 2, lat])
        q_ps, o_ps = pb(f"{name}_qps", [P, heads * lat]), pb(f"{name}_ops", [P, kvh, D])
        loaded, folded, copied = (sem(f"{name}_{w}") for w in ("loaded", "folded", "copied"))
        loads = [(wqT[:, :, :], dram["wqT"]), (wo[:, :, :], dram["wo"]), (up[:, :, :], dram["up"]),
                 (w_sb[:, heads * lat:], dram["w_down"])]
        block = ctx.enter_context(nc.Block())

        @block.sync
        def _(sp):
            for dst, src in loads:
                sp.dma_start(dst, src).then_inc(loaded, 16)
            sp.wait_ge(loaded, 16 * len(loads))

        @block.tensor
        def _(pe):
            pe.wait_ge(loaded, 16 * len(loads))
            for h in range(heads):
                ins = nc.tensor.matmul(q_ps[:, h * lat:(h + 1) * lat], wqT[:, h, :], up[:, 0, :], start=True, stop=True)
            ins.then_inc(folded, 1)
            hpg = heads // kvh
            for h in range(heads):
                r = lat * (h % hpg)
                ins = nc.tensor.matmul(o_ps[r:r + lat, h // hpg, :], up[:, 1, :], wo[:, h, :], start=True, stop=True)
            ins.then_inc(folded, 1)

        @block.scalar
        def _(act):
            act.wait_ge(folded, 1)
            nc.scalar.activation(w_sb[:, 0:heads * lat], q_ps[:, :], ACT.Copy).then_inc(copied, 1)
            act.wait_ge(folded, 2)
            nc.scalar.activation(wo_sb[:, :, :], o_ps[:, :, :], ACT.Copy).then_inc(copied, 1)
            act.wait_ge(copied, 2)


def latent_attention(nc, on, name, dram, heads, kvh):
    with nc.sbuf_tensor(f"{name}_q2", [P, TILES, heads * 32], F32) as q2, \
            nc.sbuf_tensor(f"{name}_w", [P, 3 * D], F32) as w_sb, \
            nc.sbuf_tensor(f"{name}_wo_sb", [P, kvh, D], F32) as wo_sb:
        on.q2, on.kv = q2, on.v
        latent_fold_stage(nc, on, f"{name}f", dram, w_sb, wo_sb, heads, kvh)
        project_stage(nc, on, f"{name}p", {"w_sb": w_sb}, heads, "latent")
        attention_stage(nc, on, f"{name}a", {**dram, "wo_sb": wo_sb}, heads, float(D) ** -0.5, kvh)


def attention_stage(nc, on, name, dram, heads, softmax_scale, kv_heads=None):
    latent = kv_heads is not None
    hd = 32 if latent else D // heads
    kvh = kv_heads or heads
    SLOT = 64
    CW = 3 * P
    HALF = heads // 2
    QB = 12 if latent else 8
    KB = 4 if latent else 8
    STRIPS = 3 if latent else 4
    OB = heads * hd // P
    Q_FILLS = QB // 4
    softmax = softmax_scale is not None
    LAG = 2 if softmax else 1
    ctx, sb, pb, sem = scope(nc)
    with ctx:
        wo = dram["wo_sb"] if latent else sb(f"{name}_wo", [P, 1, D])
        bo = None if latent else sb(f"{name}_bo", [P, D])
        sel = sb(f"{name}_sel", [P, heads, P], BF16) if softmax else None
        widths = (heads * hd, kvh * hd)
        parts = [sb(f"{name}_parts{j}", [P, 3, QT, w], BF16) for j, w in enumerate(widths)]
        rest = [sb(f"{name}_rest{j}", [P, QT, w]) for j, w in enumerate(widths)]
        stacks = 1 if latent else 2
        stack = [[sb(f"{name}_stack{k}{j}", [P, QT, n, P], BF16) for j, n in enumerate((QB, KB))]
                 for k in range(stacks)]
        stack = stack * 2 if latent else stack
        opT = [[sb(f"{name}_opT{k}{j}", [P, n, SEQ], BF16) for j, n in enumerate((QB, KB))] for k in range(2)]
        v1 = [sb(f"{name}_v1{k}", [P, QT, kvh, 32]) for k in range(2)]
        probs = [sb(f"{name}_probs{k}", [P, heads, CW]) for k in range(2)]
        den_cols = sb(f"{name}_dencols", [P, kvh, 32]) if latent else None
        pv_sb = sb(f"{name}_pvsb", [P, 4, SEQ])
        rden = sb(f"{name}_rden", [P, heads])
        o_sb = sb(f"{name}_o", [P, QT, heads, hd])
        oT = sb(f"{name}_oT", [P, QT, OB, P])
        score_ps = [pb(f"{name}_score{k}", [P, COLS]) for k in range(2)]
        top_ps = [pb(f"{name}_top{k}", [P, COLS]) for k in range(2)] if softmax else None
        pv_ps = [pb(f"{name}_pv{k}", [P, 2, SEQ]) for k in range(2)]
        opT_ps = pb(f"{name}_opTp", [P, 4, SEQ], BF16)
        desk = pb(f"{name}_desk", [P, 4, D])
        out_ps = desk[:, 0:QT, :]
        if softmax:
            tops = sb(f"{name}_tops", [P, QT, heads])
            ntop = sb(f"{name}_ntop", [P, QT, P], BF16)
            ntopT = [sb(f"{name}_ntopT{k}", [P, SEQ], BF16) for k in range(2)]
            ntopT_ps = desk[:, 0, :].bitcast(BF16)
        else:
            causal3 = sb(f"{name}_causal3", [P, CW])
        S = {w: sem(f"{name}_{w}") for w in (
            "w", "init", "sel", "part1", "rest1", "part2", "part3", "stack0", "stack1", "v1", "turned", "opT", "top", "topout",
            "neg", "ntop", "ntopTp", "ntopT", "score", "probs", "pv", "pvout", "tokmaj", "rden",
            "o", "oturned", "oT", "out", "s")}
        block = ctx.enter_context(nc.Block())
        loads = [] if latent else [(wo[:, 0, :], dram["wo"]), (bo[:, :], dram["bo"])]
        if latent:
            loads.append((den_cols[:, :, :], dram["den_cols"]))

        @block.sync
        def _(sp):
            for dst, src in loads:
                sp.dma_start(dst, src).then_inc(S["w"], 16)

        def q_of(t):
            return on.q2[:, t, :] if latent else on.q[:, t, :]

        def k_of(t):
            return on.kv[:, t, 0:kvh * hd] if latent else on.k[:, t, :]

        def slots(k, j, lo, n):
            a = stack[k][j][:, :, :, :].rearrange("p t b (h s) -> p (t b h) s", s=SLOT)
            return a[:, :, lo * hd:(lo + n) * hd].rearrange("p g (n d) -> p g n d", d=hd)

        def wide_slots(k, j, t, lo, n):
            hs = (heads, kvh)[j]
            if lo < 4:
                return stack[k][j][:, t, 0:hs, lo * hd:(lo + n) * hd].rearrange("p h (n d) -> p h n d", d=hd)
            a = stack[k][j][:, t, hs:, :].rearrange("p b (h s) -> p (b h) s", s=2 * hd)
            return a[:, :, (lo - 4) * hd:(lo - 4 + n) * hd].rearrange("p g (n d) -> p g n d", d=hd)

        def part(m, j, n):
            a = parts[j][:, m, :, :].rearrange("p t (h d) -> p (t h) d", d=hd).unsqueeze(2)
            return a.broadcast_to([P, QT * heads, n, hd])

        def wide_part(m, j, t, n, twice=False):
            hs = (heads, kvh)[j]
            a = parts[j][:, m, t, :].rearrange("p (h d) -> p h d", d=hd).unsqueeze(2)
            return a.broadcast_to([P, hs, 2 if twice else n, hd])

        def by_head(bank):
            return bank[:, :, :].rearrange("p s (j r) -> p (s j) r", r=32)

        @block.gpsimd
        def _(pool):
            for k in range(2):
                if k < stacks:
                    nc.gpsimd.memset(stack[k][0][:, :, :, :], 0.0)
                    nc.gpsimd.memset(stack[k][1][:, :, :, :], 0.0)
                if not latent:
                    nc.gpsimd.memset(v1[k][:, :, :, hd + 1:], 0.0)
                    ins = nc.gpsimd.memset(v1[k][:, :, :, hd:hd + 1], 1.0)
            if softmax:
                nc.gpsimd.memset(sel[:, :, :], 0.0)
                ins = nc.gpsimd.memset(ntop[:, :, :], 0.0)
            ins.then_inc(S["init"], 1)
            pool.wait_ge(S["init"], 1)
            if softmax:
                nc.gpsimd.affine_select(out=sel[:, :, :], in_=sel[:, :, :], compare_op=ALU.not_equal, fill=1.0,
                                        base=0, pattern=[[-1, heads], [0, P]], channel_multiplier=1)\
                    .then_inc(S["sel"], 1)
                pool.wait_ge(S["sel"], 1)
                nc.gpsimd.affine_select(out=sel[:, :, :], in_=sel[:, :, :], compare_op=ALU.not_equal, fill=1.0,
                                        base=-heads, pattern=[[-1, heads], [0, P]], channel_multiplier=1)\
                    .then_inc(S["sel"], 1)

            def values_in(i, k):
                pool.wait_ge(S["pv"], i * 2)
                t = bass.ds(i * QT, QT)
                v = on.kv[:, t, kvh * hd:] if latent else on.v[:, t, :]
                nc.gpsimd.tensor_copy(v1[k][:, :, :, 0:hd], v.rearrange("p t (h d) -> p t h d", d=hd))\
                    .then_inc(S["v1"], 1)

            def stack_q(i, k):
                pool.wait_ge(S["part3"], i + 1)
                pool.wait_ge(S["turned"], i * 4 + 2)
                if latent:
                    for t in range(QT):
                        q = on.q2[:, bass.ds(i * QT + t, 1), :].rearrange("p t (h d) -> p (t h) d", d=hd)
                        nc.gpsimd.tensor_copy(wide_slots(k, 0, t, 0, 3),
                                              q.unsqueeze(2).broadcast_to([P, heads, 3, hd]))
                        for m, lo, n in ((1, 3, 1), (1, 4, 1), (2, 5, 1)):
                            ins = nc.gpsimd.tensor_copy(wide_slots(k, 0, t, lo, n), wide_part(m, 0, t, n))
                    ins.then_inc(S["stack0"], 1)
                    return
                q = on.q[:, bass.ds(i * QT, QT), :].rearrange("p t (h d) -> p (t h) d", d=hd).unsqueeze(2)
                nc.gpsimd.tensor_copy(slots(k, 0, 0, 3), q.broadcast_to([P, QT * heads, 3, hd]))
                for m, lo, n in ((1, 3, 2), (2, 5, 1)):
                    ins = nc.gpsimd.tensor_copy(slots(k, 0, lo, n), part(m, 0, n))
                ins.then_inc(S["stack0"], 1)

            software_pipeline(nc.gpsimd.Fori, [(values_in, LAG), (stack_q, 0)], BATCH)

        @block.vector
        def _(dve):
            dve.sem_inc(S["topout" if softmax else "probs"], 2)
            dve.wait_ge(S["w"], 16 * len(loads))
            dve.wait_ge(S["init"], 1)
            if not softmax:
                nc.vector.memset(causal3[:, P:2 * P], 1.0)
                nc.vector.tensor_copy(causal3[:, 0:P], on.causal[:, :])
                nc.vector.tensor_copy(causal3[:, 2 * P:], on.causal[:, :]).then_inc(S["neg"], 1)
                dve.wait_ge(S["neg"], 1)

            def split(i, k):
                dve.wait_ge(S["stack0"], i)
                dve.wait_ge(S["stack1"], i)
                t = bass.ds(i * QT, QT)
                src = (q_of(t), k_of(t))
                for j in range(2):
                    ins = nc.vector.tensor_copy(parts[j][:, 0, :, :], src[j])
                ins.then_inc(S["part1"], 1)
                dve.wait_ge(S["part1"], i + 1)
                for j in range(2):
                    ins = nc.vector.tensor_tensor(rest[j][:, :, :], src[j], parts[j][:, 0, :, :], ALU.subtract)
                ins.then_inc(S["rest1"], 1)
                dve.wait_ge(S["rest1"], i + 1)
                for j in range(2):
                    ins = nc.vector.tensor_copy(parts[j][:, 1, :, :], rest[j][:, :, :])
                ins.then_inc(S["part2"], 1)
                dve.wait_ge(S["part2"], i + 1)
                for j in range(2):
                    ins = nc.vector.tensor_tensor(parts[j][:, 2, :, :], rest[j][:, :, :], parts[j][:, 1, :, :],
                                                  ALU.subtract)
                ins.then_inc(S["part3"], 1)
                dve.wait_ge(S["part3"], i + 1)
                dve.wait_ge(S["turned"], i * 4 + 4)
                if latent:
                    for t in range(QT):
                        for m, lo in ((0, 0), (1, 1), (2, 2), (0, 3)):
                            nc.vector.tensor_copy(wide_slots(k, 1, t, lo, 1), wide_part(m, 1, t, 1))
                        for m, lo in ((1, 4), (0, 5)):
                            out = stack[k][1][:, t, kvh:, :].rearrange("p b (e s) -> p b e s", s=2 * hd)
                            ins = nc.vector.tensor_copy(out[:, :, :, (lo - 4) * hd:(lo - 3) * hd],
                                                        wide_part(m, 1, t, 1, twice=True))
                    ins.then_inc(S["stack1"], 1)
                    return
                for m, lo in ((0, 0), (1, 1), (2, 2), (0, 3), (1, 4), (0, 5)):
                    ins = nc.vector.tensor_copy(slots(k, 1, lo, 1), part(m, 1, 1))
                ins.then_inc(S["stack1"], 1)

            def top(i, k):
                for h in range(heads):
                    dve.wait_ge(S["top"], i * heads + h + 1)
                    nc.vector.reduce_max(tops[:, 0, h:h + 1], top_ps[h % 2][:, 0:P], AX.X)
                    nc.vector.reduce_max(tops[:, 1, h:h + 1], top_ps[h % 2][:, P:CW], AX.X).then_inc(S["topout"], 1)
                dve.wait_ge(S["topout"], (i + 1) * heads + 2)
                dve.wait_ge(S["ntopTp"], i)
                nc.vector.tensor_scalar(ntop[:, :, 0:heads], tops[:, :, :], -1.0, None, ALU.mult).then_inc(S["neg"], 1)
                dve.wait_ge(S["neg"], i + 1)
                nc.vector.scalar_tensor_tensor(ntop[:, :, heads:2 * heads], tops[:, :, :], -1.0, ntop[:, :, 0:heads],
                                               ALU.mult, ALU.subtract).then_inc(S["ntop"], 1)
                dve.wait_ge(S["ntop"], i + 1)

            def masked(i, k):
                for h in range(heads):
                    dve.wait_ge(S["score"], i * heads + h + 1)
                    nc.vector.tensor_tensor(probs[k][:, h, :], score_ps[h % 2][:, 0:CW], causal3[:, :], ALU.mult)\
                        .then_inc(S["probs"], 1)

            def normalise(t):
                def fn(i, k):
                    n = i * QT + t
                    dve.wait_ge(S["tokmaj"], n + 1)
                    if latent:
                        den = desk[:, 2, :].rearrange("p (j r) -> p r j", r=32)[:, 0:kvh, :]
                        sums = desk[:, 0:2, :].rearrange("p g (j d) -> p (g j) d", d=hd)
                        nc.vector.reciprocal(rden[:, :].rearrange("p (g j) -> p g j", g=kvh), den)\
                            .then_inc(S["rden"], 1)
                    else:
                        sums = by_head(desk)[:, :, 0:hd]
                        nc.vector.reciprocal(rden[:, :], by_head(desk)[:, :, hd]).then_inc(S["rden"], 1)
                    dve.wait_ge(S["rden"], n + 1)
                    nc.vector.tensor_tensor(o_sb[:, t, :, :], sums,
                                            rden[:, :].unsqueeze(2).broadcast_to([P, heads, hd]), ALU.mult)\
                        .then_inc(S["o"], 1)
                    dve.wait_ge(S["o"], n + 1)
                return fn

            def store(i, k):
                dve.wait_ge(S["out"], i + 1)
                if latent:
                    nc.vector.tensor_copy(on.s[:, bass.ds(i * QT, QT), :], out_ps).then_inc(S["s"], 1)
                    return
                nc.vector.tensor_tensor(on.s[:, bass.ds(i * QT, QT), :], out_ps,
                                        bo[:, :].unsqueeze(1).broadcast_to([P, QT, D]), ALU.add).then_inc(S["s"], 1)

            steps = [(store, LAG + 3), (normalise(0), LAG + 2), (normalise(1), LAG + 2), (split, 0)]
            steps.insert(1, (top, 1)) if softmax else steps.insert(3, (masked, LAG))
            software_pipeline(nc.vector.Fori, steps, BATCH)

        @block.tensor
        def _(pe):
            pe.sem_inc(S["turned"], 4 * stacks)
            pe.sem_inc(S["pv"], 2)
            pe.wait_ge(S["w"], 16 * len(loads))
            if softmax:
                pe.wait_ge(S["sel"], 2)

            def turn(i, k):
                for n in range(4):
                    j = int(n >= Q_FILLS)
                    block = 4 * (n - Q_FILLS if j else n)
                    pe.wait_ge(S[f"stack{j}"], i + 1)
                    pe.wait_ge(S["opT"], i * 4 + n)
                    for p in range(4):
                        for t in range(QT):
                            ins = nc.tensor.transpose(opT_ps[:, p, t * P:(t + 1) * P],
                                                      stack[k][j][:, t, block + p, :], on.ident_bf[:, :])
                    ins.then_inc(S["turned"], 1)

            def operands(k, h, q0, q1, k0, k1):
                q, key = (slice(q0 * P, q1 * P), slice(k0 * P, k1 * P))
                r = slice(SLOT * (h % 2), SLOT * (h % 2) + SLOT)
                if not latent:
                    return [(opT[k][0][r, h // 2, q], opT[k][1][r, h // 2, key])]
                g = h // (heads // kvh)
                return [(opT[k][0][:, h, q], opT[k][1][:, g, key]),
                        (opT[k][0][r, heads + h // 2, q], opT[k][1][r, kvh + g, key])]

            def tops_(i, k):
                pe.wait_ge(S["opT"], (i + 1) * 4)
                for h in range(heads):
                    pe.wait_ge(S["topout"], i * heads + h + 1)
                    bank = top_ps[h % 2]
                    for qt, lo, hi, m0 in ((0, 0, P, 0), (1, P, CW, 2 * P)):
                        for n, (q, key) in enumerate(operands(k, h, qt, qt + 1, 0, qt + 1)):
                            nc.tensor.matmul(bank[:, lo:hi], q, key, start=(n == 0), stop=True,
                                             skip_group_check=(n > 0))
                        ins = nc.tensor.matmul(bank[:, m0:m0 + P], on.ident_bf[:, :], on.mask_qk[:, 0, :],
                                               start=False, stop=True, skip_group_check=True)
                    ins.then_inc(S["top"], 1)

            def turn_tops(i, k):
                pe.wait_ge(S["ntop"], i + 1)
                pe.wait_ge(S["oT"], i)
                for t in range(QT):
                    ins = nc.tensor.transpose(ntopT_ps[:, t * P:(t + 1) * P], ntop[:, t, :], on.ident_bf[:, :])
                ins.then_inc(S["ntopTp"], 1)

            def scores(i, k):
                if softmax:
                    pe.wait_ge(S["ntopT"], i + 1)
                else:
                    pe.wait_ge(S["opT"], (i + 1) * 4)
                for h in range(heads):
                    pe.wait_ge(S["probs"], i * heads + h + 1)
                    bank = score_ps[h % 2]
                    for kt, lo, hi, m0 in ((0, 0, 2 * P, 0), (1, 2 * P, CW, 2 * P)):
                        for n, (q, key) in enumerate(operands(k, h, kt, QT, kt, kt + 1)):
                            ins = nc.tensor.matmul(bank[:, lo:hi], key, q, start=(n == 0), stop=True,
                                                   skip_group_check=(n > 0))
                        if softmax:
                            nc.tensor.matmul(bank[:, lo:hi], sel[:, h, :], ntopT[k][:, kt * P:], start=False,
                                             stop=True, skip_group_check=True)
                            ins = nc.tensor.matmul(bank[:, m0:m0 + P], on.ident_bf[:, :], on.mask_kq[:, 0, :],
                                                   start=False, stop=True, skip_group_check=True)
                    ins.then_inc(S["score"], 1)

            def values(half):
                def fn(i, k):
                    if half == 0:
                        pe.wait_ge(S["probs"], (i + 1) * heads + 2)
                        pe.wait_ge(S["v1"], i + 1)
                    pe.wait_ge(S["pvout"], i * 2 + half)
                    if latent and half:
                        for kt, lo in ((0, 0), (1, 2 * P)):
                            for g in range(kvh):
                                for j in range(4):
                                    ins = nc.tensor.matmul(
                                        pv_ps[1][32 * j:32 * j + 32, 0, kt * P:SEQ], den_cols[:, g, :],
                                        probs[k][:, 4 * g + j, lo:lo + (QT - kt) * P],
                                        start=(kt == 0 and g == 0), stop=True, skip_group_check=True)
                        ins.then_inc(S["pv"], 1)
                        return
                    for strip in range(2):
                        for kt, lo in ((0, 0), (1, 2 * P)):
                            for j in range(4):
                                h = (0 if latent else half * HALF) + strip * 4 + j
                                ins = nc.tensor.matmul(
                                    pv_ps[half][32 * j:32 * j + 32, strip, kt * P:SEQ],
                                    v1[k][:, kt, strip if latent else h, :],
                                    probs[k][:, h, lo:lo + (QT - kt) * P],
                                    start=(kt == 0), stop=(kt == 1), skip_group_check=True)
                    ins.then_inc(S["pv"], 1)
                return fn

            def token_major(t):
                def fn(i, k):
                    if t == 0:
                        pe.wait_ge(S["pvout"], (i + 1) * 2)
                        pe.wait_ge(S["s"], i)
                    else:
                        pe.wait_ge(S["o"], i * QT + t)
                    for strip in range(STRIPS):
                        ins = nc.tensor.transpose(desk[:, strip, :], pv_sb[:, strip, t * P:(t + 1) * P], on.ident[:, :])
                    ins.then_inc(S["tokmaj"], 1)
                return fn

            def turn_output(i, k):
                pe.wait_ge(S["o"], (i + 1) * QT)
                for t in range(QT):
                    for c in range(OB):
                        o = o_sb[:, t, :, :].rearrange("p h d -> p (h d)")[:, c * P:(c + 1) * P]
                        ins = nc.tensor.transpose(desk[:, t * OB + c, :], o, on.ident[:, :])
                ins.then_inc(S["oturned"], 1)

            def output(i, k):
                pe.wait_ge(S["oT"], i + 3)
                if softmax:
                    pe.wait_ge(S["ntopT"], upto(i + 4, BATCH))
                for t in range(QT):
                    for c in range(OB):
                        ins = nc.tensor.matmul(desk[:, t, :], oT[:, t, c, :], wo[:, c, :], start=(c == 0),
                                               stop=(c == OB - 1))
                ins.then_inc(S["out"], 1)

            tail = [(token_major(0), LAG + 2), (values(0), LAG + 1), (token_major(1), LAG + 2), (values(1), LAG + 1),
                    (turn_output, LAG + 2), (scores, LAG)]
            if softmax:
                steps = [(output, LAG + 3), (tops_, 1)] + tail + [(turn_tops, 1), (turn, 0)]
            else:
                steps = [(output, LAG + 3)] + tail + [(turn, 0)]
            software_pipeline(nc.tensor.Fori, steps, BATCH)

        @block.scalar
        def _(act):
            if softmax:
                act.sem_inc(S["probs"], 2)

            def exps(i, k):
                for h in range(heads):
                    act.wait_ge(S["score"], i * heads + h + 1)
                    nc.scalar.activation(probs[k][:, h, :], score_ps[h % 2][:, 0:CW], ACT.Exp, scale=softmax_scale)\
                        .then_inc(S["probs"], 1)

            def copy_tops(i, k):
                act.wait_ge(S["ntopTp"], i + 1)
                nc.scalar.activation(ntopT[k][:, :], ntopT_ps, ACT.Copy).then_inc(S["ntopT"], 1)

            def copy_operands(i, k):
                for n in range(4):
                    act.wait_ge(S["turned"], i * 4 + n + 1 + 4 * stacks)
                    j = int(n >= Q_FILLS)
                    block = 4 * (n - Q_FILLS if j else n)
                    nc.scalar.activation(opT[k][j][:, block:block + 4, :], opT_ps[:, :, :], ACT.Copy)\
                        .then_inc(S["opT"], 1)

            def take_values(half):
                def fn(i, k):
                    act.wait_ge(S["pv"], i * 2 + half + 3)
                    act.wait_ge(S["tokmaj"], i * QT)
                    n = 1 if latent and half else 2
                    nc.scalar.activation(pv_sb[:, 2 * half:2 * half + n, :], pv_ps[half][:, 0:n, :], ACT.Copy)\
                        .then_inc(S["pvout"], 1)
                return fn

            def copy_output(i, k):
                act.wait_ge(S["oturned"], i + 1)
                act.wait_ge(S["out"], i)
                nc.scalar.activation(oT[:, :, :, :].rearrange("p t c d -> p (t c) d"), desk[:, 0:QT * OB, :], ACT.Copy)\
                    .then_inc(S["oT"], 1)

            act.sem_inc(S["oT"], 2)
            steps = [(take_values(0), LAG + 1), (take_values(1), LAG + 1), (copy_output, LAG + 2), (copy_operands, 0)]
            if softmax:
                steps[3:3] = [(exps, 2), (copy_tops, 1)]
            software_pipeline(nc.scalar.Fori, steps, BATCH)


def channel_attention_stage(nc, on, name, dram, heads, hd):
    PAIRS = heads // 2
    assert 2 * hd == P and PAIRS * P == 2 * COLS
    ctx, sb, pb, sem = scope(nc)
    with ctx:
        w_q, w_k = sb(f"{name}_wq", [P, PAIRS, P]), sb(f"{name}_wk", [P, PAIRS, P])
        w_vT, w_out = sb(f"{name}_wvT", [P, PAIRS, P]), sb(f"{name}_wout", [P, PAIRS, P])
        temp, gamma = sb(f"{name}_temp", [P, PAIRS]), sb(f"{name}_gamma", [P, D])
        square = sb(f"{name}_square", [P, TILES, D])
        norm2, norm = sb(f"{name}_norm2", [P, TILES]), sb(f"{name}_norm", [P, TILES])
        x_b = [sb(f"{name}_x{k}", [P, QT, D]) for k in range(2)]
        xT = sb(f"{name}_xT", [P, TOKENS])
        xT_b = sb(f"{name}_xTb", [P, SEQ])
        gram = [sb(f"{name}_gram{k}", [P, P]) for k in range(2)]
        tk = [sb(f"{name}_tk{k}", [P, PAIRS, P]) for k in range(2)]
        sq_k, sq_q = sb(f"{name}_sqk", [P, PAIRS, P]), sb(f"{name}_sqq", [P, PAIRS, P])
        rk, rq = sb(f"{name}_rk", [P, PAIRS, hd]), sb(f"{name}_rq", [P, PAIRS])
        rk_root, rq_root = sb(f"{name}_rkroot", [P, PAIRS, hd]), sb(f"{name}_rqroot", [P, PAIRS])
        logit = sb(f"{name}_logit", [P, PAIRS, hd])
        top, total = sb(f"{name}_top", [P, PAIRS]), sb(f"{name}_total", [P, PAIRS])
        attn = [sb(f"{name}_attn{k}", [P, PAIRS, P]) for k in range(2)]
        u_sb, m_sb = sb(f"{name}_u", [P, PAIRS, P]), sb(f"{name}_m", [P, P])
        tk_ps, tq_ps = pb(f"{name}_tkp", [P, 2, COLS]), pb(f"{name}_tqp", [P, 2, COLS])
        pair_ps = pb(f"{name}_pairp", [P, PAIRS, P])
        rk_ps = pb(f"{name}_rkp", [P, PAIRS, hd])
        gram_ps = pb(f"{name}_gramp", [P, 4, P])
        S = {w: sem(f"{name}_{w}") for w in (
            "w", "zero", "pre", "preroot", "temp", "x", "gramp", "gram", "tkq", "tk", "sq", "norms", "roots", "clip", "inv", "r",
            "simp", "logit", "chain", "exp", "sum", "attn", "up", "u", "mp", "m", "xTb", "out", "s")}
        block = ctx.enter_context(nc.Block())
        loads = [(w_q[:, :, :], dram["w_q"]), (w_k[:, :, :], dram["w_k"]), (w_vT[:, :, :], dram["w_vT"]),
                 (w_out[:, :, :], dram["w_out"]), (temp[:, :], dram["temp"]), (gamma[:, :], dram["gamma"])]
        halves = (slice(0, hd), slice(hd, P))

        @block.sync
        def _(sp):
            for dst, src in loads:
                sp.dma_start(dst, src).then_inc(S["w"], 16)

        @block.gpsimd
        def _(pool):
            for k in range(2):
                ins = nc.gpsimd.memset(attn[k][:, :, :], 0.0)
            ins.then_inc(S["zero"], 1)

            def copy_x(i, k):
                pool.wait_ge(S["out"], i)
                pool.wait_ge(S["gram"], i * 2 + 2)
                nc.gpsimd.tensor_copy(xT_b[:, :], xT[:, bass.ts(i, SEQ)]).then_inc(S["xTb"], 1)

            software_pipeline(nc.gpsimd.Fori, [(copy_x, 0)], BATCH)

        @block.vector
        def _(dve):
            dve.wait_ge(S["w"], 16 * len(loads))
            dve.wait_ge(S["zero"], 1)
            dve.sem_inc(S["s"], 2)
            nc.vector.tensor_tensor(square[:, :, :], on.xn[:, :, :], on.xn[:, :, :], ALU.mult).then_inc(S["pre"], 1)
            dve.wait_ge(S["pre"], 1)
            nc.vector.tensor_reduce(norm2[:, :], square[:, :, :], AX.X, ALU.add).then_inc(S["pre"], 1)
            dve.wait_ge(S["pre"], 2)
            nc.vector.tensor_scalar(norm2[:, :], norm2[:, :], 1e-24, 1.0 / D, ALU.max, ALU.mult).then_inc(S["pre"], 1)
            dve.wait_ge(S["preroot"], 1)
            nc.vector.reciprocal(norm[:, :], norm[:, :]).then_inc(S["pre"], 1)
            dve.wait_ge(S["temp"], 1)
            nc.vector.tensor_scalar(temp[:, :], temp[:, :], 8.0, None, ALU.mult).then_inc(S["pre"], 1)
            dve.wait_ge(S["pre"], 5)

            def x_in(i, k):
                dve.wait_ge(S["gramp"], i + 1)
                for t in range(QT):
                    ins = nc.vector.scalar_tensor_tensor(
                        x_b[k][:, t, :], on.xn[:, bass.ds(i * QT + t, 1), :], norm[:, bass.ds(i * QT + t, 1)],
                        gamma[:, :], ALU.mult, ALU.mult)
                ins.then_inc(S["x"], 1)

            def scores(i, k):
                dve.wait_ge(S["simp"], i + 1)
                dve.wait_ge(S["r"], i + 1)
                for r in halves:
                    ins = nc.vector.tensor_tensor(logit[r, :, :], pair_ps[r, :, r], rk[r, :, :], ALU.mult)
                ins.then_inc(S["logit"], 1)
                dve.wait_ge(S["logit"], i + 1)

                def wide(a):
                    return a[:, :].unsqueeze(2).broadcast_to([P, PAIRS, hd])

                nc.vector.tensor_tensor(logit[:, :, :], logit[:, :, :], wide(rq), ALU.mult).then_inc(S["chain"], 1)
                dve.wait_ge(S["chain"], i * 3 + 1)
                nc.vector.tensor_reduce(top[:, :], logit[:, :, :], AX.X, ALU.max).then_inc(S["chain"], 1)
                dve.wait_ge(S["chain"], i * 3 + 2)
                nc.vector.tensor_tensor(logit[:, :, :], logit[:, :, :], wide(top), ALU.subtract).then_inc(S["chain"], 1)

            def squares(i, k):
                dve.wait_ge(S["tkq"], i + 1)
                dve.wait_ge(S["norms"], i)
                nc.vector.tensor_tensor(sq_q[:, :, :].rearrange("p a b -> p (a b)"),
                                        tq_ps[:, :, :].rearrange("p a b -> p (a b)"),
                                        w_q[:, :, :].rearrange("p a b -> p (a b)"), ALU.mult)
                dve.wait_ge(S["tk"], i + 1)
                ins = nc.vector.tensor_tensor(sq_k[:, :, :], tk[k][:, :, :], w_k[:, :, :], ALU.mult)
                ins.then_inc(S["sq"], 1)

            def weights(i, k):
                dve.wait_ge(S["exp"], i + 1)
                nc.vector.tensor_reduce(total[:, :], logit[:, :, :], AX.X, ALU.add).then_inc(S["sum"], 1)
                dve.wait_ge(S["sum"], i * 2 + 1)
                nc.vector.reciprocal(total[:, :], total[:, :]).then_inc(S["sum"], 1)
                dve.wait_ge(S["sum"], i * 2 + 2)
                dve.wait_ge(S["up"], i + 1)
                for r in halves:
                    ins = nc.vector.tensor_tensor(attn[k][r, :, r], logit[r, :, :],
                                                  total[r, :].unsqueeze(2).broadcast_to([hd, PAIRS, hd]), ALU.mult)
                ins.then_inc(S["attn"], 1)
                dve.wait_ge(S["attn"], i + 1)

            def inverse_norms(i, k):
                dve.wait_ge(S["roots"], i + 1)
                nc.vector.tensor_scalar(rk_root[:, :, :], rk_root[:, :, :], 1e-12, None, ALU.max)
                nc.vector.tensor_scalar(rq_root[:, :], rq_root[:, :], 1e-12, None, ALU.max).then_inc(S["clip"], 1)
                dve.wait_ge(S["clip"], i + 1)
                nc.vector.reciprocal(rk[:, :, :], rk_root[:, :, :])
                nc.vector.reciprocal(rq[:, :], rq_root[:, :]).then_inc(S["inv"], 1)
                dve.wait_ge(S["inv"], i + 1)
                nc.vector.tensor_tensor(rq[:, :], rq[:, :], temp[:, :], ALU.mult).then_inc(S["r"], 1)

            def store(i, k):
                dve.wait_ge(S["out"], i + 1)
                nc.vector.tensor_copy(on.s[:, bass.ds(i * QT, QT), :],
                                      tk_ps[:, 1, 0:SEQ].rearrange("p (t d) -> p t d", t=QT)).then_inc(S["s"], 1)

            software_pipeline(nc.vector.Fori, [(x_in, 0), (scores, 2), (squares, 1), (weights, 2), (inverse_norms, 1),
                                               (store, 3)], BATCH)

        @block.tensor
        def _(pe):
            pe.sem_inc(S["gramp"], 2)
            pe.sem_inc(S["up"], 2)
            pe.wait_ge(S["w"], 16 * len(loads))

            def gram_of(i, k):
                pe.wait_ge(S["x"], i + 1)
                pe.wait_ge(S["gram"], i * 2)
                for t in range(QT):
                    nc.tensor.matmul(gram_ps[:, 0, :], x_b[k][:, t, :], x_b[k][:, t, :], start=(t == 0),
                                     stop=(t == QT - 1))
                for t in range(QT):
                    ins = nc.tensor.transpose(gram_ps[:, 1 + t, :], x_b[k][:, t, :], on.ident[:, :])
                ins.then_inc(S["gramp"], 1)

            def sims(i, k):
                pe.wait_ge(S["tk"], i + 1)
                pe.wait_ge(S["u"], i)
                for p in range(PAIRS):
                    ins = nc.tensor.matmul(pair_ps[:, p, :], w_q[:, p, :], tk[k][:, p, :], start=True, stop=True)
                ins.then_inc(S["simp"], 1)

            def gram_w(i, k):
                pe.wait_ge(S["gram"], i * 2 + 2)
                pe.wait_ge(S["s"], i)
                pe.wait_ge(S["roots"], i)
                for w, ps in ((w_k, tk_ps), (w_q, tq_ps)):
                    for c in range(2):
                        ins = nc.tensor.matmul(ps[:, c, :], gram[k][:, :],
                                               w[:, 4 * c:4 * c + 4, :].rearrange("p a b -> p (a b)"),
                                               start=True, stop=True)
                ins.then_inc(S["tkq"], 1)

            def mix(i, k):
                pe.wait_ge(S["attn"], i + 1)
                pe.wait_ge(S["logit"], upto(i + 2, BATCH))
                for p in range(PAIRS):
                    ins = nc.tensor.matmul(pair_ps[:, p, :], attn[k][:, p, :], w_out[:, p, :], start=True, stop=True)
                ins.then_inc(S["up"], 1)

            def norms(i, k):
                pe.wait_ge(S["sq"], i + 1)
                pe.wait_ge(S["roots"], i)
                for half, r in enumerate(halves):
                    nc.tensor.matmul(rk_ps[r, :, :], on.ones[:, 0:hd], sq_k[:, :, r], start=True, stop=True)
                for p in range(PAIRS):
                    ins = nc.tensor.matmul(tq_ps[:, 0, p:p + 1], sq_q[:, p, :], on.ones[:, 0:1], start=True, stop=True)
                ins.then_inc(S["norms"], 1)

            def fold(i, k):
                pe.wait_ge(S["u"], i + 2)
                pe.wait_ge(S["tk"], upto(i + 3, BATCH))
                pe.wait_ge(S["sq"], upto(i + 3, BATCH))
                for p in range(PAIRS):
                    ins = nc.tensor.matmul(tk_ps[:, 0, 0:P], w_vT[:, p, :], u_sb[:, p, :], start=(p == 0),
                                           stop=(p == PAIRS - 1))
                ins.then_inc(S["mp"], 1)

            def output(i, k):
                pe.wait_ge(S["m"], i + 1)
                pe.wait_ge(S["xTb"], i + 1)
                pe.wait_ge(S["s"], i + 2)
                for t in range(QT):
                    ins = nc.tensor.matmul(tk_ps[:, 1, t * P:(t + 1) * P], xT_b[:, t * P:(t + 1) * P], m_sb[:, :],
                                           start=True, stop=True)
                ins.then_inc(S["out"], 1)

            software_pipeline(nc.tensor.Fori, [(gram_of, 0), (sims, 2), (gram_w, 1), (mix, 3), (norms, 1), (fold, 3),
                                               (output, 3)], BATCH)

        @block.scalar
        def _(act):
            act.sem_inc(S["u"], 1)
            act.wait_ge(S["w"], 16 * len(loads))
            act.wait_ge(S["pre"], 3)
            nc.scalar.activation(norm[:, :], norm2[:, :], ACT.Sqrt).then_inc(S["preroot"], 1)
            nc.scalar.activation(temp[:, :], temp[:, :], ACT.Exp).then_inc(S["temp"], 1)

            def copy_gram(i, k):
                act.wait_ge(S["gramp"], i + 3)
                nc.scalar.activation(gram[k][:, :], gram_ps[:, 0, :], ACT.Copy).then_inc(S["gram"], 1)
                nc.scalar.activation(xT[:, bass.ts(i, SEQ)], gram_ps[:, 1:3, :].rearrange("p t d -> p (t d)"), ACT.Copy)\
                    .then_inc(S["gram"], 1)

            def exps(i, k):
                act.wait_ge(S["chain"], i * 3 + 3)
                nc.scalar.activation(logit[:, :, :], logit[:, :, :], ACT.Exp).then_inc(S["exp"], 1)

            def copy_tk(i, k):
                act.wait_ge(S["tkq"], i + 1)
                act.wait_ge(S["simp"], i)
                nc.scalar.activation(tk[k][:, :, :].rearrange("p a b -> p (a b)"),
                                     tk_ps[:, :, :].rearrange("p a b -> p (a b)"), ACT.Copy).then_inc(S["tk"], 1)

            def copy_u(i, k):
                act.wait_ge(S["up"], i + 3)
                act.wait_ge(S["mp"], i)
                nc.scalar.activation(u_sb[:, :, :], pair_ps[:, :, :], ACT.Copy).then_inc(S["u"], 1)

            def roots(i, k):
                act.wait_ge(S["norms"], i + 1)
                act.wait_ge(S["r"], i)
                nc.scalar.activation(rk_root[:, :, :], rk_ps[:, :, :], ACT.Sqrt)
                nc.scalar.activation(rq_root[:, :], tq_ps[:, 0, 0:PAIRS], ACT.Sqrt).then_inc(S["roots"], 1)

            def copy_m(i, k):
                act.wait_ge(S["mp"], i + 1)
                act.wait_ge(S["out"], i)
                nc.scalar.activation(m_sb[:, :], tk_ps[:, 0, 0:P], ACT.Copy).then_inc(S["m"], 1)

            software_pipeline(nc.scalar.Fori, [(copy_gram, 0), (exps, 2), (copy_tk, 1), (copy_u, 3), (roots, 1),
                                               (copy_m, 3)], BATCH)


def centroid_route_stage(nc, on, name, dram, experts, combine, w1, b1, chunks):
    ctx, sb, pb, sem = scope(nc)
    with ctx:
        centT, b2 = sb(f"{name}_centT", [P, experts]), sb(f"{name}_b2", [experts, D])
        ln_g, ln_b = sb(f"{name}_lng", [P, experts]), sb(f"{name}_lnb", [P, experts])
        rank_w = sb(f"{name}_rankw", [P, experts])
        aff, pick = sb(f"{name}_aff", [P, TILES, experts]), sb(f"{name}_pick", [P, TILES, experts])
        best, first, alpha = (sb(f"{name}_{w}", [P, TILES]) for w in ("best", "first", "alpha"))
        combT = [sb(f"{name}_combT{k}", [experts, COLS]) for k in range(2)]
        aff_ps = pb(f"{name}_affp", [P, COLS])
        bias_ps = pb(f"{name}_biasp", [P, COLS])
        turn_ps = [pb(f"{name}_turnp{k}", [P, COLS]) for k in range(2)]
        init_ps = [pb(f"{name}_initp{k}", [P, TPB, D]) for k in range(2)]
        S = {w: sem(f"{name}_{w}") for w in ("w", "aff", "bias", "chain", "alpha", "scaled", "turned", "combT", "init",
                                             "g")}
        loads = [(centT[:, :], dram["centT"]), (b2[:, :], dram["b2"]), (ln_g[:, :], dram["ln_g"]),
                 (ln_b[:, :], dram["ln_b"]), (rank_w[:, :], dram["rank_w"]), (w1[:, :, :], dram["w1"]),
                 (b1[:, :, :].rearrange("p e c -> p (e c)"), dram["b1"])]
        block = ctx.enter_context(nc.Block())

        @block.sync
        def _(sp):
            for dst, src in loads:
                sp.dma_start(dst, src).then_inc(S["w"], 16)

        @block.tensor
        def _(pe):
            pe.wait_ge(S["w"], 16 * len(loads))
            for t in range(TILES):
                ins = nc.tensor.matmul(aff_ps[:, t * experts:(t + 1) * experts], on.xnT[:, t * P:(t + 1) * P],
                                       centT[:, :], start=True, stop=True)
            ins.then_inc(S["aff"], 1)
            for e in range(experts):
                for c in range(chunks):
                    n = e * chunks + c
                    ins = nc.tensor.matmul(bias_ps[:, n:n + 1], w1[:, e, c * P:(c + 1) * P], ln_b[:, e:e + 1],
                                           start=True, stop=True)
            ins.then_inc(S["bias"], 1)
            pe.wait_ge(S["chain"], 7)
            for i in range(BLOCKS + 1):
                if i < BLOCKS:
                    if i >= 2:
                        pe.wait_ge(S["combT"], i - 1)
                    for t in range(TPB):
                        ins = nc.tensor.transpose(turn_ps[i % 2][0:experts, t * P:(t + 1) * P],
                                                  combine[:, i * TPB + t, :], on.ident[:, :])
                    ins.then_inc(S["turned"], 1)
                if i:
                    pe.wait_ge(S["combT"], i)
                    if i >= 3:
                        pe.wait_ge(S["g"], i - 2)
                    for t in range(TPB):
                        ins = nc.tensor.matmul(init_ps[(i - 1) % 2][:, t, :], combT[(i - 1) % 2][:, t * P:(t + 1) * P],
                                               b2[:, :], start=True, stop=True)
                    ins.then_inc(S["init"], 1)

        @block.scalar
        def _(act):
            act.wait_ge(S["chain"], 2)
            nc.scalar.activation(alpha[:, :], best[:, :], ACT.Sigmoid).then_inc(S["alpha"], 1)
            for i in range(BLOCKS):
                act.wait_ge(S["turned"], i + 1)
                if i >= 2:
                    act.wait_ge(S["init"], i - 1)
                nc.scalar.activation(combT[i % 2][:, :], turn_ps[i % 2][0:experts, :], ACT.Copy)\
                    .then_inc(S["combT"], 1)

        @block.vector
        def _(dve):
            done = [0]

            def link(ins):
                done[0] += 1
                ins.then_inc(S["chain"], 1)
                dve.wait_ge(S["chain"], done[0])

            def wide(a):
                return a[:, :].unsqueeze(2).broadcast_to([P, TILES, experts])

            dve.wait_ge(S["w"], 16 * len(loads))
            dve.wait_ge(S["aff"], 1)
            link(nc.vector.tensor_copy(aff[:, :, :].rearrange("p t e -> p (t e)"), aff_ps[:, 0:TILES * experts]))
            link(nc.vector.tensor_reduce(best[:, :], aff[:, :, :], AX.X, ALU.max))
            link(nc.vector.tensor_tensor(pick[:, :, :], aff[:, :, :], wide(best), ALU.is_equal))
            link(nc.vector.tensor_tensor(pick[:, :, :], pick[:, :, :],
                                         rank_w[:, :].unsqueeze(1).broadcast_to([P, TILES, experts]), ALU.mult))
            link(nc.vector.tensor_reduce(first[:, :], pick[:, :, :], AX.X, ALU.max))
            link(nc.vector.tensor_tensor(pick[:, :, :], pick[:, :, :], wide(first), ALU.is_equal))
            dve.wait_ge(S["alpha"], 1)
            link(nc.vector.tensor_tensor(combine[:, :, :], pick[:, :, :], wide(alpha), ALU.mult))
            dve.wait_ge(S["bias"], 1)
            flat = b1[:, :, :].rearrange("p e c -> p (e c)")
            nc.vector.tensor_tensor(flat, flat, bias_ps[:, 0:experts * chunks], ALU.add)
            for e in range(experts):
                nc.vector.tensor_scalar(w1[:, e, :], w1[:, e, :], ln_g[:, e:e + 1], None, ALU.mult)
            for i in range(BLOCKS):
                dve.wait_ge(S["init"], i + 1)
                t = slice(i * TPB, (i + 1) * TPB)
                nc.vector.tensor_tensor(on.g[:, t, :], init_ps[i % 2][:, :, :], on.xn[:, t, :], ALU.add)\
                    .then_inc(S["g"], 1)


def centroid_experts(nc, on, name, dram, experts, chunks):
    with nc.sbuf_tensor(f"{name}_combine", [P, TILES, experts], F32) as combine, \
            nc.sbuf_tensor(f"{name}_w1", [P, experts, chunks * P], F32) as w1, \
            nc.sbuf_tensor(f"{name}_b1", [P, experts, chunks], F32) as b1:
        centroid_route_stage(nc, on, f"{name}r", dram, experts, combine, w1, b1, chunks)
        layernorm_stage(nc, on, f"{name}n", on.xn, on.v, on.xnT, False)
        weights = {"gate": lambda e: w1[:, bass.ds(e, 1), :].rearrange("p e (c f) -> p (e c) f", f=P),
                   "down": lambda e: dram["w2"][bass.ds(e, 1), :, :].rearrange("e p (c d) -> (e p) c d", d=D),
                   "bias": lambda e: b1[:, bass.ds(e, 1), :]}
        ffn_stage(nc, on, f"{name}e", on.xnT, on.g, experts, chunks, 1, weights, False, combine=combine)


def top_route_stage(nc, on, name, dram, experts, top_k, combine):
    ctx, sb, pb, sem = scope(nc)
    with ctx:
        routerT, bias = sb(f"{name}_routerT", [P, experts]), sb(f"{name}_bias", [P, experts])
        prob, fixed, mask, equal, order, keep = (sb(f"{name}_{w}", [P, TILES, experts]) for w in (
            "prob", "fixed", "mask", "equal", "order", "keep"))
        most = sb(f"{name}_most", [P, TILES, 8])
        col = [sb(f"{name}_col{k}", [P, TILES]) for k in range(2)]
        logit_ps = [pb(f"{name}_logitp{k}", [P, TILES // 2, experts]) for k in range(2)]
        S = {w: sem(f"{name}_{w}") for w in ("w", "logit", "chain", "exp")}
        loads = [(routerT[:, :], dram["routerT"]), (bias[:, :], dram["bias"])]
        block = ctx.enter_context(nc.Block())

        @block.sync
        def _(sp):
            for dst, src in loads:
                sp.dma_start(dst, src).then_inc(S["w"], 16)

        @block.tensor
        def _(pe):
            pe.wait_ge(S["w"], 16 * len(loads))
            for t in range(TILES):
                ins = nc.tensor.matmul(logit_ps[t // (TILES // 2)][:, t % (TILES // 2), :],
                                       on.xnT[:, t * P:(t + 1) * P], routerT[:, :], start=True, stop=True)
            ins.then_inc(S["logit"], 1)

        @block.scalar
        def _(act):
            act.wait_ge(S["chain"], 4)
            nc.scalar.activation(prob[:, :, :], prob[:, :, :], ACT.Exp).then_inc(S["exp"], 1)

        @block.vector
        def _(dve):
            done = [0]

            def link(ins):
                done[0] += 1
                ins.then_inc(S["chain"], 1)
                dve.wait_ge(S["chain"], done[0])

            def wide(a):
                return a.unsqueeze(2).broadcast_to([P, TILES, experts])

            def each(out, a, b, op):
                link(nc.vector.tensor_tensor(out[:, :, :], a[:, :, :], b, op))

            nc.vector.memset(order[:, :, :], 1.0)
            dve.wait_ge(S["w"], 16 * len(loads))
            dve.wait_ge(S["logit"], 1)
            half = TILES // 2
            link(nc.vector.tensor_copy(prob[:, 0:half, :], logit_ps[0][:, :, :]))
            link(nc.vector.tensor_copy(prob[:, half:, :], logit_ps[1][:, :, :]))
            link(nc.vector.tensor_reduce(col[0][:, :], prob[:, :, :], AX.X, ALU.max))
            each(prob, prob, wide(col[0][:, :]), ALU.subtract)
            dve.wait_ge(S["exp"], 1)
            link(nc.vector.tensor_reduce(col[0][:, :], prob[:, :, :], AX.X, ALU.add))
            link(nc.vector.reciprocal(col[1][:, :], col[0][:, :]))
            each(prob, prob, wide(col[1][:, :]), ALU.mult)
            each(fixed, prob, bias[:, :].unsqueeze(1).broadcast_to([P, TILES, experts]), ALU.add)
            for t in range(TILES):
                ins = nc.vector.max(most[:, t, :], fixed[:, t, :])
            link(ins)
            last = wide(most[:, :, top_k - 1])
            each(keep, fixed, last, ALU.is_gt)
            each(equal, fixed, last, ALU.is_equal)
            link(nc.vector.tensor_reduce(col[0][:, :], keep[:, :, :], AX.X, ALU.add))
            link(nc.vector.tensor_scalar(col[0][:, :], col[0][:, :], -1.0, float(top_k), ALU.mult, ALU.add))
            link(nc.vector.memset(order[:, :, 0:1], 0.0))
            link(nc.vector.tensor_tensor_scan(mask[:, :, :].rearrange("p t e -> p (t e)"),
                                              order[:, :, :].rearrange("p t e -> p (t e)"),
                                              equal[:, :, :].rearrange("p t e -> p (t e)"), 0.0, ALU.mult, ALU.add))
            each(mask, mask, wide(col[0][:, :]), ALU.is_le)
            each(equal, equal, mask[:, :, :], ALU.mult)
            each(keep, keep, equal[:, :, :], ALU.add)
            each(keep, keep, prob[:, :, :], ALU.mult)
            link(nc.vector.tensor_reduce(col[0][:, :], keep[:, :, :], AX.X, ALU.add))
            link(nc.vector.tensor_scalar(col[0][:, :], col[0][:, :], 1e-12, None, ALU.max))
            link(nc.vector.reciprocal(col[1][:, :], col[0][:, :]))
            each(combine, keep, wide(col[1][:, :]), ALU.mult)


def top_experts(nc, on, name, dram, experts, top_k):
    with nc.sbuf_tensor(f"{name}_combine", [P, TILES, experts], F32) as combine:
        top_route_stage(nc, on, f"{name}r", dram, experts, top_k, combine)
        ffn_stage(nc, on, f"{name}s", on.xnT, on.g, 1, 1, 1,
                  {w: (lambda e, w=w: dram[f"shared_{w}"].rearrange("p (c f) -> p c f", c=1))
                   for w in ("gate", "up", "down")}, True)
        ffn_stage(nc, on, f"{name}e", on.xnT, on.g, experts // 2, 1, 2,
                  {w: (lambda e, w=w: dram[f"pair_{w}"][bass.ds(e, 1), :, :].rearrange("e p f -> p e f"))
                   for w in ("gate", "up", "down")}, True, combine=combine)


def unpack_weights_stage(nc, on, name, dram, scale, w_sb):
    ctx, sb, pb, sem = scope(nc)
    with ctx:
        kinds = list(w_sb)
        whole = {w: sb(f"{name}_{w}", [P, w_sb[w].shape[1], P], I32) for w in kinds}
        loaded, scaled = sem(f"{name}_loaded"), sem(f"{name}_scaled")
        block = ctx.enter_context(nc.Block())

        @block.sync
        def _(sp):
            for w in kinds:
                sp.dma_start(whole[w][:, :, :], dram[w]).then_inc(loaded, 16)

        @block.vector
        def _(dve):
            for n, w in enumerate(kinds):
                dve.wait_ge(loaded, 16 * len(kinds))
                nc.vector.tensor_scalar(w_sb[w][:, :, :], whole[w][:, :, :], scale, None, ALU.mult).then_inc(scaled, 1)
            dve.wait_ge(scaled, len(kinds))


def integer_ffn(nc, on, name, dram, hidden):
    chunks = hidden // P
    ctx, sb, pb, sem = scope(nc)
    with ctx:
        w_sb = {w: sb(f"{name}_{w}", [P, chunks, P]) for w in ("gate", "up", "down")}
        unpack_weights_stage(nc, on, f"{name}u", dram, 1.0 / 127.0, w_sb)
        ffn_stage(nc, on, f"{name}e", on.xnT, on.g, 1, chunks, 1,
                  {w: (lambda e, w=w: w_sb[w][:, :, :]) for w in w_sb}, True)


def choice_route_stage(nc, on, name, dram, experts, capacity, combine, chosen):
    ctx, sb, pb, sem = scope(nc)
    with ctx:
        gateT = sb(f"{name}_gateT", [P, experts])
        score, mask, equal, rank, order = (sb(f"{name}_{w}", [P, experts, TILES]) for w in (
            "score", "mask", "equal", "rank", "order"))
        count, need = sb(f"{name}_count", [P, experts]), sb(f"{name}_need", [P, experts])
        bit, step, least, trial = (sb(f"{name}_{w}", [P, experts], I32) for w in ("bit", "step", "least", "trial"))
        logit_ps = pb(f"{name}_logitp", [P, TILES, experts])
        total_ps = pb(f"{name}_totalp", [P, experts])
        within_ps, tiles_ps = (pb(f"{name}_{w}", [P, experts, TILES]) for w in ("withinp", "tilesp"))
        S = {w: sem(f"{name}_{w}") for w in ("w", "logit", "exp", "chain", "search", "halved", "counted", "rest", "final")}
        BITS = 30
        block = ctx.enter_context(nc.Block())

        @block.sync
        def _(sp):
            sp.dma_start(gateT[:, :], dram["gateT"]).then_inc(S["w"], 16)

        @block.tensor
        def _(pe):
            pe.wait_ge(S["w"], 16)
            for t in range(TILES):
                ins = nc.tensor.matmul(logit_ps[:, t, :], on.xnT[:, t * P:(t + 1) * P], gateT[:, :], start=True,
                                       stop=True)
            ins.then_inc(S["logit"], 1)
            with nc.tensor.Fori(0, BITS) as i:
                pe.wait_ge(S["search"], i * 4 + 3)
                nc.tensor.matmul(total_ps[:, :], on.ones[:, :], count[:, :], start=True, stop=True)\
                    .then_inc(S["counted"], 1)
            pe.wait_ge(S["rest"], 3)
            nc.tensor.matmul(total_ps[:, :], on.ones[:, :], count[:, :], start=True, stop=True)
            nc.tensor.matmul(within_ps[:, :, :], on.causal[:, :], equal[:, :, :], start=True, stop=True)
            nc.tensor.matmul(tiles_ps[:, :, :], on.ones[:, :], equal[:, :, :], start=True, stop=True)\
                .then_inc(S["final"], 1)

        @block.scalar
        def _(act):
            act.wait_ge(S["logit"], 1)
            nc.scalar.activation(score[:, :, :], logit_ps[:, :, :].rearrange("p t e -> p e t"), ACT.Exp, scale=-1.0)\
                .then_inc(S["exp"], 1)

        @block.vector
        def _(dve):
            done = {w: 0 for w in ("chain", "rest")}

            def link(ins, w="chain"):
                done[w] += 1
                ins.then_inc(S[w], 1)
                dve.wait_ge(S[w], done[w])

            def wide(a):
                return a.unsqueeze(2).broadcast_to([P, experts, TILES])

            nc.vector.memset(order[:, :, :], 1.0)
            nc.vector.memset(bit[:, :], 1 << (BITS - 1))
            link(nc.vector.memset(least[:, :], 0))
            dve.wait_ge(S["exp"], 1)
            link(nc.vector.tensor_scalar(mask[:, :, :], score[:, :, :], 1.0, None, ALU.add))
            link(nc.vector.reciprocal(score[:, :, :], mask[:, :, :]))
            with nc.vector.Fori(0, BITS) as i:
                nc.vector.tensor_tensor(trial[:, :], least[:, :], bit[:, :], ALU.bitwise_or).then_inc(S["search"], 1)
                dve.wait_ge(S["search"], i * 4 + 1)
                nc.vector.tensor_tensor(mask[:, :, :], score[:, :, :], wide(trial[:, :].bitcast(F32)), ALU.is_ge)\
                    .then_inc(S["search"], 1)
                dve.wait_ge(S["search"], i * 4 + 2)
                nc.vector.tensor_reduce(count[:, :], mask[:, :, :], AX.X, ALU.add).then_inc(S["search"], 1)
                dve.wait_ge(S["counted"], i + 1)
                nc.vector.scalar_tensor_tensor(step[:, :], total_ps[:, :], float(capacity), bit[:, :], ALU.is_ge,
                                               ALU.mult).then_inc(S["search"], 1)
                dve.wait_ge(S["search"], i * 4 + 4)
                nc.vector.tensor_tensor(least[:, :], least[:, :], step[:, :], ALU.bitwise_or)
                nc.vector.tensor_scalar(bit[:, :], bit[:, :], 1, None, ALU.logical_shift_right)\
                    .then_inc(S["halved"], 1)
                dve.wait_ge(S["halved"], i + 1)
            last = wide(least[:, :].bitcast(F32))
            link(nc.vector.tensor_tensor(mask[:, :, :], score[:, :, :], last, ALU.is_gt), "rest")
            link(nc.vector.tensor_tensor(equal[:, :, :], score[:, :, :], last, ALU.is_equal), "rest")
            link(nc.vector.tensor_reduce(count[:, :], mask[:, :, :], AX.X, ALU.add), "rest")
            dve.wait_ge(S["final"], 1)
            link(nc.vector.tensor_scalar(need[:, :], total_ps[:, :], -1.0, float(capacity), ALU.mult, ALU.add))
            before_tiles(nc, dve, link, order, rank, tiles_ps, within_ps)
            link(nc.vector.tensor_tensor(rank[:, :, :], rank[:, :, :], wide(need[:, :]), ALU.is_le))
            link(nc.vector.tensor_tensor(equal[:, :, :], equal[:, :, :], rank[:, :, :], ALU.mult))
            link(nc.vector.tensor_tensor(chosen[:, :, :], mask[:, :, :], equal[:, :, :], ALU.add))
            link(nc.vector.tensor_tensor(combine[:, :, :], chosen[:, :, :], score[:, :, :], ALU.mult))


def before_tiles(nc, dve, link, order, rank, tiles_ps, within_ps):
    flat = "p e t -> p (e t)"
    link(nc.vector.memset(order[:, :, 0:1], 0.0))
    link(nc.vector.tensor_copy(rank[:, :, :], tiles_ps[:, :, :]))
    link(nc.vector.tensor_tensor_scan(rank[:, :, :].rearrange(flat), order[:, :, :].rearrange(flat),
                                      rank[:, :, :].rearrange(flat), 0.0, ALU.mult, ALU.add))
    link(nc.vector.tensor_tensor(rank[:, :, :], rank[:, :, :], tiles_ps[:, :, :], ALU.subtract))
    link(nc.vector.tensor_tensor(rank[:, :, :], rank[:, :, :], within_ps[:, :, :], ALU.add))


def mixed_bias_stage(nc, on, name, dram, experts, combine):
    ctx, sb, pb, sem = scope(nc)
    with ctx:
        down_b = sb(f"{name}_down_b", [experts, D])
        combT = [sb(f"{name}_combT{k}", [experts, COLS]) for k in range(2)]
        turn_ps = [pb(f"{name}_turnp{k}", [P, COLS]) for k in range(2)]
        sum_ps = [pb(f"{name}_sump{k}", [P, TPB, D]) for k in range(2)]
        loaded, s_turned, s_copied, s_sum, s_added = (sem(f"{name}_{w}") for w in (
            "loaded", "turned", "copied", "sum", "added"))
        block = ctx.enter_context(nc.Block())

        @block.sync
        def _(sp):
            sp.dma_start(down_b[:, :], dram["down_b"]).then_inc(loaded, 16)

        @block.tensor
        def _(pe):
            pe.wait_ge(loaded, 16)
            for i in range(BLOCKS + 1):
                if i < BLOCKS:
                    if i >= 2:
                        pe.wait_ge(s_copied, i - 1)
                    for t in range(TPB):
                        ins = nc.tensor.transpose(turn_ps[i % 2][0:experts, t * P:(t + 1) * P],
                                                  combine[:, :, i * TPB + t], on.ident[:, :])
                    ins.then_inc(s_turned, 1)
                if i:
                    pe.wait_ge(s_copied, i)
                    if i >= 3:
                        pe.wait_ge(s_added, i - 2)
                    for t in range(TPB):
                        ins = nc.tensor.matmul(sum_ps[(i - 1) % 2][:, t, :], combT[(i - 1) % 2][:, t * P:(t + 1) * P],
                                               down_b[:, :], start=True, stop=True)
                    ins.then_inc(s_sum, 1)

        @block.scalar
        def _(act):
            for i in range(BLOCKS):
                act.wait_ge(s_turned, i + 1)
                if i >= 2:
                    act.wait_ge(s_sum, i - 1)
                nc.scalar.activation(combT[i % 2][:, :], turn_ps[i % 2][0:experts, :], ACT.Copy).then_inc(s_copied, 1)

        @block.vector
        def _(dve):
            for i in range(BLOCKS):
                dve.wait_ge(s_sum, i + 1)
                t = slice(i * TPB, (i + 1) * TPB)
                nc.vector.tensor_tensor(on.g[:, t, :], sum_ps[i % 2][:, :, :], on.g[:, t, :], ALU.add)\
                    .then_inc(s_added, 1)


def choice_experts(nc, on, name, dram, experts, capacity, chunks):
    ctx, sb, pb, sem = scope(nc)
    with ctx:
        combine, chosen = sb(f"{name}_combine", [P, experts, TILES]), sb(f"{name}_chosen", [P, experts, TILES])
        choice_route_stage(nc, on, f"{name}r", dram, experts, capacity, combine, chosen)
        shared = dram["shared_gate"].shape[1]
        ffn_stage(nc, on, f"{name}s", on.xnT, on.g, 1, shared, 1,
                  {w: (lambda e, w=w: dram[f"shared_{w}"]) for w in ("gate", "up", "down")}, True)
        mixed_bias_stage(nc, on, f"{name}b", dram, experts, combine)
        weights = {w: (lambda e, w=w: dram[w][bass.ds(e, 1), :, :].rearrange("e p (c f) -> (e p) c f", f=P))
                   for w in ("gate", "up", "down")}
        weights["bias"] = lambda e: dram["bias"][bass.ds(e, 1), :, :].rearrange("e p b -> p e b")
        ffn_stage(nc, on, f"{name}e", on.xnT, on.g, experts, chunks, 1, weights, True,
                  combine=combine[:, :, :].rearrange("p e t -> p t e"))


class Chip:
    pass


def persistent(nc, ctx):
    def sb(name, shape, dt=F32):
        return ctx.enter_context(nc.sbuf_tensor(name, shape, dt))

    on = Chip()
    on.x = sb("x_sb", [P, TILES, D])
    on.xn = sb("xn_sb", [P, TILES, D])
    on.xnT = sb("xnT_sb", [P, TOKENS])
    on.s = sb("s_sb", [P, TILES, D])
    on.g = sb("g_sb", [P, TILES, D])
    on.q = on.g
    on.k = on.s
    on.v = sb("v_sb", [P, TILES, D])
    on.ident = sb("ident", [P, P])
    on.ident_bf = sb("ident_bf", [P, P], BF16)
    on.ones = sb("ones", [P, P])
    on.causal = sb("causal", [P, P])
    on.mask_kq = sb("mask_kq", [P, 4, P], BF16)
    on.mask_qk = sb("mask_qk", [P, 4, P], BF16)
    return on


def final_stage(nc, on, out):
    ctx, sb, pb, sem = scope(nc)
    with ctx:
        gate = [sb(f"out_gate{k}", [P, COLS]) for k in range(2)]
        s_gate, s_prod, s_added, s_stored = (sem(f"out_{w}") for w in ("silu", "prod", "added", "stored"))
        block = ctx.enter_context(nc.Block())

        def block_of(t, i):
            return t[:, i * TPB:(i + 1) * TPB, :].rearrange("p t d -> p (t d)")

        @block.scalar
        def _(act):
            for i in range(BLOCKS):
                if i >= 2:
                    act.wait_ge(s_added, i - 1)
                nc.scalar.activation(gate[i % 2][:, :], block_of(on.g, i), ACT.Silu).then_inc(s_gate, 1)

        @block.vector
        def _(dve):
            for i in range(BLOCKS):
                dve.wait_ge(s_gate, i + 1)
                nc.vector.tensor_tensor(gate[i % 2][:, :], gate[i % 2][:, :], block_of(on.s, i), ALU.mult)\
                    .then_inc(s_prod, 1)
                dve.wait_ge(s_prod, i + 1)
                nc.vector.tensor_tensor(block_of(on.x, i), block_of(on.x, i), gate[i % 2][:, :], ALU.add)\
                    .then_inc(s_added, 1)

        @block.sync
        def _(sp):
            rows = out.rearrange("(t p) d -> p t d", p=P)
            for i in range(BLOCKS):
                sp.wait_ge(s_added, i + 1)
                t = slice(i * TPB, (i + 1) * TPB)
                sp.dma_start(rows[:, t, :], on.x[:, t, :]).then_inc(s_stored, 16)
            sp.wait_ge(s_stored, 16 * BLOCKS)


def gated_mixers_kernel(nc, dram, out):
    def of(layer):
        return {name[len(layer) + 1:]: dram[name] for name in dram if name.startswith(layer + "_")}

    with ExitStack() as ctx:
        on = persistent(nc, ctx)
        constants_stage(nc, on, dram)
        layernorm_stage(nc, on, "n0", on.x, on.xn, on.xnT, False)
        project_stage(nc, on, "p0", of("a0"), 16, "softplus")
        attention_stage(nc, on, "a0", of("a0"), 16, None)
        integer_ffn(nc, on, "f0", of("f0"), 384)
        layernorm_stage(nc, on, "n1", on.x, on.xn, on.xnT, True)
        project_stage(nc, on, "p1", of("a1"), 16, "rope")
        attention_stage(nc, on, "a1", of("a1"), 16, 8 ** -0.5)
        centroid_experts(nc, on, "f1", of("f1"), 8, 4)
        layernorm_stage(nc, on, "n2", on.x, on.xn, on.xnT, True)
        latent_attention(nc, on, "a2", of("a2"), 8, 2)
        top_experts(nc, on, "f2", of("f2"), 32, 6)
        layernorm_stage(nc, on, "n3", on.x, on.xn, on.xnT, True)
        channel_attention_stage(nc, on, "a3", of("a3"), 16, 64)
        choice_experts(nc, on, "f3", of("f3"), 16, 512, 4)
        final_stage(nc, on, out)


def rope_tables():
    pos = np.arange(SEQ, dtype=np.float32)[:, None]
    turn = np.arange(0, 8, 2, dtype=np.float32) / np.float32(8)
    theta = pos * np.exp(-turn * np.float32(np.log(10000.0)))
    tables = np.stack([np.repeat(np.cos(theta), 2, 1), np.repeat(np.sin(theta), 2, 1)]).astype(np.float32)
    return tables.reshape(2, QT, P, 8).transpose(2, 0, 1, 3)


def every_partition(a):
    return np.tile(a[None], (P,) + (1,) * a.ndim)


def row_chunks(w):
    return w.reshape(-1, P, w.shape[1]).transpose(1, 0, 2)


def layouts(i):
    d = {"x": i["L0_attn_x"].reshape(TOKENS, D)}
    for layer, mixer in (("a0", "L0_attn_"), ("a1", "L1_attn_")):
        d[f"{layer}_w"] = np.concatenate([i[mixer + w].T for w in ("Wq", "Wk", "Wv")], 1)
        d[f"{layer}_wo"] = i[mixer + "Wo"].T
        d[f"{layer}_bo"] = every_partition(i[mixer + "bo"])
    d["a0_bias"] = every_partition(np.stack([i["L0_attn_bq"], i["L0_attn_bk"], i["L0_attn_bv"]]))
    for w in ("gate", "up"):
        d[f"f0_{w}"] = i[f"L0_ffn_w_{w}"].T.reshape(P, 3, P)
    d["f0_down"] = row_chunks(i["L0_ffn_w_down"].T)

    d["a1_cos_sin"] = rope_tables()
    d["a1_gamma_beta"] = every_partition(np.stack([np.stack([i[f"L1_attn_{w}_{p}"] for w in "qk"])
                                                   for p in ("gamma", "beta")]))
    d["f1_centT"] = i["L1_ffn_centroids"].T
    d["f1_b2"] = i["L1_ffn_b2"]
    d["f1_ln_g"], d["f1_ln_b"] = i["L1_ffn_ln_g"].T, i["L1_ffn_ln_b"].T
    d["f1_rank_w"] = every_partition(8 - np.arange(8, dtype=np.float32))
    d["f1_w1"] = i["L1_ffn_w1"].transpose(1, 0, 2)
    d["f1_b1"] = i["L1_ffn_b1"].reshape(8, 4, P).transpose(2, 0, 1).reshape(P, 32)
    d["f1_w2"] = i["L1_ffn_w2"].reshape(8, 4, P, P).transpose(0, 2, 1, 3).reshape(8, P, 512)

    d["a2_wqT"] = i["L2_attn_wq"].reshape(P, 8, P).transpose(2, 1, 0)
    d["a2_wo"] = row_chunks(i["L2_attn_wo"])
    d["a2_up"] = np.stack([i["L2_attn_wk_up"].T, i["L2_attn_wv_up"].T], 1)
    d["a2_w_down"] = np.concatenate([i["L2_attn_wk_down"], i["L2_attn_wv_down"]], 1)
    den_cols = np.zeros((P, 2, 32), np.float32)
    den_cols[:, 0, 0] = 1
    den_cols[:, 1, 1] = 1
    d["a2_den_cols"] = den_cols
    gate_up = i["L2_ffn_gate_up_proj"]
    for w, half in (("gate", slice(0, 64)), ("up", slice(64, 128))):
        d[f"f2_pair_{w}"] = gate_up[:, half].reshape(16, P, P).transpose(0, 2, 1)
    d["f2_pair_down"] = i["L2_ffn_down_proj"].transpose(0, 2, 1).reshape(16, P, P)
    d["f2_routerT"] = i["L2_ffn_router_weight"].T
    d["f2_bias"] = every_partition(i["L2_ffn_e_score_bias"])
    for w in ("gate", "up", "down"):
        d[f"f2_shared_{w}"] = i[f"L2_ffn_shared_{w}_w"].T

    wq, wk, wv = (i["L3_attn_w_qkv"][:, j * 1024:(j + 1) * 1024] for j in range(3))
    d["a3_w_q"], d["a3_w_k"] = wq.reshape(P, 8, P), wk.reshape(P, 8, P)
    d["a3_w_vT"] = row_chunks(wv.T)
    d["a3_w_out"] = row_chunks(i["L3_attn_w_out"])
    d["a3_temp"] = np.repeat(i["L3_attn_temperature"].reshape(8, 2).T, 64, axis=0)
    d["a3_gamma"] = every_partition(i["L3_attn_gamma"])
    d["f3_gateT"] = i["L3_ffn_gate_w"].T
    for w in ("gate", "up"):
        d[f"f3_shared_{w}"] = i[f"L3_ffn_sh_{w}_w"].T.reshape(P, 2, P)
    d["f3_shared_down"] = row_chunks(i["L3_ffn_sh_down_w"].T)
    d["f3_gate"], d["f3_up"] = i["L3_ffn_gw"].transpose(0, 2, 1), i["L3_ffn_up_w"].transpose(0, 2, 1)
    d["f3_down"] = i["L3_ffn_down_w"].transpose(0, 2, 1).reshape(16, 4, P, P).transpose(0, 2, 1, 3).reshape(16, P, 512)
    d["f3_bias"] = np.concatenate([i["L3_ffn_gb"].reshape(16, 4, P), i["L3_ffn_up_b"].reshape(16, 4, P)], 1)\
        .transpose(0, 2, 1)
    d["f3_down_b"] = i["L3_ffn_down_b"]
    return d


def kernel(**inputs):
    import concourse.bacc as _bacc
    from concourse.bass_utils import run_bass_kernel_spmd as _run

    arrays = {f"in_{n}": np.ascontiguousarray(a) for n, a in
              layouts({n: np.asarray(a) for n, a in inputs.items()}).items()}
    nc = _bacc.Bacc("TRN2", target_bir_lowering=False, num_devices=1)
    dram = {n[3:]: nc.dram_tensor(n, a.shape, mybir.dt.from_np(a.dtype), kind="ExternalInput").ap()
            for n, a in arrays.items()}
    out = nc.dram_tensor("out", (TOKENS, D), F32, kind="ExternalOutput").ap()
    gated_mixers_kernel(nc, dram, out)
    r = _run(nc, [arrays], core_ids=[0])
    return r.results[0]["out"].reshape(BATCH, SEQ, D)
```

```python
from contextlib import ExitStack

import concourse.bass as bass
import numpy as np
from concourse import mybir

F32 = mybir.dt.float32
BF16 = mybir.dt.bfloat16
I32 = mybir.dt.int32
U32 = mybir.dt.uint32
ALU = mybir.AluOpType
ACT = mybir.ActivationFunctionType
AX = mybir.AxisListType

P = 128
BATCH, SEQ, D = 16, 256, 128
TOKENS = BATCH * SEQ
TILES = TOKENS // P
QT = SEQ // P
COLS = 512
BLOCKS = TOKENS // COLS
TPB = COLS // P
LN_EPS = 1e-5
BIG_NEG = -1e30


def software_pipeline(fori, steps, n):
    lags = [lag for _, lag in steps]
    first, last = max(lags) + (max(lags) > 0), n + min(lags)
    last -= (last - first) % 2

    def turn(t, parity):
        for fn, lag in steps:
            if not isinstance(t, int) or 0 <= t - lag < n:
                fn(t - lag, (parity - lag) % 2)

    if last - first < 4:
        first = last = 0
    for t in range(first):
        turn(t, t % 2)
    if last > first:
        with fori(0, (last - first) // 2) as r:
            for k in range(2):
                turn(r * 2 + (first + k), (first + k) % 2)
    for t in range(last, n + max(lags)):
        turn(t, t % 2)


def scope(nc):
    ctx = ExitStack()
    sems = []

    def clear():
        nc.clear_and_free_semaphores(sems)
        nc.all_engine_barrier()

    ctx.callback(clear)

    def sb(name, shape, dt=F32):
        return ctx.enter_context(nc.sbuf_tensor(name, shape, dt))

    def pb(name, shape, dt=F32):
        return ctx.enter_context(nc.psum_tensor(name, shape, dt))

    def sem(name):
        sems.append(nc.alloc_semaphore(name))
        return sems[-1]

    return ctx, sb, pb, sem


def constants_stage(nc, on, dram):
    ctx, sb, pb, sem = scope(nc)
    with ctx:
        filled, shaped, loaded = sem("c_filled"), sem("c_shaped"), sem("c_loaded")
        block = ctx.enter_context(nc.Block())

        @block.sync
        def _(sp):
            sp.dma_start(on.x[:, :, :], dram["x"].rearrange("(t p) d -> p t d", p=P)).then_inc(loaded, 16)
            sp.wait_ge(loaded, 16)

        @block.gpsimd
        def _(pool):
            nc.gpsimd.memset(on.ident[:, :], 0.0)
            nc.gpsimd.memset(on.ident_bf[:, :], 0.0)
            nc.gpsimd.memset(on.ones[:, :], 1.0)
            nc.gpsimd.memset(on.causal[:, :], 1.0)
            nc.gpsimd.memset(on.mask_kq[:, :], 0.0)
            nc.gpsimd.memset(on.mask_qk[:, :], 0.0).then_inc(filled, 1)
            pool.wait_ge(filled, 1)
            for m in (on.ident, on.ident_bf):
                nc.gpsimd.affine_select(out=m[:, :], in_=m[:, :], compare_op=ALU.not_equal, fill=1.0, base=0,
                                        pattern=[[-1, P]], channel_multiplier=1)
            nc.gpsimd.affine_select(out=on.causal[:, :], in_=on.causal[:, :], compare_op=ALU.is_ge, fill=0.0, base=0,
                                    pattern=[[1, P]], channel_multiplier=-1)
            nc.gpsimd.affine_select(out=on.mask_kq[:, :], in_=on.mask_kq[:, :], compare_op=ALU.is_ge,
                                    fill=BIG_NEG, base=0, pattern=[[1, P]], channel_multiplier=-1)
            nc.gpsimd.affine_select(out=on.mask_qk[:, :], in_=on.mask_qk[:, :], compare_op=ALU.is_ge,
                                    fill=BIG_NEG, base=0, pattern=[[-1, P]], channel_multiplier=1)\
                .then_inc(shaped, 1)
            pool.wait_ge(shaped, 1)


def layernorm_stage(nc, on, name, src, dst, dst_t, gated):
    ctx, sb, pb, sem = scope(nc)
    with ctx:
        gate = [sb(f"{name}_gate{k}", [P, COLS]) for k in range(2)]
        stats = sb(f"{name}_stats", [P, TILES, 6])
        mean_var = sb(f"{name}_mv", [P, TILES, 2])
        rstd = sb(f"{name}_rstd", [P, TILES])
        std = sb(f"{name}_std", [P, TILES])
        turned = [pb(f"{name}_turned{k}", [P, COLS]) for k in range(2)]
        s_gate, s_gate_free, s_prod, s_added = (sem(f"{name}_{w}") for w in ("silu", "silufree", "prod", "added"))
        s_stats, s_aggr, s_eps, s_std, s_rstd = (sem(f"{name}_{w}") for w in ("stats", "aggr", "eps", "std", "rstd"))
        s_norm, s_turned, s_turned_free = (sem(f"{name}_{w}") for w in ("norm", "turned", "turnedfree"))
        block = ctx.enter_context(nc.Block())

        def block_of(t, i):
            return t[:, bass.ds(i * TPB, TPB), :].rearrange("p t d -> p (t d)")

        @block.scalar
        def _(act):
            act.sem_inc(s_turned_free, 2)
            if gated:
                def silu(i, k):
                    act.wait_ge(s_gate_free, i + 1)
                    nc.scalar.activation(gate[k][:, :], block_of(on.g, i), ACT.Silu).then_inc(s_gate, 1)

                software_pipeline(nc.scalar.Fori, [(silu, 0)], BLOCKS)
            act.wait_ge(s_eps, 1)
            nc.scalar.activation(std[:, :], rstd[:, :], ACT.Sqrt).then_inc(s_std, 1)

            def copy_out(i, k):
                act.wait_ge(s_turned, i + 1)
                nc.scalar.activation(dst_t[:, bass.ts(i, COLS)], turned[k][:, :], ACT.Copy).then_inc(s_turned_free, 1)

            software_pipeline(nc.scalar.Fori, [(copy_out, 0)], BLOCKS)

        @block.gpsimd
        def _(pool):
            if gated:
                def add(i, k):
                    pool.wait_ge(s_prod, i + 1)
                    nc.gpsimd.tensor_tensor(block_of(on.x, i), block_of(on.x, i), gate[k][:, :], ALU.add)\
                        .then_inc(s_added, 1)

                pool.sem_inc(s_gate_free, 2)
                software_pipeline(nc.gpsimd.Fori, [(add, 0)], BLOCKS)

        @block.vector
        def _(dve):
            if gated:
                def product(i, k):
                    dve.wait_ge(s_gate, i + 1)
                    nc.vector.tensor_tensor(gate[k][:, :], gate[k][:, :], block_of(on.s, i), ALU.mult)\
                        .then_inc(s_prod, 1)

                def block_stats(i, k):
                    dve.wait_ge(s_added, i + 1)
                    dve.sem_inc(s_gate_free, 1)
                    for t in range(TPB):
                        nc.vector.bn_stats(stats[:, bass.ds(i * TPB + t, 1), :], src[:, bass.ds(i * TPB + t, 1), :])\
                            .then_inc(s_stats, 1)

                software_pipeline(nc.vector.Fori, [(product, 0), (block_stats, 1)], BLOCKS)
            else:
                with nc.vector.Fori(0, TILES) as t:
                    nc.vector.bn_stats(stats[:, bass.ds(t, 1), :], src[:, bass.ds(t, 1), :]).then_inc(s_stats, 1)
            dve.wait_ge(s_stats, TILES)
            for t in range(TILES):
                nc.vector.bn_aggr(mean_var[:, t, :], stats[:, t, :]).then_inc(s_aggr, 1)
            dve.wait_ge(s_aggr, TILES)
            nc.vector.tensor_scalar(rstd[:, :], mean_var[:, :, 1], LN_EPS, None, ALU.add).then_inc(s_eps, 1)
            dve.wait_ge(s_std, 1)
            nc.vector.reciprocal(rstd[:, :], std[:, :]).then_inc(s_rstd, 1)
            dve.wait_ge(s_rstd, 1)
            with nc.vector.Fori(0, TILES) as t:
                nc.vector.tensor_scalar(dst[:, bass.ds(t, 1), :], src[:, bass.ds(t, 1), :],
                                        mean_var[:, bass.ds(t, 1), 0], rstd[:, bass.ds(t, 1)],
                                        ALU.subtract, ALU.mult).then_inc(s_norm, 1)

        @block.tensor
        def _(pe):
            for i in range(BLOCKS):
                pe.wait_ge(s_norm, (i + 1) * TPB)
                pe.wait_ge(s_turned_free, i + 1)
                for t in range(TPB):
                    ins = nc.tensor.transpose(turned[i % 2][:, t * P:(t + 1) * P], dst[:, i * TPB + t, :],
                                              on.ident[:, :])
                ins.then_inc(s_turned, 1)


def ffn_stage(nc, on, name, src_t, acc, experts, chunks, down_outs, weights, gated, combine=None):
    ctx, sb, pb, sem = scope(nc)
    with ctx:
        kinds = [w for w in ("gate", "up", "down", "bias") if w in weights]
        biased = "bias" in weights
        w_sb = {w: [sb(f"{name}_w_{w}{k}", [P, 1, (1 + gated) * chunks] if w == "bias" else [P, chunks, P])
                    for k in range(min(2, experts))] for w in kinds}
        h = [[sb(f"{name}_h{k}_{c}", [P, COLS]) for c in range(chunks)] for k in range(2)]
        silu = [sb(f"{name}_silu{k}", [P, COLS]) for k in range(2)] if gated else None
        gate_ps = [pb(f"{name}_gate{k}", [P, COLS]) for k in range(2)]
        up_ps = [pb(f"{name}_up{k}", [P, COLS]) for k in range(2)] if gated else None
        down_ps = [[pb(f"{name}_down{k}_{o}", [P, TPB, P]) for o in range(down_outs)] for k in range(2)]
        w_loaded = [sem(f"{name}_w_loaded{k}") for k in range(2)]
        s_proj, s_gate_free, s_silu, s_up_free, s_acc, s_down, s_down_free = (
            sem(f"{name}_{w}") for w in ("proj", "gatefree", "silu", "upfree", "acc", "down", "downfree"))
        block = ctx.enter_context(nc.Block())

        def each_expert(fori, body):
            if experts == 1:
                body(0, 0)
            else:
                with fori(0, experts // 2) as r:
                    for k in range(2):
                        body(r * 2 + k, k)

        @block.sync
        def _(sp):
            def load(e, k):
                for w in kinds:
                    sp.dma_start(w_sb[w][k][:, :, :], weights[w](e)).then_inc(w_loaded[k], 16)

            for e in range(min(2, experts)):
                load(e, e)
            if experts > 2:
                with nc.sync.Fori(0, experts // 2 - 1) as r:
                    for k in range(2):
                        sp.wait_ge(s_down, r * (2 * BLOCKS) + ((k + 1) * BLOCKS + 2))
                        load(r * 2 + (2 + k), k)

        @block.tensor
        def _(pe):
            pe.sem_inc(s_down, 2)

            def project(e, k, i, par):
                u = e * BLOCKS + i
                cols = src_t[:, bass.ts(i, COLS)]
                for c in range(chunks):
                    n, b = u * chunks + c, (par * chunks + c) % 2
                    pe.wait_ge(s_gate_free, n + 1)
                    ins = nc.tensor.matmul(gate_ps[b][:, :], w_sb["gate"][k][:, c, :], cols, start=True, stop=True)
                    if gated:
                        pe.wait_ge(s_up_free, n + 1)
                        ins = nc.tensor.matmul(up_ps[b][:, :], w_sb["up"][k][:, c, :], cols, start=True, stop=True)
                    ins.then_inc(s_proj, 1)

            def down(e, k, i, par):
                u = e * BLOCKS + i
                pe.wait_ge(s_up_free if gated else s_gate_free, (u + 1) * chunks + 2)
                pe.wait_ge(s_down_free, u + 1)
                rows = P // down_outs
                for t in range(TPB):
                    for o in range(down_outs):
                        r = slice(o * rows, (o + 1) * rows)
                        for c in range(chunks):
                            ins = nc.tensor.matmul(down_ps[par][o][:, t, :], h[par][c][r, t * P:(t + 1) * P],
                                                   w_sb["down"][k][r, c, :], start=(c == 0), stop=(c == chunks - 1))
                ins.then_inc(s_down, 1)

            def expert(e, k):
                pe.wait_ge(w_loaded[k], (e // 2 + 1) * 16 * len(kinds) if isinstance(e, int)
                           else (e - k) * (8 * len(kinds)) + 16 * len(kinds))
                software_pipeline(nc.tensor.Fori, [(lambda i, par: project(e, k, i, par), 0),
                                                   (lambda i, par: down(e, k, i, par), 1)], BLOCKS)

            each_expert(nc.tensor.Fori, expert)

        @block.scalar
        def _(act):
            act.sem_inc(s_gate_free, 2)

            def unit(e, k, i, par):
                u = e * BLOCKS + i
                if not gated:
                    act.wait_ge(s_down, u + 1)
                for c in range(chunks):
                    n, b = u * chunks + c, (par * chunks + c) % 2
                    act.wait_ge(s_proj, n + 1)
                    if gated:
                        act.wait_ge(s_up_free, n + 1)
                        if biased:
                            nc.scalar.activation(silu[b][:, :], gate_ps[b][:, :], ACT.Silu,
                                                 bias=w_sb["bias"][k][:, 0, c:c + 1]).then_inc(s_gate_free, 1)
                        else:
                            nc.scalar.activation(silu[b][:, :], gate_ps[b][:, :], ACT.Silu).then_inc(s_gate_free, 1)
                    else:
                        nc.scalar.activation(h[par][c][:, :], gate_ps[b][:, :], ACT.Relu,
                                             bias=w_sb["bias"][k][:, 0, c:c + 1]).then_inc(s_gate_free, 1)

            each_expert(nc.scalar.Fori, lambda e, k: software_pipeline(
                nc.scalar.Fori, [(lambda i, par: unit(e, k, i, par), 0)], BLOCKS))

        @block.vector
        def _(dve):
            dve.sem_inc(s_up_free, 2)
            dve.sem_inc(s_down_free, 2)

            def hidden(e, k, i, par):
                u = e * BLOCKS + i
                dve.wait_ge(s_down, u + 1)
                for c in range(chunks):
                    n, b = u * chunks + c, (par * chunks + c) % 2
                    dve.wait_ge(s_gate_free, n + 3)
                    if biased:
                        nc.vector.scalar_tensor_tensor(h[par][c][:, :], up_ps[b][:, :],
                                                       w_sb["bias"][k][:, 0, chunks + c:chunks + c + 1],
                                                       silu[b][:, :], ALU.add, ALU.mult).then_inc(s_up_free, 1)
                    else:
                        nc.vector.tensor_tensor(h[par][c][:, :], up_ps[b][:, :], silu[b][:, :], ALU.mult)\
                            .then_inc(s_up_free, 1)

            def take(e, k, i, par):
                u = e * BLOCKS + i
                dve.wait_ge(s_down, u + 3)
                if combine is None:
                    nc.vector.tensor_copy(acc[:, bass.ts(i, TPB), :], down_ps[par][0][:, :, :]).then_inc(s_down_free, 1)
                    return
                for o in range(down_outs):
                    if o:
                        dve.wait_ge(s_acc, u * (down_outs - 1) + 1)
                    for t in range(TPB):
                        tile = i * TPB + t
                        ins = nc.vector.scalar_tensor_tensor(
                            acc[:, bass.ds(tile, 1), :], down_ps[par][o][:, t:t + 1, :],
                            combine[:, bass.ds(tile, 1), bass.ds(e * down_outs + o, 1)],
                            acc[:, bass.ds(tile, 1), :], ALU.mult, ALU.add)
                    ins.then_inc(s_down_free if o == down_outs - 1 else s_acc, 1)

            steps = [(hidden, 0)] * gated + [(take, 1)]
            each_expert(nc.vector.Fori, lambda e, k: software_pipeline(
                nc.vector.Fori, [((lambda i, par, fn=fn: fn(e, k, i, par)), lag) for fn, lag in steps], BLOCKS))


def upto(value, limit):
    return min(value, limit) if isinstance(value, int) else value


def project_stage(nc, on, name, dram, heads, finish):
    hd = D // heads
    GROUPS = TILES // 2
    ctx, sb, pb, sem = scope(nc)
    with ctx:
        w = dram["w_sb"] if finish == "latent" else sb(f"{name}_w", [P, 3 * D])
        xb = [sb(f"{name}_xb{k}", [P, 2 * P]) for k in range(2)]
        prod = [[pb(f"{name}_prod{k}{t}", [P, 3, D]) for t in range(2)] for k in range(2)]
        loaded, s_xb, s_prod, s_taken, s_chain, s_act = (
            sem(f"{name}_{n}") for n in ("loaded", "xb", "prod", "taken", "chain", "act"))
        loads = [] if finish == "latent" else [(w[:, :], dram["w"])]
        if finish == "latent":
            pass
        elif finish == "softplus":
            bias = sb(f"{name}_bias", [P, 3, D])
            loads.append((bias[:, :, :], dram["bias"]))
            terms = [sb(f"{name}_terms{j}", [P, TILES, D]) for j in range(2)]
        else:
            cos_sin = sb(f"{name}_cos_sin", [P, 2, QT, hd])
            gamma_beta = sb(f"{name}_gamma_beta", [P, 2, 2, hd])
            loads += [(cos_sin[:, :, :, :], dram["cos_sin"]), (gamma_beta[:, :, :, :], dram["gamma_beta"])]
            mean = sb(f"{name}_mean", [P, TILES, heads])
            var = sb(f"{name}_var", [P, TILES, heads])
            square = sb(f"{name}_square", [P, TILES, D])
            turned = sb(f"{name}_turned", [P, TILES, D])
        block = ctx.enter_context(nc.Block())

        @block.sync
        def _(sp):
            for dst, src in loads:
                sp.dma_start(dst, src).then_inc(loaded, 16)

        @block.gpsimd
        def _(pool):
            def copy_x(i, k):
                pool.wait_ge(s_prod, i + 1)
                nc.gpsimd.tensor_copy(xb[k][:, :], on.xnT[:, bass.ts(i, 2 * P)]).then_inc(s_xb, 1)

            software_pipeline(nc.gpsimd.Fori, [(copy_x, 0)], GROUPS)

        @block.tensor
        def _(pe):
            pe.sem_inc(s_prod, 2)
            pe.wait_ge(loaded, 16 * len(loads))

            def product(i, k):
                pe.wait_ge(s_xb, i + 1)
                pe.wait_ge(s_taken, i + 1)
                for t in range(2):
                    ins = nc.tensor.matmul(prod[k][t][:, :, :].rearrange("p j d -> p (j d)"),
                                           xb[k][:, t * P:(t + 1) * P], w[:, :], start=True, stop=True)
                ins.then_inc(s_prod, 1)

            software_pipeline(nc.tensor.Fori, [(product, 0)], GROUPS)

        @block.vector
        def _(dve):
            dve.sem_inc(s_taken, 2)
            dve.wait_ge(loaded, 16 * len(loads))

            def take(i, k):
                dve.wait_ge(s_prod, i + 3)
                for t in range(2):
                    if finish == "latent":
                        tile = bass.ds(i * 2 + t, 1)
                        nc.vector.tensor_copy(on.q2[:, tile, :], prod[k][t][:, 0:2, :].rearrange("p j d -> p (j d)"))
                        ins = nc.vector.tensor_copy(on.kv[:, tile, :], prod[k][t][:, 2:3, :])
                        continue
                    for j, dst in enumerate((on.q, on.k, on.v)):
                        out = dst[:, bass.ds(i * 2 + t, 1), :]
                        if finish == "softplus":
                            ins = nc.vector.tensor_tensor(out, prod[k][t][:, j:j + 1, :], bias[:, j:j + 1, :], ALU.add)
                        else:
                            ins = nc.vector.tensor_copy(out, prod[k][t][:, j:j + 1, :])
                ins.then_inc(s_taken, 1)

            software_pipeline(nc.vector.Fori, [(take, 0)], GROUPS)
            done = [0]

            def link(ins):
                done[0] += 1
                ins.then_inc(s_chain, 1)
                dve.wait_ge(s_chain, done[0])

            dve.wait_ge(s_taken, GROUPS + 2)
            if finish == "latent":
                return
            if finish == "softplus":
                for j, z in enumerate((on.q, on.k)):
                    dve.wait_ge(s_act, 5 + j)
                    nc.vector.scalar_tensor_tensor(z[:, :, :], z[:, :, :], 0.0, terms[j][:, :, :], ALU.max, ALU.add)\
                        .then_inc(s_chain, 1)
                dve.wait_ge(s_chain, 2)
                return
            for j, z in enumerate((on.q, on.k)):
                by_head = z[:, :, :].rearrange("p t (h d) -> p t h d", d=hd)
                flat = z[:, :, :].rearrange("p t (h d) -> p (t h) d", d=hd)
                sq = square[:, :, :].rearrange("p t (h d) -> p (t h) d", d=hd)

                def wide(a):
                    return a.unsqueeze(2).broadcast_to([P, TILES * heads, hd])

                m, v = (a[:, :, :].rearrange("p t h -> p (t h)") for a in (mean, var))
                link(nc.vector.tensor_reduce(m, flat, AX.X, ALU.add))
                link(nc.vector.tensor_scalar(m, m, 1.0 / hd, None, ALU.mult))
                link(nc.vector.tensor_tensor(flat, flat, wide(m), ALU.subtract))
                link(nc.vector.tensor_tensor(sq, flat, flat, ALU.mult))
                link(nc.vector.tensor_reduce(v, sq, AX.X, ALU.add))
                link(nc.vector.tensor_scalar(v, v, 1.0 / hd, LN_EPS, ALU.mult, ALU.add))
                dve.wait_ge(s_act, j + 1)
                link(nc.vector.reciprocal(v, v))
                link(nc.vector.tensor_tensor(flat, flat, wide(v), ALU.mult))
                for op, row in ((ALU.mult, 0), (ALU.add, 1)):
                    gb = gamma_beta[:, row, j, :].unsqueeze(1).broadcast_to([P, TILES * heads, hd])
                    link(nc.vector.tensor_tensor(flat, flat, gb, op))
                half = hd // 2
                rot = turned[:, :, :].rearrange("p t (h d) -> p (t h) d", d=hd)
                nc.vector.tensor_scalar(rot[:, :, 0:half], flat[:, :, 1:hd:2], -1.0, None, ALU.mult)
                link(nc.vector.tensor_copy(rot[:, :, half:hd], flat[:, :, 0:hd:2]))
                for t in range(QT):
                    for src, row in ((z, 0), (turned, 1)):
                        part = src[:, t:TILES:QT, :].rearrange("p t (h d) -> p t h d", d=hd)
                        table = cos_sin[:, row, t, :].unsqueeze(1).unsqueeze(1).broadcast_to([P, TILES // QT, heads, hd])
                        ins = nc.vector.tensor_tensor(part, part, table, ALU.mult)
                link(ins)
                link(nc.vector.tensor_tensor(z[:, :, :], z[:, :, :], turned[:, :, :], ALU.add))

        @block.scalar
        def _(act):
            if finish == "softplus":
                act.wait_ge(s_taken, GROUPS + 2)
                for n, (func, scale, plus) in enumerate(((ACT.Abs, 1.0, 0.0), (ACT.Exp, -1.0, 0.0), (ACT.Ln, 1.0, 1.0))):
                    for j, z in enumerate((on.q, on.k)):
                        if n:
                            act.wait_ge(s_act, 2 * (n - 1) + j + 1)
                        nc.scalar.activation(terms[j][:, :, :], (terms[j] if n else z)[:, :, :], func, scale=scale,
                                             bias=plus).then_inc(s_act, 1)
            elif finish == "rope":
                for j in range(2):
                    act.wait_ge(s_chain, 13 * j + 6)
                    nc.scalar.activation(var[:, :, :], var[:, :, :], ACT.Sqrt).then_inc(s_act, 1)


def latent_fold_stage(nc, on, name, dram, w_sb, wo_sb, heads, kvh):
    lat = 32
    ctx, sb, pb, sem = scope(nc)
    with ctx:
        wqT, wo = sb(f"{name}_wqT", [P, heads, D]), sb(f"{name}_wo", [P, heads, D])
        up = sb(f"{name}_up", [P, 2, lat])
        q_ps, o_ps = pb(f"{name}_qps", [P, heads * lat]), pb(f"{name}_ops", [P, kvh, D])
        loaded, folded, copied = (sem(f"{name}_{w}") for w in ("loaded", "folded", "copied"))
        loads = [(wqT[:, :, :], dram["wqT"]), (wo[:, :, :], dram["wo"]), (up[:, :, :], dram["up"]),
                 (w_sb[:, heads * lat:], dram["w_down"])]
        block = ctx.enter_context(nc.Block())

        @block.sync
        def _(sp):
            for dst, src in loads:
                sp.dma_start(dst, src).then_inc(loaded, 16)
            sp.wait_ge(loaded, 16 * len(loads))

        @block.tensor
        def _(pe):
            pe.wait_ge(loaded, 16 * len(loads))
            for h in range(heads):
                ins = nc.tensor.matmul(q_ps[:, h * lat:(h + 1) * lat], wqT[:, h, :], up[:, 0, :], start=True, stop=True)
            ins.then_inc(folded, 1)
            hpg = heads // kvh
            for h in range(heads):
                r = lat * (h % hpg)
                ins = nc.tensor.matmul(o_ps[r:r + lat, h // hpg, :], up[:, 1, :], wo[:, h, :], start=True, stop=True)
            ins.then_inc(folded, 1)

        @block.scalar
        def _(act):
            act.wait_ge(folded, 1)
            nc.scalar.activation(w_sb[:, 0:heads * lat], q_ps[:, :], ACT.Copy).then_inc(copied, 1)
            act.wait_ge(folded, 2)
            nc.scalar.activation(wo_sb[:, :, :], o_ps[:, :, :], ACT.Copy).then_inc(copied, 1)
            act.wait_ge(copied, 2)


def latent_attention(nc, on, name, dram, heads, kvh):
    with nc.sbuf_tensor(f"{name}_q2", [P, TILES, heads * 32], F32) as q2, \
            nc.sbuf_tensor(f"{name}_w", [P, 3 * D], F32) as w_sb, \
            nc.sbuf_tensor(f"{name}_wo_sb", [P, kvh, D], F32) as wo_sb:
        on.q2, on.kv = q2, on.v
        latent_fold_stage(nc, on, f"{name}f", dram, w_sb, wo_sb, heads, kvh)
        project_stage(nc, on, f"{name}p", {"w_sb": w_sb}, heads, "latent")
        attention_stage(nc, on, f"{name}a", {**dram, "wo_sb": wo_sb}, heads, float(D) ** -0.5, kvh)


def attention_stage(nc, on, name, dram, heads, softmax_scale, kv_heads=None):
    latent = kv_heads is not None
    hd = 32 if latent else D // heads
    kvh = kv_heads or heads
    SLOT = 64
    CW = 3 * P
    HALF = heads // 2
    QB = 12 if latent else 8
    KB = 4 if latent else 8
    STRIPS = 3 if latent else 4
    OB = heads * hd // P
    softmax = softmax_scale is not None
    FILL = 1 if latent else 0
    TOP = FILL + 1
    LAG = FILL + (2 if softmax else 1)
    ROUNDS = heads // 2
    FILLS = ((0, 0), (0, 4), (0, 8), (1, 0)) if latent else ((0, 0), (1, 0), (0, 4), (1, 4))
    ctx, sb, pb, sem = scope(nc)
    with ctx:
        wo = dram["wo_sb"] if latent else sb(f"{name}_wo", [P, 1, D])
        bo = None if latent else sb(f"{name}_bo", [P, D])
        sel = sb(f"{name}_sel", [P, heads, P], BF16) if softmax else None
        widths = (heads * hd, kvh * hd)
        parts = [sb(f"{name}_parts{j}", [P, 3, QT, w], BF16) for j, w in enumerate(widths)]
        rest = [sb(f"{name}_rest{j}", [P, QT, w]) for j, w in enumerate(widths)]
        stacks = 2
        stack = [[sb(f"{name}_stack{k}{j}", [P, QT, n, P], BF16) for j, n in enumerate((QB, KB))]
                 for k in range(stacks)]
        stack = stack * 2 if latent else stack
        opT = [[sb(f"{name}_opT{k}{j}", [P, n, SEQ], BF16) for j, n in enumerate((QB, KB))] for k in range(2)]
        v1 = [sb(f"{name}_v1{k}", [P, QT, kvh, 32]) for k in range(2)]
        probs = [sb(f"{name}_probs{k}", [P, heads, CW]) for k in range(2)]
        den_cols = sb(f"{name}_dencols", [P, kvh, 32]) if latent else None
        pv_sb = sb(f"{name}_pvsb", [P, 4, SEQ])
        rden = sb(f"{name}_rden", [P, heads])
        o_sb = sb(f"{name}_o", [P, QT, heads, hd])
        oT = sb(f"{name}_oT", [P, QT, OB, P])
        score_ps = [pb(f"{name}_score{k}", [P, COLS]) for k in range(2)]
        top_ps = [pb(f"{name}_top{k}", [P, COLS]) for k in range(2)] if softmax else None
        pv_ps = [pb(f"{name}_pv{k}", [P, 2, SEQ]) for k in range(2)]
        opT_ps = pb(f"{name}_opTp", [P, 4, SEQ], BF16)
        desk = pb(f"{name}_desk", [P, 4, D])
        out_ps = desk[:, 0:QT, :]
        if softmax:
            tops = sb(f"{name}_tops", [P, QT, heads])
            ntop = sb(f"{name}_ntop", [P, QT, P], BF16)
            ntopT = [sb(f"{name}_ntopT{k}", [P, SEQ], BF16) for k in range(2)]
            ntopT_ps = desk[:, 0, :].bitcast(BF16)
        else:
            causal3 = sb(f"{name}_causal3", [P, CW])
        S = {w: sem(f"{name}_{w}") for w in (
            "w", "init", "sel", "part1", "rest1", "part2", "part3", "stack0", "stack1", "v1", "turned", "opT", "top", "topout",
            "neg", "ntop", "ntopTp", "ntopT", "score", "probs", "pv", "pvout", "tokmaj", "rden",
            "o", "oturned", "oT", "out", "s")}
        block = ctx.enter_context(nc.Block())
        loads = [] if latent else [(wo[:, 0, :], dram["wo"]), (bo[:, :], dram["bo"])]
        if latent:
            loads.append((den_cols[:, :, :], dram["den_cols"]))

        @block.sync
        def _(sp):
            for dst, src in loads:
                sp.dma_start(dst, src).then_inc(S["w"], 16)

        def q_of(t):
            return on.q2[:, t, :] if latent else on.q[:, t, :]

        def k_of(t):
            return on.kv[:, t, 0:kvh * hd] if latent else on.k[:, t, :]

        def slots(k, j, lo, n):
            a = stack[k][j][:, :, :, :].rearrange("p t b (h s) -> p (t b h) s", s=SLOT)
            return a[:, :, lo * hd:(lo + n) * hd].rearrange("p g (n d) -> p g n d", d=hd)

        def wide_slots(k, j, t, lo, n):
            hs = (heads, kvh)[j]
            if lo < 4:
                return stack[k][j][:, t, 0:hs, lo * hd:(lo + n) * hd].rearrange("p h (n d) -> p h n d", d=hd)
            a = stack[k][j][:, t, hs:, :].rearrange("p b (h s) -> p (b h) s", s=2 * hd)
            return a[:, :, (lo - 4) * hd:(lo - 4 + n) * hd].rearrange("p g (n d) -> p g n d", d=hd)

        def part(m, j, n):
            a = parts[j][:, m, :, :].rearrange("p t (h d) -> p (t h) d", d=hd).unsqueeze(2)
            return a.broadcast_to([P, QT * heads, n, hd])

        def wide_part(m, j, t, n, twice=False):
            hs = (heads, kvh)[j]
            a = parts[j][:, m, t, :].rearrange("p (h d) -> p h d", d=hd).unsqueeze(2)
            return a.broadcast_to([P, hs, 2 if twice else n, hd])

        def step(fn, *args):
            return lambda i, k: fn(*args, i, k)

        def two_heads(r):
            return range(2 * r, 2 * r + 2)

        def by_head(bank):
            return bank[:, :, :].rearrange("p s (j r) -> p (s j) r", r=32)

        @block.gpsimd
        def _(pool):
            for k in range(2):
                if k < stacks:
                    nc.gpsimd.memset(stack[k][0][:, :, :, :], 0.0)
                    nc.gpsimd.memset(stack[k][1][:, :, :, :], 0.0)
                if not latent:
                    nc.gpsimd.memset(v1[k][:, :, :, hd + 1:], 0.0)
                    ins = nc.gpsimd.memset(v1[k][:, :, :, hd:hd + 1], 1.0)
            if softmax:
                nc.gpsimd.memset(sel[:, :, :], 0.0)
                ins = nc.gpsimd.memset(ntop[:, :, :], 0.0)
            ins.then_inc(S["init"], 1)
            pool.wait_ge(S["init"], 1)
            if softmax:
                nc.gpsimd.affine_select(out=sel[:, :, :], in_=sel[:, :, :], compare_op=ALU.not_equal, fill=1.0,
                                        base=0, pattern=[[-1, heads], [0, P]], channel_multiplier=1)\
                    .then_inc(S["sel"], 1)
                pool.wait_ge(S["sel"], 1)
                nc.gpsimd.affine_select(out=sel[:, :, :], in_=sel[:, :, :], compare_op=ALU.not_equal, fill=1.0,
                                        base=-heads, pattern=[[-1, heads], [0, P]], channel_multiplier=1)\
                    .then_inc(S["sel"], 1)

            def values_in(i, k):
                pool.wait_ge(S["pv"], i * 2)
                t = bass.ds(i * QT, QT)
                v = on.kv[:, t, kvh * hd:] if latent else on.v[:, t, :]
                nc.gpsimd.tensor_copy(v1[k][:, :, :, 0:hd], v.rearrange("p t (h d) -> p t h d", d=hd))\
                    .then_inc(S["v1"], 1)

            def stack_q(i, k):
                pool.wait_ge(S["part3"], i + 1)
                pool.wait_ge(S["turned"], i * 4 + 3)
                if latent:
                    for t in range(QT):
                        q = on.q2[:, bass.ds(i * QT + t, 1), :].rearrange("p t (h d) -> p (t h) d", d=hd)
                        nc.gpsimd.tensor_copy(wide_slots(k, 0, t, 0, 3),
                                              q.unsqueeze(2).broadcast_to([P, heads, 3, hd]))
                        for m, lo, n in ((1, 3, 1), (1, 4, 1), (2, 5, 1)):
                            ins = nc.gpsimd.tensor_copy(wide_slots(k, 0, t, lo, n), wide_part(m, 0, t, n))
                    ins.then_inc(S["stack0"], 1)
                    return
                q = on.q[:, bass.ds(i * QT, QT), :].rearrange("p t (h d) -> p (t h) d", d=hd).unsqueeze(2)
                nc.gpsimd.tensor_copy(slots(k, 0, 0, 3), q.broadcast_to([P, QT * heads, 3, hd]))
                for m, lo, n in ((1, 3, 2), (2, 5, 1)):
                    ins = nc.gpsimd.tensor_copy(slots(k, 0, lo, n), part(m, 0, n))
                ins.then_inc(S["stack0"], 1)

            software_pipeline(nc.gpsimd.Fori, [(values_in, LAG), (stack_q, 0)], BATCH)

        @block.vector
        def _(dve):
            dve.sem_inc(S["topout" if softmax else "probs"], 2)
            dve.wait_ge(S["w"], 16 * len(loads))
            dve.wait_ge(S["init"], 1)
            if not softmax:
                nc.vector.memset(causal3[:, P:2 * P], 1.0)
                nc.vector.tensor_copy(causal3[:, 0:P], on.causal[:, :])
                nc.vector.tensor_copy(causal3[:, 2 * P:], on.causal[:, :]).then_inc(S["neg"], 1)
                dve.wait_ge(S["neg"], 1)

            def split(stage, i, k):
                t = bass.ds(i * QT, QT)
                src = (q_of(t), k_of(t))
                if stage == 0:
                    dve.wait_ge(S["stack0"], i)
                    dve.wait_ge(S["stack1"], i)
                    for j in range(2):
                        ins = nc.vector.tensor_copy(parts[j][:, 0, :, :], src[j])
                    ins.then_inc(S["part1"], 1)
                elif stage == 1:
                    dve.wait_ge(S["part1"], i + 1)
                    for j in range(2):
                        ins = nc.vector.tensor_tensor(rest[j][:, :, :], src[j], parts[j][:, 0, :, :], ALU.subtract)
                    ins.then_inc(S["rest1"], 1)
                elif stage == 2:
                    dve.wait_ge(S["rest1"], i + 1)
                    for j in range(2):
                        ins = nc.vector.tensor_copy(parts[j][:, 1, :, :], rest[j][:, :, :])
                    ins.then_inc(S["part2"], 1)
                elif stage == 3:
                    dve.wait_ge(S["part2"], i + 1)
                    for j in range(2):
                        ins = nc.vector.tensor_tensor(parts[j][:, 2, :, :], rest[j][:, :, :], parts[j][:, 1, :, :],
                                                      ALU.subtract)
                    ins.then_inc(S["part3"], 1)
                else:
                    dve.wait_ge(S["part3"], i + 1)
                    dve.wait_ge(S["turned"], i * 4 + 4)
                    stack_k(i, k)

            def stack_k(i, k):
                if latent:
                    for t in range(QT):
                        for m, lo in ((0, 0), (1, 1), (2, 2), (0, 3)):
                            nc.vector.tensor_copy(wide_slots(k, 1, t, lo, 1), wide_part(m, 1, t, 1))
                        for m, lo in ((1, 4), (0, 5)):
                            out = stack[k][1][:, t, kvh:, :].rearrange("p b (e s) -> p b e s", s=2 * hd)
                            ins = nc.vector.tensor_copy(out[:, :, :, (lo - 4) * hd:(lo - 3) * hd],
                                                        wide_part(m, 1, t, 1, twice=True))
                    ins.then_inc(S["stack1"], 1)
                    return
                for m, lo in ((0, 0), (1, 1), (2, 2), (0, 3), (1, 4), (0, 5)):
                    ins = nc.vector.tensor_copy(slots(k, 1, lo, 1), part(m, 1, 1))
                ins.then_inc(S["stack1"], 1)

            def top(r, i, k):
                for h in two_heads(r):
                    dve.wait_ge(S["top"], i * heads + h + 1)
                    nc.vector.reduce_max(tops[:, 0, h:h + 1], top_ps[h % 2][:, 0:P], AX.X)
                    nc.vector.reduce_max(tops[:, 1, h:h + 1], top_ps[h % 2][:, P:CW], AX.X).then_inc(S["topout"], 1)

            def negate_tops(i, k):
                dve.wait_ge(S["topout"], (i + 1) * heads + 2)
                dve.wait_ge(S["ntopTp"], i)
                nc.vector.tensor_scalar(ntop[:, :, 0:heads], tops[:, :, :], -1.0, None, ALU.mult).then_inc(S["neg"], 1)
                dve.wait_ge(S["neg"], i + 1)
                nc.vector.scalar_tensor_tensor(ntop[:, :, heads:2 * heads], tops[:, :, :], -1.0, ntop[:, :, 0:heads],
                                               ALU.mult, ALU.subtract).then_inc(S["ntop"], 1)
                dve.wait_ge(S["ntop"], i + 1)

            def masked(r, i, k):
                for h in two_heads(r):
                    dve.wait_ge(S["score"], i * heads + h + 1)
                    nc.vector.tensor_tensor(probs[k][:, h, :], score_ps[h % 2][:, 0:CW], causal3[:, :], ALU.mult)\
                        .then_inc(S["probs"], 1)

            def normalise(t):
                def fn(i, k):
                    n = i * QT + t
                    dve.wait_ge(S["tokmaj"], n + 1)
                    if latent:
                        den = desk[:, 2, :].rearrange("p (j r) -> p r j", r=32)[:, 0:kvh, :]
                        sums = desk[:, 0:2, :].rearrange("p g (j d) -> p (g j) d", d=hd)
                        nc.vector.reciprocal(rden[:, :].rearrange("p (g j) -> p g j", g=kvh), den)\
                            .then_inc(S["rden"], 1)
                    else:
                        sums = by_head(desk)[:, :, 0:hd]
                        nc.vector.reciprocal(rden[:, :], by_head(desk)[:, :, hd]).then_inc(S["rden"], 1)
                    dve.wait_ge(S["rden"], n + 1)
                    nc.vector.tensor_tensor(o_sb[:, t, :, :], sums,
                                            rden[:, :].unsqueeze(2).broadcast_to([P, heads, hd]), ALU.mult)\
                        .then_inc(S["o"], 1)
                    dve.wait_ge(S["o"], n + 1)
                return fn

            def store(i, k):
                dve.wait_ge(S["out"], i + 1)
                if latent:
                    nc.vector.tensor_copy(on.s[:, bass.ds(i * QT, QT), :], out_ps).then_inc(S["s"], 1)
                    return
                nc.vector.tensor_tensor(on.s[:, bass.ds(i * QT, QT), :], out_ps,
                                        bo[:, :].unsqueeze(1).broadcast_to([P, QT, D]), ALU.add).then_inc(S["s"], 1)

            steps = []
            for r in range(ROUNDS):
                if r < 4:
                    steps.append((step(split, r), 0))
                if r == 4 or ROUNDS == 4 and r == 3:
                    steps.append((step(split, 4), 0))
                steps.append((step(top, r), TOP) if softmax else (step(masked, r), LAG))
                if r == ROUNDS // 4:
                    steps.append((normalise(0), LAG + 2))
                elif r == ROUNDS // 2:
                    steps.append((normalise(1), LAG + 2))
            steps += [(negate_tops, TOP)] * softmax + [(store, LAG + 2)]
            software_pipeline(nc.vector.Fori, steps, BATCH)

        @block.tensor
        def _(pe):
            pe.sem_inc(S["turned"], 4 * stacks)
            pe.sem_inc(S["pv"], 2)
            pe.wait_ge(S["w"], 16 * len(loads))
            if softmax:
                pe.wait_ge(S["sel"], 2)

            def turn(n, i, k):
                j, block = FILLS[n]
                pe.wait_ge(S[f"stack{j}"], i + 1)
                pe.wait_ge(S["opT"], i * 4 + n)
                for p in range(4):
                    for t in range(QT):
                        ins = nc.tensor.transpose(opT_ps[:, p, t * P:(t + 1) * P],
                                                  stack[k][j][:, t, block + p, :], on.ident_bf[:, :])
                ins.then_inc(S["turned"], 1)

            def operands_ready(r, i):
                if r == 0:
                    pe.wait_ge(S["opT"], i * 4 + (4 if latent else 2))
                elif r == ROUNDS // 2:
                    pe.wait_ge(S["opT"], i * 4 + 4)

            def operands(k, h, q0, q1, k0, k1):
                q, key = (slice(q0 * P, q1 * P), slice(k0 * P, k1 * P))
                r = slice(SLOT * (h % 2), SLOT * (h % 2) + SLOT)
                if not latent:
                    return [(opT[k][0][r, h // 2, q], opT[k][1][r, h // 2, key])]
                g = h // (heads // kvh)
                return [(opT[k][0][:, h, q], opT[k][1][:, g, key]),
                        (opT[k][0][r, heads + h // 2, q], opT[k][1][r, kvh + g, key])]

            def tops_(r, i, k):
                operands_ready(r, i)
                for h in two_heads(r):
                    pe.wait_ge(S["topout"], i * heads + h + 1)
                    bank = top_ps[h % 2]
                    for qt, lo, hi, m0 in ((0, 0, P, 0), (1, P, CW, 2 * P)):
                        for n, (q, key) in enumerate(operands(k, h, qt, qt + 1, 0, qt + 1)):
                            nc.tensor.matmul(bank[:, lo:hi], q, key, start=(n == 0), stop=True,
                                             skip_group_check=(n > 0))
                        ins = nc.tensor.matmul(bank[:, m0:m0 + P], on.ident_bf[:, :], on.mask_qk[:, :],
                                               start=False, stop=True, skip_group_check=True)
                    ins.then_inc(S["top"], 1)

            def turn_tops(i, k):
                pe.wait_ge(S["ntop"], i + 1)
                if not isinstance(i, int) or i >= 3:
                    pe.wait_ge(S["s"], i - 2)
                for t in range(QT):
                    ins = nc.tensor.transpose(ntopT_ps[:, t * P:(t + 1) * P], ntop[:, t, :], on.ident_bf[:, :])
                ins.then_inc(S["ntopTp"], 1)

            def scores(r, i, k):
                if softmax:
                    pe.wait_ge(S["ntopT"], i + 1)
                else:
                    operands_ready(r, i)
                for h in two_heads(r):
                    pe.wait_ge(S["probs"], i * heads + h + 1)
                    bank = score_ps[h % 2]
                    for kt, lo, hi, m0 in ((0, 0, 2 * P, 0), (1, 2 * P, CW, 2 * P)):
                        for n, (q, key) in enumerate(operands(k, h, kt, QT, kt, kt + 1)):
                            ins = nc.tensor.matmul(bank[:, lo:hi], key, q, start=(n == 0), stop=True,
                                                   skip_group_check=(n > 0))
                        if softmax:
                            nc.tensor.matmul(bank[:, lo:hi], sel[:, h, :], ntopT[k][:, kt * P:], start=False,
                                             stop=True, skip_group_check=True)
                            ins = nc.tensor.matmul(bank[:, m0:m0 + P], on.ident_bf[:, :], on.mask_kq[:, :],
                                                   start=False, stop=True, skip_group_check=True)
                    ins.then_inc(S["score"], 1)

            def values(half):
                def fn(i, k):
                    if half == 0:
                        pe.wait_ge(S["v1"], i + 1)
                    pe.wait_ge(S["probs"], i * heads + ((heads if half or latent else HALF) + 2))
                    pe.wait_ge(S["pvout"], i * 2)
                    if latent and half:
                        for kt, lo in ((0, 0), (1, 2 * P)):
                            for g in range(kvh):
                                for j in range(4):
                                    ins = nc.tensor.matmul(
                                        pv_ps[1][32 * j:32 * j + 32, 0, kt * P:SEQ], den_cols[:, g, :],
                                        probs[k][:, 4 * g + j, lo:lo + (QT - kt) * P],
                                        start=(kt == 0 and g == 0), stop=True, skip_group_check=True)
                        ins.then_inc(S["pv"], 1)
                        return
                    for strip in range(2):
                        for kt, lo in ((0, 0), (1, 2 * P)):
                            for j in range(4):
                                h = (0 if latent else half * HALF) + strip * 4 + j
                                ins = nc.tensor.matmul(
                                    pv_ps[half][32 * j:32 * j + 32, strip, kt * P:SEQ],
                                    v1[k][:, kt, strip if latent else h, :],
                                    probs[k][:, h, lo:lo + (QT - kt) * P],
                                    start=(kt == 0), stop=(kt == 1), skip_group_check=True)
                    ins.then_inc(S["pv"], 1)
                return fn

            def token_major(t):
                def fn(i, k):
                    if t == 0:
                        pe.wait_ge(S["pvout"], (i + 1) * 2)
                        pe.wait_ge(S["s"], i)
                        if softmax:
                            pe.wait_ge(S["ntopT"], upto(i + 3, BATCH))
                    else:
                        pe.wait_ge(S["o"], i * QT + t)
                    for strip in range(STRIPS):
                        ins = nc.tensor.transpose(desk[:, strip, :], pv_sb[:, strip, t * P:(t + 1) * P], on.ident[:, :])
                    ins.then_inc(S["tokmaj"], 1)
                return fn

            def turn_output(i, k):
                pe.wait_ge(S["o"], (i + 1) * QT)
                for t in range(QT):
                    for c in range(OB):
                        o = o_sb[:, t, :, :].rearrange("p h d -> p (h d)")[:, c * P:(c + 1) * P]
                        ins = nc.tensor.transpose(desk[:, t * OB + c, :], o, on.ident[:, :])
                ins.then_inc(S["oturned"], 1)

            def output(i, k):
                pe.wait_ge(S["oT"], i + 1)
                for t in range(QT):
                    for c in range(OB):
                        ins = nc.tensor.matmul(desk[:, t, :], oT[:, t, c, :], wo[:, c, :], start=(c == 0),
                                               stop=(c == OB - 1))
                ins.then_inc(S["out"], 1)

            after = {r: [] for r in range(ROUNDS)}
            after[0] = [(token_major(0), LAG + 2)]
            after[ROUNDS // 4 + 1] += [(values(1), LAG + 1)]
            after[ROUNDS // 2 - 1] += [(token_major(1), LAG + 2)]
            after[ROUNDS // 2 + 1] += [(turn_output, LAG + 2)]
            if latent:
                after[2] += [(step(turn, 0), FILL)]
                after[3] += [(step(turn, 1), FILL), (step(turn, 2), FILL), (output, LAG + 2), (step(turn, 3), FILL)]
            else:
                after[0] += [(step(turn, 2), 1)]
                after[2] += [(step(turn, 3), 1)]
                after[4] += [(step(turn, 0), FILL)]
                after[6] += [(step(turn, 1), FILL)]
                after[7] += [(output, LAG + 2)]
            steps = [(values(0), LAG + 1)] + [(turn_tops, LAG)] * softmax
            for r in range(ROUNDS):
                steps += [(step(tops_, r), TOP)] * softmax + [(step(scores, r), LAG)] + after[r]
            software_pipeline(nc.tensor.Fori, steps, BATCH)

        @block.scalar
        def _(act):
            if softmax:
                act.sem_inc(S["probs"], 2)

            def exps(r, i, k):
                for h in two_heads(r):
                    act.wait_ge(S["score"], i * heads + h + 1)
                    nc.scalar.activation(probs[k][:, h, :], score_ps[h % 2][:, 0:CW], ACT.Exp, scale=softmax_scale)\
                        .then_inc(S["probs"], 1)

            def copy_tops(i, k):
                act.wait_ge(S["ntopTp"], i + 1)
                nc.scalar.activation(ntopT[k][:, :], ntopT_ps, ACT.Copy).then_inc(S["ntopT"], 1)

            def copy_operands(n, i, k):
                act.wait_ge(S["turned"], i * 4 + n + 1 + 4 * stacks)
                j, block = FILLS[n]
                nc.scalar.activation(opT[k][j][:, block:block + 4, :], opT_ps[:, :, :], ACT.Copy)\
                    .then_inc(S["opT"], 1)

            def take_values(half):
                def fn(i, k):
                    act.wait_ge(S["pv"], i * 2 + half + 3)
                    act.wait_ge(S["tokmaj"], i * QT)
                    n = 1 if latent and half else 2
                    nc.scalar.activation(pv_sb[:, 2 * half:2 * half + n, :], pv_ps[half][:, 0:n, :], ACT.Copy)\
                        .then_inc(S["pvout"], 1)
                return fn

            def copy_output(i, k):
                act.wait_ge(S["oturned"], i + 1)
                act.wait_ge(S["out"], i)
                nc.scalar.activation(oT[:, :, :, :].rearrange("p t c d -> p (t c) d"), desk[:, 0:QT * OB, :], ACT.Copy)\
                    .then_inc(S["oT"], 1)

            after = {r: [] for r in range(ROUNDS)}
            after[ROUNDS // 2] += [(take_values(0), LAG + 1), (take_values(1), LAG + 1)]
            if latent:
                after[3] += [(step(copy_operands, 0), FILL), (copy_output, LAG + 2), (step(copy_operands, 1), FILL),
                             (step(copy_operands, 2), FILL), (step(copy_operands, 3), FILL)]
            else:
                after[0] += [(step(copy_operands, 2), 1)]
                after[2] += [(step(copy_operands, 3), 1)]
                after[4] += [(step(copy_operands, 0), FILL)]
                after[6] += [(copy_output, LAG + 2), (step(copy_operands, 1), FILL)]
            steps = [(copy_tops, LAG)] * softmax
            for r in range(ROUNDS):
                steps += [(step(exps, r), LAG)] * softmax + after[r]
            software_pipeline(nc.scalar.Fori, steps, BATCH)


def channel_attention_stage(nc, on, name, dram, heads, hd):
    PAIRS = heads // 2
    assert 2 * hd == P and PAIRS * P == 2 * COLS
    ctx, sb, pb, sem = scope(nc)
    with ctx:
        w_q, w_k = sb(f"{name}_wq", [P, PAIRS, P]), sb(f"{name}_wk", [P, PAIRS, P])
        w_vT, w_out = sb(f"{name}_wvT", [P, PAIRS, P]), sb(f"{name}_wout", [P, PAIRS, P])
        temp, gamma = sb(f"{name}_temp", [P, PAIRS]), sb(f"{name}_gamma", [P, D])
        square = sb(f"{name}_square", [P, TILES, D])
        norm2, norm = sb(f"{name}_norm2", [P, TILES]), sb(f"{name}_norm", [P, TILES])
        x_b = [sb(f"{name}_x{k}", [P, QT, D]) for k in range(2)]
        xT = sb(f"{name}_xT", [P, TOKENS])
        xT_b = sb(f"{name}_xTb", [P, SEQ])
        gram = [sb(f"{name}_gram{k}", [P, P]) for k in range(2)]
        tk = [sb(f"{name}_tk{k}", [P, PAIRS, P]) for k in range(2)]
        sq_k, sq_q = sb(f"{name}_sqk", [P, PAIRS, P]), sb(f"{name}_sqq", [P, PAIRS, P])
        rk, rq = sb(f"{name}_rk", [P, PAIRS, hd]), sb(f"{name}_rq", [P, PAIRS])
        rk_root, rq_root = sb(f"{name}_rkroot", [P, PAIRS, hd]), sb(f"{name}_rqroot", [P, PAIRS])
        logit = sb(f"{name}_logit", [P, PAIRS, hd])
        top, total = sb(f"{name}_top", [P, PAIRS]), sb(f"{name}_total", [P, PAIRS])
        attn = [sb(f"{name}_attn{k}", [P, PAIRS, P]) for k in range(2)]
        u_sb, m_sb = sb(f"{name}_u", [P, PAIRS, P]), sb(f"{name}_m", [P, P])
        tk_ps, tq_ps = pb(f"{name}_tkp", [P, 2, COLS]), pb(f"{name}_tqp", [P, 2, COLS])
        pair_ps = pb(f"{name}_pairp", [P, PAIRS, P])
        rk_ps = pb(f"{name}_rkp", [P, PAIRS, hd])
        gram_ps = pb(f"{name}_gramp", [P, 4, P])
        S = {w: sem(f"{name}_{w}") for w in (
            "w", "zero", "pre", "preroot", "temp", "x", "gramp", "gram", "tkq", "tk", "sq", "norms", "roots", "clip", "inv", "r",
            "simp", "logit", "chain", "exp", "sum", "attn", "up", "u", "mp", "m", "xTb", "out", "s")}
        block = ctx.enter_context(nc.Block())
        loads = [(w_q[:, :, :], dram["w_q"]), (w_k[:, :, :], dram["w_k"]), (w_vT[:, :, :], dram["w_vT"]),
                 (w_out[:, :, :], dram["w_out"]), (temp[:, :], dram["temp"]), (gamma[:, :], dram["gamma"])]
        halves = (slice(0, hd), slice(hd, P))

        @block.sync
        def _(sp):
            for dst, src in loads:
                sp.dma_start(dst, src).then_inc(S["w"], 16)

        @block.gpsimd
        def _(pool):
            for k in range(2):
                ins = nc.gpsimd.memset(attn[k][:, :, :], 0.0)
            ins.then_inc(S["zero"], 1)

            def copy_x(i, k):
                pool.wait_ge(S["out"], i)
                pool.wait_ge(S["gram"], i * 2 + 2)
                nc.gpsimd.tensor_copy(xT_b[:, :], xT[:, bass.ts(i, SEQ)]).then_inc(S["xTb"], 1)

            software_pipeline(nc.gpsimd.Fori, [(copy_x, 0)], BATCH)

        @block.vector
        def _(dve):
            dve.wait_ge(S["w"], 16 * len(loads))
            dve.wait_ge(S["zero"], 1)
            dve.sem_inc(S["s"], 2)
            nc.vector.tensor_tensor(square[:, :, :], on.xn[:, :, :], on.xn[:, :, :], ALU.mult).then_inc(S["pre"], 1)
            dve.wait_ge(S["pre"], 1)
            nc.vector.tensor_reduce(norm2[:, :], square[:, :, :], AX.X, ALU.add).then_inc(S["pre"], 1)
            dve.wait_ge(S["pre"], 2)
            nc.vector.tensor_scalar(norm2[:, :], norm2[:, :], 1e-24, 1.0 / D, ALU.max, ALU.mult).then_inc(S["pre"], 1)
            dve.wait_ge(S["preroot"], 1)
            nc.vector.reciprocal(norm[:, :], norm[:, :]).then_inc(S["pre"], 1)
            dve.wait_ge(S["temp"], 1)
            nc.vector.tensor_scalar(temp[:, :], temp[:, :], 8.0, None, ALU.mult).then_inc(S["pre"], 1)
            dve.wait_ge(S["pre"], 5)

            def x_in(i, k):
                dve.wait_ge(S["gramp"], i + 1)
                for t in range(QT):
                    ins = nc.vector.scalar_tensor_tensor(
                        x_b[k][:, t, :], on.xn[:, bass.ds(i * QT + t, 1), :], norm[:, bass.ds(i * QT + t, 1)],
                        gamma[:, :], ALU.mult, ALU.mult)
                ins.then_inc(S["x"], 1)

            def scores(i, k):
                dve.wait_ge(S["simp"], i + 1)
                dve.wait_ge(S["r"], i + 1)
                for r in halves:
                    ins = nc.vector.tensor_tensor(logit[r, :, :], pair_ps[r, :, r], rk[r, :, :], ALU.mult)
                ins.then_inc(S["logit"], 1)
                dve.wait_ge(S["logit"], i + 1)

                def wide(a):
                    return a[:, :].unsqueeze(2).broadcast_to([P, PAIRS, hd])

                nc.vector.tensor_tensor(logit[:, :, :], logit[:, :, :], wide(rq), ALU.mult).then_inc(S["chain"], 1)
                dve.wait_ge(S["chain"], i * 3 + 1)
                nc.vector.tensor_reduce(top[:, :], logit[:, :, :], AX.X, ALU.max).then_inc(S["chain"], 1)
                dve.wait_ge(S["chain"], i * 3 + 2)
                nc.vector.tensor_tensor(logit[:, :, :], logit[:, :, :], wide(top), ALU.subtract).then_inc(S["chain"], 1)

            def squares(i, k):
                dve.wait_ge(S["tkq"], i + 1)
                dve.wait_ge(S["norms"], i)
                nc.vector.tensor_tensor(sq_q[:, :, :].rearrange("p a b -> p (a b)"),
                                        tq_ps[:, :, :].rearrange("p a b -> p (a b)"),
                                        w_q[:, :, :].rearrange("p a b -> p (a b)"), ALU.mult)
                dve.wait_ge(S["tk"], i + 1)
                ins = nc.vector.tensor_tensor(sq_k[:, :, :], tk[k][:, :, :], w_k[:, :, :], ALU.mult)
                ins.then_inc(S["sq"], 1)

            def weights(i, k):
                dve.wait_ge(S["exp"], i + 1)
                nc.vector.tensor_reduce(total[:, :], logit[:, :, :], AX.X, ALU.add).then_inc(S["sum"], 1)
                dve.wait_ge(S["sum"], i * 2 + 1)
                nc.vector.reciprocal(total[:, :], total[:, :]).then_inc(S["sum"], 1)
                dve.wait_ge(S["sum"], i * 2 + 2)
                dve.wait_ge(S["up"], i + 1)
                for r in halves:
                    ins = nc.vector.tensor_tensor(attn[k][r, :, r], logit[r, :, :],
                                                  total[r, :].unsqueeze(2).broadcast_to([hd, PAIRS, hd]), ALU.mult)
                ins.then_inc(S["attn"], 1)
                dve.wait_ge(S["attn"], i + 1)

            def inverse_norms(i, k):
                dve.wait_ge(S["roots"], i + 1)
                nc.vector.tensor_scalar(rk_root[:, :, :], rk_root[:, :, :], 1e-12, None, ALU.max)
                nc.vector.tensor_scalar(rq_root[:, :], rq_root[:, :], 1e-12, None, ALU.max).then_inc(S["clip"], 1)
                dve.wait_ge(S["clip"], i + 1)
                nc.vector.reciprocal(rk[:, :, :], rk_root[:, :, :])
                nc.vector.reciprocal(rq[:, :], rq_root[:, :]).then_inc(S["inv"], 1)
                dve.wait_ge(S["inv"], i + 1)
                nc.vector.tensor_tensor(rq[:, :], rq[:, :], temp[:, :], ALU.mult).then_inc(S["r"], 1)

            def store(i, k):
                dve.wait_ge(S["out"], i + 1)
                nc.vector.tensor_copy(on.s[:, bass.ds(i * QT, QT), :],
                                      tk_ps[:, 1, 0:SEQ].rearrange("p (t d) -> p t d", t=QT)).then_inc(S["s"], 1)

            software_pipeline(nc.vector.Fori, [(x_in, 0), (scores, 2), (squares, 1), (weights, 2), (inverse_norms, 1),
                                               (store, 3)], BATCH)

        @block.tensor
        def _(pe):
            pe.sem_inc(S["gramp"], 2)
            pe.sem_inc(S["up"], 2)
            pe.wait_ge(S["w"], 16 * len(loads))

            def gram_of(i, k):
                pe.wait_ge(S["x"], i + 1)
                pe.wait_ge(S["gram"], i * 2)
                for t in range(QT):
                    nc.tensor.matmul(gram_ps[:, 0, :], x_b[k][:, t, :], x_b[k][:, t, :], start=(t == 0),
                                     stop=(t == QT - 1))
                for t in range(QT):
                    ins = nc.tensor.transpose(gram_ps[:, 1 + t, :], x_b[k][:, t, :], on.ident[:, :])
                ins.then_inc(S["gramp"], 1)

            def sims(i, k):
                pe.wait_ge(S["tk"], i + 1)
                pe.wait_ge(S["u"], i)
                for p in range(PAIRS):
                    ins = nc.tensor.matmul(pair_ps[:, p, :], w_q[:, p, :], tk[k][:, p, :], start=True, stop=True)
                ins.then_inc(S["simp"], 1)

            def gram_w(i, k):
                pe.wait_ge(S["gram"], i * 2 + 2)
                pe.wait_ge(S["s"], i)
                pe.wait_ge(S["roots"], i)
                for w, ps in ((w_k, tk_ps), (w_q, tq_ps)):
                    for c in range(2):
                        ins = nc.tensor.matmul(ps[:, c, :], gram[k][:, :],
                                               w[:, 4 * c:4 * c + 4, :].rearrange("p a b -> p (a b)"),
                                               start=True, stop=True)
                ins.then_inc(S["tkq"], 1)

            def mix(i, k):
                pe.wait_ge(S["attn"], i + 1)
                pe.wait_ge(S["logit"], upto(i + 2, BATCH))
                for p in range(PAIRS):
                    ins = nc.tensor.matmul(pair_ps[:, p, :], attn[k][:, p, :], w_out[:, p, :], start=True, stop=True)
                ins.then_inc(S["up"], 1)

            def norms(i, k):
                pe.wait_ge(S["sq"], i + 1)
                pe.wait_ge(S["roots"], i)
                for half, r in enumerate(halves):
                    nc.tensor.matmul(rk_ps[r, :, :], on.ones[:, 0:hd], sq_k[:, :, r], start=True, stop=True)
                for p in range(PAIRS):
                    ins = nc.tensor.matmul(tq_ps[:, 0, p:p + 1], sq_q[:, p, :], on.ones[:, 0:1], start=True, stop=True)
                ins.then_inc(S["norms"], 1)

            def fold(i, k):
                pe.wait_ge(S["u"], i + 2)
                pe.wait_ge(S["tk"], upto(i + 3, BATCH))
                pe.wait_ge(S["sq"], upto(i + 3, BATCH))
                for p in range(PAIRS):
                    ins = nc.tensor.matmul(tk_ps[:, 0, 0:P], w_vT[:, p, :], u_sb[:, p, :], start=(p == 0),
                                           stop=(p == PAIRS - 1))
                ins.then_inc(S["mp"], 1)

            def output(i, k):
                pe.wait_ge(S["m"], i + 1)
                pe.wait_ge(S["xTb"], i + 1)
                pe.wait_ge(S["s"], i + 2)
                for t in range(QT):
                    ins = nc.tensor.matmul(tk_ps[:, 1, t * P:(t + 1) * P], xT_b[:, t * P:(t + 1) * P], m_sb[:, :],
                                           start=True, stop=True)
                ins.then_inc(S["out"], 1)

            software_pipeline(nc.tensor.Fori, [(gram_of, 0), (sims, 2), (gram_w, 1), (mix, 3), (norms, 1), (fold, 3),
                                               (output, 3)], BATCH)

        @block.scalar
        def _(act):
            act.sem_inc(S["u"], 1)
            act.wait_ge(S["w"], 16 * len(loads))
            act.wait_ge(S["pre"], 3)
            nc.scalar.activation(norm[:, :], norm2[:, :], ACT.Sqrt).then_inc(S["preroot"], 1)
            nc.scalar.activation(temp[:, :], temp[:, :], ACT.Exp).then_inc(S["temp"], 1)

            def copy_gram(i, k):
                act.wait_ge(S["gramp"], i + 3)
                nc.scalar.activation(gram[k][:, :], gram_ps[:, 0, :], ACT.Copy).then_inc(S["gram"], 1)
                nc.scalar.activation(xT[:, bass.ts(i, SEQ)], gram_ps[:, 1:3, :].rearrange("p t d -> p (t d)"), ACT.Copy)\
                    .then_inc(S["gram"], 1)

            def exps(i, k):
                act.wait_ge(S["chain"], i * 3 + 3)
                nc.scalar.activation(logit[:, :, :], logit[:, :, :], ACT.Exp).then_inc(S["exp"], 1)

            def copy_tk(i, k):
                act.wait_ge(S["tkq"], i + 1)
                act.wait_ge(S["simp"], i)
                nc.scalar.activation(tk[k][:, :, :].rearrange("p a b -> p (a b)"),
                                     tk_ps[:, :, :].rearrange("p a b -> p (a b)"), ACT.Copy).then_inc(S["tk"], 1)

            def copy_u(i, k):
                act.wait_ge(S["up"], i + 3)
                act.wait_ge(S["mp"], i)
                nc.scalar.activation(u_sb[:, :, :], pair_ps[:, :, :], ACT.Copy).then_inc(S["u"], 1)

            def roots(i, k):
                act.wait_ge(S["norms"], i + 1)
                act.wait_ge(S["r"], i)
                nc.scalar.activation(rk_root[:, :, :], rk_ps[:, :, :], ACT.Sqrt)
                nc.scalar.activation(rq_root[:, :], tq_ps[:, 0, 0:PAIRS], ACT.Sqrt).then_inc(S["roots"], 1)

            def copy_m(i, k):
                act.wait_ge(S["mp"], i + 1)
                act.wait_ge(S["out"], i)
                nc.scalar.activation(m_sb[:, :], tk_ps[:, 0, 0:P], ACT.Copy).then_inc(S["m"], 1)

            software_pipeline(nc.scalar.Fori, [(copy_gram, 0), (exps, 2), (copy_tk, 1), (copy_u, 3), (roots, 1),
                                               (copy_m, 3)], BATCH)


def centroid_route_stage(nc, on, name, dram, experts, combine, w1, b1, chunks):
    ctx, sb, pb, sem = scope(nc)
    with ctx:
        centT, b2 = sb(f"{name}_centT", [P, experts]), sb(f"{name}_b2", [experts, D])
        ln_g, ln_b = sb(f"{name}_lng", [P, experts]), sb(f"{name}_lnb", [P, experts])
        rank_w = sb(f"{name}_rankw", [P, experts])
        aff, pick = sb(f"{name}_aff", [P, TILES, experts]), sb(f"{name}_pick", [P, TILES, experts])
        best, first, alpha = (sb(f"{name}_{w}", [P, TILES]) for w in ("best", "first", "alpha"))
        combT = [sb(f"{name}_combT{k}", [experts, COLS]) for k in range(2)]
        aff_ps = pb(f"{name}_affp", [P, COLS])
        bias_ps = pb(f"{name}_biasp", [P, COLS])
        turn_ps = [pb(f"{name}_turnp{k}", [P, COLS]) for k in range(2)]
        init_ps = [pb(f"{name}_initp{k}", [P, TPB, D]) for k in range(2)]
        S = {w: sem(f"{name}_{w}") for w in ("w", "aff", "bias", "chain", "alpha", "scaled", "turned", "combT", "init",
                                             "g")}
        loads = [(centT[:, :], dram["centT"]), (b2[:, :], dram["b2"]), (ln_g[:, :], dram["ln_g"]),
                 (ln_b[:, :], dram["ln_b"]), (rank_w[:, :], dram["rank_w"]), (w1[:, :, :], dram["w1"]),
                 (b1[:, :, :].rearrange("p e c -> p (e c)"), dram["b1"])]
        block = ctx.enter_context(nc.Block())

        @block.sync
        def _(sp):
            for dst, src in loads:
                sp.dma_start(dst, src).then_inc(S["w"], 16)

        @block.tensor
        def _(pe):
            pe.wait_ge(S["w"], 16 * len(loads))
            for t in range(TILES):
                ins = nc.tensor.matmul(aff_ps[:, t * experts:(t + 1) * experts], on.xnT[:, t * P:(t + 1) * P],
                                       centT[:, :], start=True, stop=True)
            ins.then_inc(S["aff"], 1)
            for e in range(experts):
                for c in range(chunks):
                    n = e * chunks + c
                    ins = nc.tensor.matmul(bias_ps[:, n:n + 1], w1[:, e, c * P:(c + 1) * P], ln_b[:, e:e + 1],
                                           start=True, stop=True)
            ins.then_inc(S["bias"], 1)
            pe.wait_ge(S["chain"], 7)
            for i in range(BLOCKS + 1):
                if i < BLOCKS:
                    if i >= 2:
                        pe.wait_ge(S["combT"], i - 1)
                    for t in range(TPB):
                        ins = nc.tensor.transpose(turn_ps[i % 2][0:experts, t * P:(t + 1) * P],
                                                  combine[:, i * TPB + t, :], on.ident[:, :])
                    ins.then_inc(S["turned"], 1)
                if i:
                    pe.wait_ge(S["combT"], i)
                    if i >= 3:
                        pe.wait_ge(S["g"], i - 2)
                    for t in range(TPB):
                        ins = nc.tensor.matmul(init_ps[(i - 1) % 2][:, t, :], combT[(i - 1) % 2][:, t * P:(t + 1) * P],
                                               b2[:, :], start=True, stop=True)
                    ins.then_inc(S["init"], 1)

        @block.scalar
        def _(act):
            act.wait_ge(S["chain"], 2)
            nc.scalar.activation(alpha[:, :], best[:, :], ACT.Sigmoid).then_inc(S["alpha"], 1)
            for i in range(BLOCKS):
                act.wait_ge(S["turned"], i + 1)
                if i >= 2:
                    act.wait_ge(S["init"], i - 1)
                nc.scalar.activation(combT[i % 2][:, :], turn_ps[i % 2][0:experts, :], ACT.Copy)\
                    .then_inc(S["combT"], 1)

        @block.vector
        def _(dve):
            done = [0]

            def link(ins):
                done[0] += 1
                ins.then_inc(S["chain"], 1)
                dve.wait_ge(S["chain"], done[0])

            def wide(a):
                return a[:, :].unsqueeze(2).broadcast_to([P, TILES, experts])

            dve.wait_ge(S["w"], 16 * len(loads))
            dve.wait_ge(S["aff"], 1)
            link(nc.vector.tensor_copy(aff[:, :, :].rearrange("p t e -> p (t e)"), aff_ps[:, 0:TILES * experts]))
            link(nc.vector.tensor_reduce(best[:, :], aff[:, :, :], AX.X, ALU.max))
            link(nc.vector.tensor_tensor(pick[:, :, :], aff[:, :, :], wide(best), ALU.is_equal))
            link(nc.vector.tensor_tensor(pick[:, :, :], pick[:, :, :],
                                         rank_w[:, :].unsqueeze(1).broadcast_to([P, TILES, experts]), ALU.mult))
            link(nc.vector.tensor_reduce(first[:, :], pick[:, :, :], AX.X, ALU.max))
            link(nc.vector.tensor_tensor(pick[:, :, :], pick[:, :, :], wide(first), ALU.is_equal))
            dve.wait_ge(S["alpha"], 1)
            link(nc.vector.tensor_tensor(combine[:, :, :], pick[:, :, :], wide(alpha), ALU.mult))
            dve.wait_ge(S["bias"], 1)
            flat = b1[:, :, :].rearrange("p e c -> p (e c)")
            nc.vector.tensor_tensor(flat, flat, bias_ps[:, 0:experts * chunks], ALU.add)
            for e in range(experts):
                nc.vector.tensor_scalar(w1[:, e, :], w1[:, e, :], ln_g[:, e:e + 1], None, ALU.mult)
            for i in range(BLOCKS):
                dve.wait_ge(S["init"], i + 1)
                t = slice(i * TPB, (i + 1) * TPB)
                nc.vector.tensor_tensor(on.g[:, t, :], init_ps[i % 2][:, :, :], on.xn[:, t, :], ALU.add)\
                    .then_inc(S["g"], 1)


def centroid_experts(nc, on, name, dram, experts, chunks):
    with nc.sbuf_tensor(f"{name}_combine", [P, TILES, experts], F32) as combine, \
            nc.sbuf_tensor(f"{name}_w1", [P, experts, chunks * P], F32) as w1, \
            nc.sbuf_tensor(f"{name}_b1", [P, experts, chunks], F32) as b1:
        centroid_route_stage(nc, on, f"{name}r", dram, experts, combine, w1, b1, chunks)
        layernorm_stage(nc, on, f"{name}n", on.xn, on.v, on.xnT, False)
        weights = {"gate": lambda e: w1[:, bass.ds(e, 1), :].rearrange("p e (c f) -> p (e c) f", f=P),
                   "down": lambda e: dram["w2"][bass.ds(e, 1), :, :].rearrange("e p (c d) -> (e p) c d", d=D),
                   "bias": lambda e: b1[:, bass.ds(e, 1), :]}
        ffn_stage(nc, on, f"{name}e", on.xnT, on.g, experts, chunks, 1, weights, False, combine=combine)


def top_route_stage(nc, on, name, dram, experts, top_k, combine):
    ctx, sb, pb, sem = scope(nc)
    with ctx:
        routerT, bias = sb(f"{name}_routerT", [P, experts]), sb(f"{name}_bias", [P, experts])
        prob, fixed, mask, equal, order, keep = (sb(f"{name}_{w}", [P, TILES, experts]) for w in (
            "prob", "fixed", "mask", "equal", "order", "keep"))
        most = sb(f"{name}_most", [P, TILES, 8])
        col = [sb(f"{name}_col{k}", [P, TILES]) for k in range(2)]
        logit_ps = [pb(f"{name}_logitp{k}", [P, TILES // 2, experts]) for k in range(2)]
        S = {w: sem(f"{name}_{w}") for w in ("w", "logit", "chain", "exp")}
        loads = [(routerT[:, :], dram["routerT"]), (bias[:, :], dram["bias"])]
        block = ctx.enter_context(nc.Block())

        @block.sync
        def _(sp):
            for dst, src in loads:
                sp.dma_start(dst, src).then_inc(S["w"], 16)

        @block.tensor
        def _(pe):
            pe.wait_ge(S["w"], 16 * len(loads))
            for t in range(TILES):
                ins = nc.tensor.matmul(logit_ps[t // (TILES // 2)][:, t % (TILES // 2), :],
                                       on.xnT[:, t * P:(t + 1) * P], routerT[:, :], start=True, stop=True)
            ins.then_inc(S["logit"], 1)

        @block.scalar
        def _(act):
            act.wait_ge(S["chain"], 4)
            nc.scalar.activation(prob[:, :, :], prob[:, :, :], ACT.Exp).then_inc(S["exp"], 1)

        @block.vector
        def _(dve):
            done = [0]

            def link(ins):
                done[0] += 1
                ins.then_inc(S["chain"], 1)
                dve.wait_ge(S["chain"], done[0])

            def wide(a):
                return a.unsqueeze(2).broadcast_to([P, TILES, experts])

            def each(out, a, b, op):
                link(nc.vector.tensor_tensor(out[:, :, :], a[:, :, :], b, op))

            nc.vector.memset(order[:, :, :], 1.0)
            dve.wait_ge(S["w"], 16 * len(loads))
            dve.wait_ge(S["logit"], 1)
            half = TILES // 2
            link(nc.vector.tensor_copy(prob[:, 0:half, :], logit_ps[0][:, :, :]))
            link(nc.vector.tensor_copy(prob[:, half:, :], logit_ps[1][:, :, :]))
            link(nc.vector.tensor_reduce(col[0][:, :], prob[:, :, :], AX.X, ALU.max))
            each(prob, prob, wide(col[0][:, :]), ALU.subtract)
            dve.wait_ge(S["exp"], 1)
            link(nc.vector.tensor_reduce(col[0][:, :], prob[:, :, :], AX.X, ALU.add))
            link(nc.vector.reciprocal(col[1][:, :], col[0][:, :]))
            each(prob, prob, wide(col[1][:, :]), ALU.mult)
            each(fixed, prob, bias[:, :].unsqueeze(1).broadcast_to([P, TILES, experts]), ALU.add)
            for t in range(TILES):
                ins = nc.vector.max(most[:, t, :], fixed[:, t, :])
            link(ins)
            last = wide(most[:, :, top_k - 1])
            each(keep, fixed, last, ALU.is_gt)
            each(equal, fixed, last, ALU.is_equal)
            link(nc.vector.tensor_reduce(col[0][:, :], keep[:, :, :], AX.X, ALU.add))
            link(nc.vector.tensor_scalar(col[0][:, :], col[0][:, :], -1.0, float(top_k), ALU.mult, ALU.add))
            link(nc.vector.memset(order[:, :, 0:1], 0.0))
            link(nc.vector.tensor_tensor_scan(mask[:, :, :].rearrange("p t e -> p (t e)"),
                                              order[:, :, :].rearrange("p t e -> p (t e)"),
                                              equal[:, :, :].rearrange("p t e -> p (t e)"), 0.0, ALU.mult, ALU.add))
            each(mask, mask, wide(col[0][:, :]), ALU.is_le)
            each(equal, equal, mask[:, :, :], ALU.mult)
            each(keep, keep, equal[:, :, :], ALU.add)
            each(keep, keep, prob[:, :, :], ALU.mult)
            link(nc.vector.tensor_reduce(col[0][:, :], keep[:, :, :], AX.X, ALU.add))
            link(nc.vector.tensor_scalar(col[0][:, :], col[0][:, :], 1e-12, None, ALU.max))
            link(nc.vector.reciprocal(col[1][:, :], col[0][:, :]))
            each(combine, keep, wide(col[1][:, :]), ALU.mult)


def top_experts(nc, on, name, dram, experts, top_k):
    with nc.sbuf_tensor(f"{name}_combine", [P, TILES, experts], F32) as combine:
        top_route_stage(nc, on, f"{name}r", dram, experts, top_k, combine)
        ffn_stage(nc, on, f"{name}s", on.xnT, on.g, 1, 1, 1,
                  {w: (lambda e, w=w: dram[f"shared_{w}"].rearrange("p (c f) -> p c f", c=1))
                   for w in ("gate", "up", "down")}, True)
        ffn_stage(nc, on, f"{name}e", on.xnT, on.g, experts // 2, 1, 2,
                  {w: (lambda e, w=w: dram[f"pair_{w}"][bass.ds(e, 1), :, :].rearrange("e p f -> p e f"))
                   for w in ("gate", "up", "down")}, True, combine=combine)


def unpack_weights_stage(nc, on, name, dram, scale, w_sb):
    ctx, sb, pb, sem = scope(nc)
    with ctx:
        kinds = list(w_sb)
        whole = {w: sb(f"{name}_{w}", [P, w_sb[w].shape[1], P], I32) for w in kinds}
        loaded, scaled = sem(f"{name}_loaded"), sem(f"{name}_scaled")
        block = ctx.enter_context(nc.Block())

        @block.sync
        def _(sp):
            for w in kinds:
                sp.dma_start(whole[w][:, :, :], dram[w]).then_inc(loaded, 16)

        @block.vector
        def _(dve):
            for n, w in enumerate(kinds):
                dve.wait_ge(loaded, 16 * len(kinds))
                nc.vector.tensor_scalar(w_sb[w][:, :, :], whole[w][:, :, :], scale, None, ALU.mult).then_inc(scaled, 1)
            dve.wait_ge(scaled, len(kinds))


def integer_ffn(nc, on, name, dram, hidden):
    chunks = hidden // P
    ctx, sb, pb, sem = scope(nc)
    with ctx:
        w_sb = {w: sb(f"{name}_{w}", [P, chunks, P]) for w in ("gate", "up", "down")}
        unpack_weights_stage(nc, on, f"{name}u", dram, 1.0 / 127.0, w_sb)
        ffn_stage(nc, on, f"{name}e", on.xnT, on.g, 1, chunks, 1,
                  {w: (lambda e, w=w: w_sb[w][:, :, :]) for w in w_sb}, True)


def choice_route_stage(nc, on, name, dram, experts, capacity, combine, place, values):
    ctx, sb, pb, sem = scope(nc)
    with ctx:
        gateT = sb(f"{name}_gateT", [P, experts])
        score, mask, equal, rank, order = (sb(f"{name}_{w}", [P, experts, TILES]) for w in (
            "score", "mask", "equal", "rank", "order"))
        count, need = sb(f"{name}_count", [P, experts]), sb(f"{name}_need", [P, experts])
        slot, part = (sb(f"{name}_{w}", [P, experts, TILES], I32) for w in ("slot", "part"))
        number = sb(f"{name}_number", [P, P + 1])
        bit, step, least, trial = (sb(f"{name}_{w}", [P, experts], I32) for w in ("bit", "step", "least", "trial"))
        logit_ps = pb(f"{name}_logitp", [P, TILES, experts])
        total_ps = pb(f"{name}_totalp", [P, experts])
        within_ps, tiles_ps = (pb(f"{name}_{w}", [P, experts, TILES]) for w in ("withinp", "tilesp"))
        S = {w: sem(f"{name}_{w}") for w in ("w", "logit", "exp", "chain", "search", "halved", "counted", "rest", "final")}
        BITS = 30
        block = ctx.enter_context(nc.Block())

        loads = [(gateT[:, :], dram["gateT"]), (number[:, :], dram["number"])]

        @block.sync
        def _(sp):
            for dst, src in loads:
                sp.dma_start(dst, src).then_inc(S["w"], 16)

        @block.tensor
        def _(pe):
            pe.wait_ge(S["w"], 16 * len(loads))
            for t in range(TILES):
                ins = nc.tensor.matmul(logit_ps[:, t, :], on.xnT[:, t * P:(t + 1) * P], gateT[:, :], start=True,
                                       stop=True)
            ins.then_inc(S["logit"], 1)
            with nc.tensor.Fori(0, BITS) as i:
                pe.wait_ge(S["search"], i * 4 + 3)
                nc.tensor.matmul(total_ps[:, :], on.ones[:, :], count[:, :], start=True, stop=True)\
                    .then_inc(S["counted"], 1)
            pe.wait_ge(S["rest"], 3)
            nc.tensor.matmul(total_ps[:, :], on.ones[:, :], count[:, :], start=True, stop=True)
            nc.tensor.matmul(within_ps[:, :, :], on.causal[:, :], equal[:, :, :], start=True, stop=True)
            nc.tensor.matmul(tiles_ps[:, :, :], on.ones[:, :], equal[:, :, :], start=True, stop=True)\
                .then_inc(S["final"], 1)
            pe.wait_ge(S["rest"], 4)
            nc.tensor.matmul(within_ps[:, :, :], on.causal[:, :], equal[:, :, :], start=True, stop=True)
            nc.tensor.matmul(tiles_ps[:, :, :], on.ones[:, :], equal[:, :, :], start=True, stop=True)\
                .then_inc(S["final"], 1)

        @block.scalar
        def _(act):
            act.wait_ge(S["logit"], 1)
            nc.scalar.activation(score[:, :, :], logit_ps[:, :, :].rearrange("p t e -> p e t"), ACT.Exp, scale=-1.0)\
                .then_inc(S["exp"], 1)

        @block.vector
        def _(dve):
            done = {w: 0 for w in ("chain", "rest")}

            def link(ins, w="chain"):
                done[w] += 1
                ins.then_inc(S[w], 1)
                dve.wait_ge(S[w], done[w])

            def wide(a):
                return a.unsqueeze(2).broadcast_to([P, experts, TILES])

            nc.vector.memset(order[:, :, :], 1.0)
            nc.vector.memset(bit[:, :], 1 << (BITS - 1))
            link(nc.vector.memset(least[:, :], 0))
            dve.wait_ge(S["exp"], 1)
            link(nc.vector.tensor_scalar(mask[:, :, :], score[:, :, :], 1.0, None, ALU.add))
            link(nc.vector.reciprocal(score[:, :, :], mask[:, :, :]))
            with nc.vector.Fori(0, BITS) as i:
                nc.vector.tensor_tensor(trial[:, :], least[:, :], bit[:, :], ALU.bitwise_or).then_inc(S["search"], 1)
                dve.wait_ge(S["search"], i * 4 + 1)
                nc.vector.tensor_tensor(mask[:, :, :], score[:, :, :], wide(trial[:, :].bitcast(F32)), ALU.is_ge)\
                    .then_inc(S["search"], 1)
                dve.wait_ge(S["search"], i * 4 + 2)
                nc.vector.tensor_reduce(count[:, :], mask[:, :, :], AX.X, ALU.add).then_inc(S["search"], 1)
                dve.wait_ge(S["counted"], i + 1)
                nc.vector.scalar_tensor_tensor(step[:, :], total_ps[:, :], float(capacity), bit[:, :], ALU.is_ge,
                                               ALU.mult).then_inc(S["search"], 1)
                dve.wait_ge(S["search"], i * 4 + 4)
                nc.vector.tensor_tensor(least[:, :], least[:, :], step[:, :], ALU.bitwise_or)
                nc.vector.tensor_scalar(bit[:, :], bit[:, :], 1, None, ALU.logical_shift_right)\
                    .then_inc(S["halved"], 1)
                dve.wait_ge(S["halved"], i + 1)
            last = wide(least[:, :].bitcast(F32))
            link(nc.vector.tensor_tensor(mask[:, :, :], score[:, :, :], last, ALU.is_gt), "rest")
            link(nc.vector.tensor_tensor(equal[:, :, :], score[:, :, :], last, ALU.is_equal), "rest")
            link(nc.vector.tensor_reduce(count[:, :], mask[:, :, :], AX.X, ALU.add), "rest")
            dve.wait_ge(S["final"], 1)
            link(nc.vector.tensor_scalar(need[:, :], total_ps[:, :], -1.0, float(capacity), ALU.mult, ALU.add))
            before_tiles(nc, dve, link, order, rank, tiles_ps, within_ps)
            link(nc.vector.tensor_tensor(rank[:, :, :], rank[:, :, :], wide(need[:, :]), ALU.is_le))
            link(nc.vector.tensor_tensor(equal[:, :, :], equal[:, :, :], rank[:, :, :], ALU.mult))
            link(nc.vector.tensor_tensor(equal[:, :, :], mask[:, :, :], equal[:, :, :], ALU.add), "rest")
            link(nc.vector.tensor_tensor(combine[:, :, :], equal[:, :, :], score[:, :, :], ALU.mult))
            dve.wait_ge(S["final"], 2)
            before_tiles(nc, dve, link, order, rank, tiles_ps, within_ps)
            link(nc.vector.tensor_scalar(slot[:, :, :], rank[:, :, :], -1.0, None, ALU.add))
            link(nc.vector.tensor_scalar(part[:, :, :], slot[:, :, :], P - 1, None, ALU.bitwise_and))
            link(nc.vector.scalar_tensor_tensor(mask[:, :, :], part[:, :, :], 1.0, equal[:, :, :], ALU.add, ALU.mult))
            link(nc.vector.tensor_scalar(place[:, :, :], mask[:, :, :], -1.0, None, ALU.add))
            link(nc.vector.tensor_scalar(part[:, :, :], slot[:, :, :], 7, None, ALU.arith_shift_right))
            dve.wait_ge(S["w"], 16 * len(loads))
            for c in range(capacity // P):
                link(nc.vector.tensor_scalar(mask[:, :, :], part[:, :, :], float(c), None, ALU.is_equal))
                nc.vector.tensor_tensor(values[:, :, :, c, 0].rearrange("p t e -> p e t"), mask[:, :, :],
                                        number[:, 0:TILES].unsqueeze(1).broadcast_to([P, experts, TILES]), ALU.mult)
                link(nc.vector.tensor_scalar(values[:, :, :, c, 1].rearrange("p t e -> p e t"), mask[:, :, :],
                                             number[:, P:P + 1], None, ALU.mult))


def before_tiles(nc, dve, link, order, rank, tiles_ps, within_ps):
    flat = "p e t -> p (e t)"
    link(nc.vector.memset(order[:, :, 0:1], 0.0))
    link(nc.vector.tensor_copy(rank[:, :, :], tiles_ps[:, :, :]))
    link(nc.vector.tensor_tensor_scan(rank[:, :, :].rearrange(flat), order[:, :, :].rearrange(flat),
                                      rank[:, :, :].rearrange(flat), 0.0, ALU.mult, ALU.add))
    link(nc.vector.tensor_tensor(rank[:, :, :], rank[:, :, :], tiles_ps[:, :, :], ALU.subtract))
    link(nc.vector.tensor_tensor(rank[:, :, :], rank[:, :, :], within_ps[:, :, :], ALU.add))


def mixed_bias_stage(nc, on, name, dram, experts, combine):
    ctx, sb, pb, sem = scope(nc)
    with ctx:
        down_b = sb(f"{name}_down_b", [experts, D])
        combT = [sb(f"{name}_combT{k}", [experts, COLS]) for k in range(2)]
        turn_ps = [pb(f"{name}_turnp{k}", [P, COLS]) for k in range(2)]
        sum_ps = [pb(f"{name}_sump{k}", [P, TPB, D]) for k in range(2)]
        loaded, s_turned, s_copied, s_sum, s_added = (sem(f"{name}_{w}") for w in (
            "loaded", "turned", "copied", "sum", "added"))
        block = ctx.enter_context(nc.Block())

        @block.sync
        def _(sp):
            sp.dma_start(down_b[:, :], dram["down_b"]).then_inc(loaded, 16)

        @block.tensor
        def _(pe):
            pe.wait_ge(loaded, 16)
            for i in range(BLOCKS + 1):
                if i < BLOCKS:
                    if i >= 2:
                        pe.wait_ge(s_copied, i - 1)
                    for t in range(TPB):
                        ins = nc.tensor.transpose(turn_ps[i % 2][0:experts, t * P:(t + 1) * P],
                                                  combine[:, :, i * TPB + t], on.ident[:, :])
                    ins.then_inc(s_turned, 1)
                if i:
                    pe.wait_ge(s_copied, i)
                    if i >= 3:
                        pe.wait_ge(s_added, i - 2)
                    for t in range(TPB):
                        ins = nc.tensor.matmul(sum_ps[(i - 1) % 2][:, t, :], combT[(i - 1) % 2][:, t * P:(t + 1) * P],
                                               down_b[:, :], start=True, stop=True)
                    ins.then_inc(s_sum, 1)

        @block.scalar
        def _(act):
            for i in range(BLOCKS):
                act.wait_ge(s_turned, i + 1)
                if i >= 2:
                    act.wait_ge(s_sum, i - 1)
                nc.scalar.activation(combT[i % 2][:, :], turn_ps[i % 2][0:experts, :], ACT.Copy).then_inc(s_copied, 1)

        @block.vector
        def _(dve):
            for i in range(BLOCKS):
                dve.wait_ge(s_sum, i + 1)
                t = slice(i * TPB, (i + 1) * TPB)
                nc.vector.tensor_tensor(on.g[:, t, :], sum_ps[i % 2][:, :, :], on.g[:, t, :], ALU.add)\
                    .then_inc(s_added, 1)


def slot_tokens_stage(nc, on, name, dram, experts, chunks, place, values, token):
    ctx, sb, pb, sem = scope(nc)
    with ctx:
        number = sb(f"{name}_number", [P, P + 1])
        number_bf = sb(f"{name}_number_bf", [P, P], BF16)
        onehot = [sb(f"{name}_onehot{k}", [P, experts, P], BF16) for k in range(2)]
        whole = sb(f"{name}_whole", [P, experts, chunks, 2])
        token_ps = pb(f"{name}_tokenp", [P, experts, chunks * 2])
        loaded, s_onehot, s_used, s_chain = (sem(f"{name}_{w}") for w in ("loaded", "onehot", "used", "chain"))
        block = ctx.enter_context(nc.Block())

        @block.sync
        def _(sp):
            sp.dma_start(number[:, :], dram["number"]).then_inc(loaded, 16)

        @block.vector
        def _(dve):
            dve.wait_ge(loaded, 16)
            nc.vector.tensor_copy(number_bf[:, :], number[:, 0:P]).then_inc(s_chain, 1)
            dve.wait_ge(s_chain, 1)

            def mark(t, k):
                dve.wait_ge(s_used, t + 1)
                nc.vector.tensor_tensor(
                    onehot[k][:, :, :],
                    place[:, :, bass.ds(t, 1)].broadcast_to([P, experts, P]),
                    number_bf[:, :].unsqueeze(1).broadcast_to([P, experts, P]), ALU.is_equal).then_inc(s_onehot, 1)

            software_pipeline(nc.vector.Fori, [(mark, 0)], TILES)
            dve.wait_ge(s_used, TILES + 2)
            nc.vector.tensor_copy(whole[:, :, :, :].rearrange("p e c v -> p e (c v)"), token_ps[:, :, :])\
                .then_inc(s_chain, 1)
            dve.wait_ge(s_chain, 2)
            nc.vector.scalar_tensor_tensor(token[:, :, :], whole[:, :, :, 0], float(P), whole[:, :, :, 1],
                                           ALU.mult, ALU.add).then_inc(s_chain, 1)
            dve.wait_ge(s_chain, 3)

        @block.tensor
        def _(pe):
            pe.sem_inc(s_used, 2)

            def gather(t, k):
                pe.wait_ge(s_onehot, t + 1)
                for e in range(experts):
                    ins = nc.tensor.matmul(
                        token_ps[:, e, :], onehot[k][:, e, :],
                        values[:, bass.ds(t, 1), e, :, :].rearrange("p t c v -> p (t c v)"),
                        start=isinstance(t, int) and t == 0 and e == 0, stop=True, skip_group_check=True)
                ins.then_inc(s_used, 1)

            software_pipeline(nc.tensor.Fori, [(gather, 1)], TILES)


def chosen_experts_stage(nc, on, name, dram, experts, chunks, token, rows, table, sums):
    ctx, sb, pb, sem = scope(nc)
    with ctx:
        RT = rows // P
        W = table.shape[1]
        kinds = ("gate", "up", "down", "bias")
        w_sb = {w: [sb(f"{name}_w_{w}{k}", [P, 1, 2 * chunks] if w == "bias" else [P, chunks, P])
                    for k in range(2)] for w in kinds}
        taken = [sb(f"{name}_taken{k}", [P, RT], U32) for k in range(2)]
        given = [sb(f"{name}_given{k}", [P, RT], U32) for k in range(2)]
        xg = [sb(f"{name}_xg{k}", [P, RT, W]) for k in range(2)]
        xinT = [sb(f"{name}_xinT{k}", [P, rows]) for k in range(2)]
        weight = [sb(f"{name}_weight{k}", [P, RT]) for k in range(2)]
        silu = [sb(f"{name}_silu{k}", [P, rows]) for k in range(2)]
        h = [[sb(f"{name}_h{k}_{c}", [P, rows]) for c in range(chunks)] for k in range(2)]
        scaled = [sb(f"{name}_scaled{k}", [P, RT, D]) for k in range(2)]
        turn_ps = pb(f"{name}_turnp", [P, rows])
        gate_ps = [pb(f"{name}_gatep{k}", [P, rows]) for k in range(2)]
        up_ps = [pb(f"{name}_upp{k}", [P, rows]) for k in range(2)]
        down_ps = [pb(f"{name}_downp{k}", [P, RT, D]) for k in range(2)]
        w_loaded = [sem(f"{name}_w_loaded{k}") for k in range(2)]
        S = {w: sem(f"{name}_{w}") for w in ("init", "taken", "going", "turned", "xinT", "weight", "proj", "silu",
                                             "h", "down", "scaled", "given", "added", "result")}
        gathered = [sem(f"{name}_gathered{k}") for k in range(2)]
        block = ctx.enter_context(nc.Block())

        def gathers(e, k):
            return (e // 2 + 1) * (16 * RT) if isinstance(e, int) else (e - k) * (8 * RT) + 16 * RT

        def pipeline(fori, *steps):
            software_pipeline(fori, list(steps), experts)

        def row_of(kind, e):
            return dram[kind][bass.ds(e, 1), :, :]

        @block.sync
        def _(sp):
            sp.dma_start(sums.rearrange("(t p) d -> p t d", p=P), on.g[:, :, :]).then_inc(S["init"], 16)

            def load(e, k):
                sp.wait_ge(S["down"], e + 1)
                for w in ("gate", "up", "down"):
                    sp.dma_start(w_sb[w][k][:, :, :], row_of(w, e).rearrange("e p (c f) -> (e p) c f", f=P))\
                        .then_inc(w_loaded[k], 16)
                sp.dma_start(w_sb["bias"][k][:, :, :], row_of("bias", e).rearrange("e p b -> p e b"))\
                    .then_inc(w_loaded[k], 16)

            pipeline(nc.sync.Fori, (load, 0))
            sp.wait_ge(S["added"], 16 * RT * experts)
            sp.dma_start(on.g[:, :, :], sums.rearrange("(t p) d -> p t d", p=P)).then_inc(S["result"], 16)
            sp.wait_ge(S["result"], 16)

        @block.gpsimd
        def _(pool):
            pool.wait_ge(S["init"], 16)

            def gather(e, k):
                pool.wait_ge(S["weight"], e + 1)
                pool.wait_ge(S["turned"], e + 1)
                pool.wait_ge(S["taken"], e + 1)
                pool.sem_inc(S["going"], 1)
                for c in range(RT):
                    nc.gpsimd.indirect_dma_start(
                        out=xg[k][:, c, :], out_offset=None, in_=table,
                        in_offset=bass.IndirectOffsetOnAxis(ap=taken[k][:, c:c + 1], axis=0))\
                        .then_inc(gathered[k], 16)

            def scatter(e, k):
                pool.wait_ge(S["added"], e * (16 * RT))
                pool.wait_ge(S["given"], e + 1)
                pool.sem_inc(S["going"], 1)
                for c in range(RT):
                    nc.gpsimd.indirect_dma_start(
                        out=sums, out_offset=bass.IndirectOffsetOnAxis(ap=given[k][:, c:c + 1], axis=0),
                        in_=scaled[k][:, c, :], in_offset=None, compute_op=ALU.add).then_inc(S["added"], 16)

            pipeline(nc.gpsimd.Fori, (gather, 0), (scatter, 3))

        @block.tensor
        def _(pe):
            pe.sem_inc(S["turned"], 2)
            pe.sem_inc(S["down"], 2)

            def turn(e, k):
                pe.wait_ge(gathered[k], gathers(e, k))
                pe.wait_ge(S["xinT"], e + 1)
                for c in range(RT):
                    ins = nc.tensor.transpose(turn_ps[:, c * P:(c + 1) * P], xg[k][:, c, 0:D], on.ident[:, :])
                ins.then_inc(S["turned"], 1)

            def project(e, k):
                pe.wait_ge(w_loaded[k], (e // 2 + 1) * 64 if isinstance(e, int) else (e - k) * 32 + 64)
                pe.wait_ge(S["xinT"], e + 2)
                for c in range(chunks):
                    n, b = e * chunks + c, c % 2
                    pe.wait_ge(S["silu"], n + 1)
                    nc.tensor.matmul(gate_ps[b][:, :], w_sb["gate"][k][:, c, :], xinT[k][:, :], start=True, stop=True)
                    pe.wait_ge(S["h"], n + 1)
                    nc.tensor.matmul(up_ps[b][:, :], w_sb["up"][k][:, c, :], xinT[k][:, :], start=True, stop=True)\
                        .then_inc(S["proj"], 1)

            def down(e, k):
                pe.wait_ge(S["h"], e * chunks + (chunks + 2))
                pe.wait_ge(S["scaled"], e + 1)
                for t in range(RT):
                    for c in range(chunks):
                        ins = nc.tensor.matmul(down_ps[k][:, t, :], h[k][c][:, t * P:(t + 1) * P],
                                               w_sb["down"][k][:, c, :], start=(c == 0), stop=(c == chunks - 1))
                ins.then_inc(S["down"], 1)

            pipeline(nc.tensor.Fori, (down, 3), (project, 2), (turn, 1))

        @block.scalar
        def _(act):
            act.sem_inc(S["xinT"], 1)
            act.sem_inc(S["silu"], 2)

            def copy_x(e, k):
                act.wait_ge(S["turned"], e + 3)
                act.wait_ge(S["proj"], e * chunks - chunks if isinstance(e, int) and e > 0 or not isinstance(e, int)
                            else 0)
                nc.scalar.activation(xinT[k][:, :], turn_ps[:, :], ACT.Copy).then_inc(S["xinT"], 1)

            def silus(e, k):
                for c in range(chunks):
                    n, b = e * chunks + c, c % 2
                    act.wait_ge(S["proj"], n + 1)
                    act.wait_ge(S["h"], n + 1)
                    nc.scalar.activation(silu[b][:, :], gate_ps[b][:, :], ACT.Silu,
                                         bias=w_sb["bias"][k][:, 0, c:c + 1]).then_inc(S["silu"], 1)

            pipeline(nc.scalar.Fori, (silus, 2), (copy_x, 1))

        @block.vector
        def _(dve):
            dve.sem_inc(S["weight"], 2)
            dve.sem_inc(S["scaled"], 2)
            dve.sem_inc(S["h"], 2)

            def take(e, k):
                if not isinstance(e, int) or e >= 2:
                    dve.wait_ge(gathered[k], gathers(e, k) - 16 * RT)
                nc.vector.tensor_copy(taken[k][:, :], token[:, bass.ds(e, 1), :]).then_inc(S["taken"], 1)

            def weights_of(e, k):
                dve.wait_ge(gathered[k], gathers(e, k))
                dve.wait_ge(S["scaled"], e + 1)
                nc.vector.tensor_copy(weight[k][:, :], xg[k][:, :, bass.ds(e + D, 1)]).then_inc(S["weight"], 1)

            def hidden(e, k):
                dve.wait_ge(S["down"], e + 1)
                for c in range(chunks):
                    n, b = e * chunks + c, c % 2
                    dve.wait_ge(S["silu"], n + 3)
                    nc.vector.scalar_tensor_tensor(h[k][c][:, :], up_ps[b][:, :],
                                                   w_sb["bias"][k][:, 0, chunks + c:chunks + c + 1], silu[b][:, :],
                                                   ALU.add, ALU.mult).then_inc(S["h"], 1)

            def scale(e, k):
                dve.wait_ge(S["down"], e + 3)
                dve.wait_ge(S["weight"], e + 3)
                if not isinstance(e, int) or e >= 2:
                    dve.wait_ge(S["added"], e * (16 * RT) - 16 * RT)
                for t in range(RT):
                    ins = nc.vector.tensor_scalar(scaled[k][:, t, :], down_ps[k][:, t, :], weight[k][:, t:t + 1],
                                                  None, ALU.mult)
                ins.then_inc(S["scaled"], 1)
                nc.vector.tensor_copy(given[k][:, :], token[:, bass.ds(e, 1), :]).then_inc(S["given"], 1)

            pipeline(nc.vector.Fori, (take, 0), (scale, 3), (hidden, 2), (weights_of, 1))


def write_table_stage(nc, on, name, experts, combine, table):
    ctx, sb, pb, sem = scope(nc)
    with ctx:
        score = sb(f"{name}_score", [P, TILES, experts])
        ordered, written = sem(f"{name}_ordered"), sem(f"{name}_written")
        block = ctx.enter_context(nc.Block())

        @block.vector
        def _(dve):
            nc.vector.tensor_copy(score[:, :, :], combine[:, :, :].rearrange("p e t -> p t e")).then_inc(ordered, 1)

        @block.sync
        def _(sp):
            rows = table.rearrange("(t p) d -> p t d", p=P)
            sp.dma_start(rows[:, :, 0:D], on.xn[:, :, :]).then_inc(written, 16)
            sp.wait_ge(ordered, 1)
            sp.dma_start(rows[:, :, D:], score[:, :, :]).then_inc(written, 16)
            sp.wait_ge(written, 32)


def choice_experts(nc, on, name, dram, experts, capacity, chunks):
    RT = capacity // P
    table = nc.dram_tensor(f"{name}_table", (TOKENS, D + experts), F32, kind="Internal").ap()
    sums = nc.dram_tensor(f"{name}_sums", (TOKENS, D), F32, kind="Internal").ap()
    with nc.sbuf_tensor(f"{name}_combine", [P, experts, TILES], F32) as combine, \
            nc.sbuf_tensor(f"{name}_token", [P, experts, RT], U32) as token:
        with nc.sbuf_tensor(f"{name}_place", [P, experts, TILES], BF16) as place, \
                nc.sbuf_tensor(f"{name}_values", [P, TILES, experts, RT, 2], BF16) as values:
            choice_route_stage(nc, on, f"{name}r", dram, experts, capacity, combine, place, values)
            slot_tokens_stage(nc, on, f"{name}t", dram, experts, RT, place, values, token)
        write_table_stage(nc, on, f"{name}w", experts, combine, table)
        shared = dram["shared_gate"].shape[1]
        ffn_stage(nc, on, f"{name}s", on.xnT, on.g, 1, shared, 1,
                  {w: (lambda e, w=w: dram[f"shared_{w}"]) for w in ("gate", "up", "down")}, True)
        mixed_bias_stage(nc, on, f"{name}b", dram, experts, combine)
        chosen_experts_stage(nc, on, f"{name}e", dram, experts, chunks, token, capacity, table, sums)


class Chip:
    pass


def persistent(nc, ctx):
    def sb(name, shape, dt=F32):
        return ctx.enter_context(nc.sbuf_tensor(name, shape, dt))

    on = Chip()
    on.x = sb("x_sb", [P, TILES, D])
    on.xn = sb("xn_sb", [P, TILES, D])
    on.xnT = sb("xnT_sb", [P, TOKENS])
    on.s = sb("s_sb", [P, TILES, D])
    on.g = sb("g_sb", [P, TILES, D])
    on.q = on.g
    on.k = on.s
    on.v = sb("v_sb", [P, TILES, D])
    on.ident = sb("ident", [P, P])
    on.ident_bf = sb("ident_bf", [P, P], BF16)
    on.ones = sb("ones", [P, P])
    on.causal = sb("causal", [P, P])
    on.mask_kq = sb("mask_kq", [P, P], BF16)
    on.mask_qk = sb("mask_qk", [P, P], BF16)
    return on


def final_stage(nc, on, out):
    ctx, sb, pb, sem = scope(nc)
    with ctx:
        gate = [sb(f"out_gate{k}", [P, COLS]) for k in range(2)]
        s_gate, s_prod, s_added, s_stored = (sem(f"out_{w}") for w in ("silu", "prod", "added", "stored"))
        block = ctx.enter_context(nc.Block())

        def block_of(t, i):
            return t[:, i * TPB:(i + 1) * TPB, :].rearrange("p t d -> p (t d)")

        @block.scalar
        def _(act):
            for i in range(BLOCKS):
                if i >= 2:
                    act.wait_ge(s_added, i - 1)
                nc.scalar.activation(gate[i % 2][:, :], block_of(on.g, i), ACT.Silu).then_inc(s_gate, 1)

        @block.vector
        def _(dve):
            for i in range(BLOCKS):
                dve.wait_ge(s_gate, i + 1)
                nc.vector.tensor_tensor(gate[i % 2][:, :], gate[i % 2][:, :], block_of(on.s, i), ALU.mult)\
                    .then_inc(s_prod, 1)
                dve.wait_ge(s_prod, i + 1)
                nc.vector.tensor_tensor(block_of(on.x, i), block_of(on.x, i), gate[i % 2][:, :], ALU.add)\
                    .then_inc(s_added, 1)

        @block.sync
        def _(sp):
            rows = out.rearrange("(t p) d -> p t d", p=P)
            for i in range(BLOCKS):
                sp.wait_ge(s_added, i + 1)
                t = slice(i * TPB, (i + 1) * TPB)
                sp.dma_start(rows[:, t, :], on.x[:, t, :]).then_inc(s_stored, 16)
            sp.wait_ge(s_stored, 16 * BLOCKS)


def gated_mixers_kernel(nc, dram, out):
    def of(layer):
        return {name[len(layer) + 1:]: dram[name] for name in dram if name.startswith(layer + "_")}

    with ExitStack() as ctx:
        on = persistent(nc, ctx)
        constants_stage(nc, on, dram)
        layernorm_stage(nc, on, "n0", on.x, on.xn, on.xnT, False)
        project_stage(nc, on, "p0", of("a0"), 16, "softplus")
        attention_stage(nc, on, "a0", of("a0"), 16, None)
        integer_ffn(nc, on, "f0", of("f0"), 384)
        layernorm_stage(nc, on, "n1", on.x, on.xn, on.xnT, True)
        project_stage(nc, on, "p1", of("a1"), 16, "rope")
        attention_stage(nc, on, "a1", of("a1"), 16, 8 ** -0.5)
        centroid_experts(nc, on, "f1", of("f1"), 8, 4)
        layernorm_stage(nc, on, "n2", on.x, on.xn, on.xnT, True)
        latent_attention(nc, on, "a2", of("a2"), 8, 2)
        top_experts(nc, on, "f2", of("f2"), 32, 6)
        layernorm_stage(nc, on, "n3", on.x, on.xn, on.xnT, True)
        channel_attention_stage(nc, on, "a3", of("a3"), 16, 64)
        choice_experts(nc, on, "f3", of("f3"), 16, 512, 4)
        final_stage(nc, on, out)


def rope_tables():
    pos = np.arange(SEQ, dtype=np.float32)[:, None]
    turn = np.arange(0, 8, 2, dtype=np.float32) / np.float32(8)
    theta = pos * np.exp(-turn * np.float32(np.log(10000.0)))
    tables = np.stack([np.repeat(np.cos(theta), 2, 1), np.repeat(np.sin(theta), 2, 1)]).astype(np.float32)
    return tables.reshape(2, QT, P, 8).transpose(2, 0, 1, 3)


def every_partition(a):
    return np.tile(a[None], (P,) + (1,) * a.ndim)


def row_chunks(w):
    return w.reshape(-1, P, w.shape[1]).transpose(1, 0, 2)


def layouts(i):
    d = {"x": i["L0_attn_x"].reshape(TOKENS, D)}
    for layer, mixer in (("a0", "L0_attn_"), ("a1", "L1_attn_")):
        d[f"{layer}_w"] = np.concatenate([i[mixer + w].T for w in ("Wq", "Wk", "Wv")], 1)
        d[f"{layer}_wo"] = i[mixer + "Wo"].T
        d[f"{layer}_bo"] = every_partition(i[mixer + "bo"])
    d["a0_bias"] = every_partition(np.stack([i["L0_attn_bq"], i["L0_attn_bk"], i["L0_attn_bv"]]))
    for w in ("gate", "up"):
        d[f"f0_{w}"] = i[f"L0_ffn_w_{w}"].T.reshape(P, 3, P)
    d["f0_down"] = row_chunks(i["L0_ffn_w_down"].T)

    d["a1_cos_sin"] = rope_tables()
    d["a1_gamma_beta"] = every_partition(np.stack([np.stack([i[f"L1_attn_{w}_{p}"] for w in "qk"])
                                                   for p in ("gamma", "beta")]))
    d["f1_centT"] = i["L1_ffn_centroids"].T
    d["f1_b2"] = i["L1_ffn_b2"]
    d["f1_ln_g"], d["f1_ln_b"] = i["L1_ffn_ln_g"].T, i["L1_ffn_ln_b"].T
    d["f1_rank_w"] = every_partition(8 - np.arange(8, dtype=np.float32))
    d["f1_w1"] = i["L1_ffn_w1"].transpose(1, 0, 2)
    d["f1_b1"] = i["L1_ffn_b1"].reshape(8, 4, P).transpose(2, 0, 1).reshape(P, 32)
    d["f1_w2"] = i["L1_ffn_w2"].reshape(8, 4, P, P).transpose(0, 2, 1, 3).reshape(8, P, 512)

    d["a2_wqT"] = i["L2_attn_wq"].reshape(P, 8, P).transpose(2, 1, 0)
    d["a2_wo"] = row_chunks(i["L2_attn_wo"])
    d["a2_up"] = np.stack([i["L2_attn_wk_up"].T, i["L2_attn_wv_up"].T], 1)
    d["a2_w_down"] = np.concatenate([i["L2_attn_wk_down"], i["L2_attn_wv_down"]], 1)
    den_cols = np.zeros((P, 2, 32), np.float32)
    den_cols[:, 0, 0] = 1
    den_cols[:, 1, 1] = 1
    d["a2_den_cols"] = den_cols
    gate_up = i["L2_ffn_gate_up_proj"]
    for w, half in (("gate", slice(0, 64)), ("up", slice(64, 128))):
        d[f"f2_pair_{w}"] = gate_up[:, half].reshape(16, P, P).transpose(0, 2, 1)
    d["f2_pair_down"] = i["L2_ffn_down_proj"].transpose(0, 2, 1).reshape(16, P, P)
    d["f2_routerT"] = i["L2_ffn_router_weight"].T
    d["f2_bias"] = every_partition(i["L2_ffn_e_score_bias"])
    for w in ("gate", "up", "down"):
        d[f"f2_shared_{w}"] = i[f"L2_ffn_shared_{w}_w"].T

    wq, wk, wv = (i["L3_attn_w_qkv"][:, j * 1024:(j + 1) * 1024] for j in range(3))
    d["a3_w_q"], d["a3_w_k"] = wq.reshape(P, 8, P), wk.reshape(P, 8, P)
    d["a3_w_vT"] = row_chunks(wv.T)
    d["a3_w_out"] = row_chunks(i["L3_attn_w_out"])
    d["a3_temp"] = np.repeat(i["L3_attn_temperature"].reshape(8, 2).T, 64, axis=0)
    d["a3_gamma"] = every_partition(i["L3_attn_gamma"])
    d["f3_number"] = np.concatenate([np.tile(np.arange(P), (P, 1)), np.arange(P)[:, None]], 1).astype(np.float32)
    d["f3_gateT"] = i["L3_ffn_gate_w"].T
    for w in ("gate", "up"):
        d[f"f3_shared_{w}"] = i[f"L3_ffn_sh_{w}_w"].T.reshape(P, 2, P)
    d["f3_shared_down"] = row_chunks(i["L3_ffn_sh_down_w"].T)
    d["f3_gate"], d["f3_up"] = i["L3_ffn_gw"].transpose(0, 2, 1), i["L3_ffn_up_w"].transpose(0, 2, 1)
    d["f3_down"] = i["L3_ffn_down_w"].transpose(0, 2, 1).reshape(16, 4, P, P).transpose(0, 2, 1, 3).reshape(16, P, 512)
    d["f3_bias"] = np.concatenate([i["L3_ffn_gb"].reshape(16, 4, P), i["L3_ffn_up_b"].reshape(16, 4, P)], 1)\
        .transpose(0, 2, 1)
    d["f3_down_b"] = i["L3_ffn_down_b"]
    return d


def kernel(**inputs):
    import concourse.bacc as _bacc
    from concourse.bass_utils import run_bass_kernel_spmd as _run

    arrays = {f"in_{n}": np.ascontiguousarray(a) for n, a in
              layouts({n: np.asarray(a) for n, a in inputs.items()}).items()}
    nc = _bacc.Bacc("TRN2", target_bir_lowering=False, num_devices=1)
    dram = {n[3:]: nc.dram_tensor(n, a.shape, mybir.dt.from_np(a.dtype), kind="ExternalInput").ap()
            for n, a in arrays.items()}
    out = nc.dram_tensor("out", (TOKENS, D), F32, kind="ExternalOutput").ap()
    gated_mixers_kernel(nc, dram, out)
    r = _run(nc, [arrays], core_ids=[0])
    return r.results[0]["out"].reshape(BATCH, SEQ, D)
```

```python
from contextlib import ExitStack

import concourse.bass as bass
import numpy as np
from concourse import mybir

F32 = mybir.dt.float32
BF16 = mybir.dt.bfloat16
I32 = mybir.dt.int32
U32 = mybir.dt.uint32
ALU = mybir.AluOpType
ACT = mybir.ActivationFunctionType
AX = mybir.AxisListType

P = 128
BATCH, SEQ, D = 16, 256, 128
TOKENS = BATCH * SEQ
TILES = TOKENS // P
QT = SEQ // P
COLS = 512
BLOCKS = TOKENS // COLS
TPB = COLS // P
LN_EPS = 1e-5
BIG_NEG = -1e30


def software_pipeline(fori, steps, n):
    lags = [lag for _, lag in steps]
    first, last = max(lags) + (max(lags) > 0), n + min(lags)
    last -= (last - first) % 2

    def turn(t, parity):
        for fn, lag in steps:
            if not isinstance(t, int) or 0 <= t - lag < n:
                fn(t - lag, (parity - lag) % 2)

    if last - first < 4:
        first = last = 0
    for t in range(first):
        turn(t, t % 2)
    if last > first:
        with fori(0, (last - first) // 2) as r:
            for k in range(2):
                turn(r * 2 + (first + k), (first + k) % 2)
    for t in range(last, n + max(lags)):
        turn(t, t % 2)


def scope(nc):
    ctx = ExitStack()
    sems = []

    def clear():
        nc.clear_and_free_semaphores(sems)
        nc.all_engine_barrier()

    ctx.callback(clear)

    def sb(name, shape, dt=F32):
        return ctx.enter_context(nc.sbuf_tensor(name, shape, dt))

    def pb(name, shape, dt=F32):
        return ctx.enter_context(nc.psum_tensor(name, shape, dt))

    def sem(name):
        sems.append(nc.alloc_semaphore(name))
        return sems[-1]

    return ctx, sb, pb, sem


def constants_stage(nc, on, dram):
    ctx, sb, pb, sem = scope(nc)
    with ctx:
        filled, shaped, loaded = sem("c_filled"), sem("c_shaped"), sem("c_loaded")
        block = ctx.enter_context(nc.Block())

        @block.sync
        def _(sp):
            sp.dma_start(on.x[:, :, :], dram["x"].rearrange("(t p) d -> p t d", p=P)).then_inc(loaded, 16)
            sp.wait_ge(loaded, 16)

        @block.gpsimd
        def _(pool):
            nc.gpsimd.memset(on.ident[:, :], 0.0)
            nc.gpsimd.memset(on.ident_bf[:, :], 0.0)
            nc.gpsimd.memset(on.ones[:, :], 1.0)
            nc.gpsimd.memset(on.causal[:, :], 1.0)
            nc.gpsimd.memset(on.mask_kq[:, :], 0.0)
            nc.gpsimd.memset(on.mask_qk[:, :], 0.0).then_inc(filled, 1)
            pool.wait_ge(filled, 1)
            for m in (on.ident, on.ident_bf):
                nc.gpsimd.affine_select(out=m[:, :], in_=m[:, :], compare_op=ALU.not_equal, fill=1.0, base=0,
                                        pattern=[[-1, P]], channel_multiplier=1)
            nc.gpsimd.affine_select(out=on.causal[:, :], in_=on.causal[:, :], compare_op=ALU.is_ge, fill=0.0, base=0,
                                    pattern=[[1, P]], channel_multiplier=-1)
            nc.gpsimd.affine_select(out=on.mask_kq[:, :], in_=on.mask_kq[:, :], compare_op=ALU.is_ge,
                                    fill=BIG_NEG, base=0, pattern=[[1, P]], channel_multiplier=-1)
            nc.gpsimd.affine_select(out=on.mask_qk[:, :], in_=on.mask_qk[:, :], compare_op=ALU.is_ge,
                                    fill=BIG_NEG, base=0, pattern=[[-1, P]], channel_multiplier=1)\
                .then_inc(shaped, 1)
            pool.wait_ge(shaped, 1)


def layernorm_stage(nc, on, name, src, dst, dst_t, gated):
    ctx, sb, pb, sem = scope(nc)
    with ctx:
        stats = sb(f"{name}_stats", [P, TILES, 6])
        mean_var = sb(f"{name}_mv", [P, TILES, 2])
        rstd = sb(f"{name}_rstd", [P, TILES])
        std = sb(f"{name}_std", [P, TILES])
        turned = [pb(f"{name}_turned{k}", [P, COLS]) for k in range(2)]
        s_gate, s_prod, s_added = (sem(f"{name}_{w}") for w in ("silu", "prod", "added"))
        s_stats, s_aggr, s_eps, s_std, s_rstd = (sem(f"{name}_{w}") for w in ("stats", "aggr", "eps", "std", "rstd"))
        s_norm, s_turned, s_turned_free = (sem(f"{name}_{w}") for w in ("norm", "turned", "turnedfree"))
        block = ctx.enter_context(nc.Block())

        def block_of(t, i):
            return t[:, i * TPB:(i + 1) * TPB, :].rearrange("p t d -> p (t d)")

        @block.scalar
        def _(act):
            act.sem_inc(s_turned_free, 2)
            if gated:
                for i in range(BLOCKS):
                    nc.scalar.activation(block_of(on.g, i), block_of(on.g, i), ACT.Silu).then_inc(s_gate, 1)
            act.wait_ge(s_eps, 1)
            nc.scalar.activation(std[:, :], rstd[:, :], ACT.Sqrt).then_inc(s_std, 1)

            def copy_out(i, k):
                act.wait_ge(s_turned, i + 1)
                nc.scalar.activation(dst_t[:, bass.ts(i, COLS)], turned[k][:, :], ACT.Copy).then_inc(s_turned_free, 1)

            if dst_t is not None:
                software_pipeline(nc.scalar.Fori, [(copy_out, 0)], BLOCKS)

        @block.gpsimd
        def _(pool):
            for i in range(BLOCKS if gated else 0):
                pool.wait_ge(s_prod, i + 1)
                nc.gpsimd.tensor_tensor(block_of(on.x, i), block_of(on.x, i), block_of(on.g, i), ALU.add)\
                    .then_inc(s_added, 1)

        @block.vector
        def _(dve):
            for i in range(BLOCKS + 2):
                if gated and i < BLOCKS:
                    dve.wait_ge(s_gate, i + 1)
                    nc.vector.tensor_tensor(block_of(on.g, i), block_of(on.g, i), block_of(on.s, i), ALU.mult)\
                        .then_inc(s_prod, 1)
                if i >= 2:
                    if gated:
                        dve.wait_ge(s_added, i - 1)
                    for t in range((i - 2) * TPB, (i - 1) * TPB):
                        nc.vector.bn_stats(stats[:, t, :], src[:, t, :]).then_inc(s_stats, 1)
            dve.wait_ge(s_stats, TILES)
            for t in range(TILES):
                nc.vector.bn_aggr(mean_var[:, t, :], stats[:, t, :]).then_inc(s_aggr, 1)
            dve.wait_ge(s_aggr, TILES)
            nc.vector.tensor_scalar(rstd[:, :], mean_var[:, :, 1], LN_EPS, None, ALU.add).then_inc(s_eps, 1)
            dve.wait_ge(s_std, 1)
            nc.vector.reciprocal(rstd[:, :], std[:, :]).then_inc(s_rstd, 1)
            dve.wait_ge(s_rstd, 1)
            for t in range(TILES):
                nc.vector.tensor_scalar(dst[:, t, :], src[:, t, :], mean_var[:, t, 0:1], rstd[:, t:t + 1],
                                        ALU.subtract, ALU.mult).then_inc(s_norm, 1)

        @block.tensor
        def _(pe):
            for i in range(BLOCKS if dst_t is not None else 0):
                pe.wait_ge(s_norm, (i + 1) * TPB)
                pe.wait_ge(s_turned_free, i + 1)
                for t in range(TPB):
                    ins = nc.tensor.transpose(turned[i % 2][:, t * P:(t + 1) * P], dst[:, i * TPB + t, :],
                                              on.ident[:, :])
                ins.then_inc(s_turned, 1)


def ffn_stage(nc, on, name, chunks, w_sb):
    ctx, sb, pb, sem = scope(nc)
    with ctx:
        h = [[sb(f"{name}_h{k}_{c}", [P, COLS]) for c in range(chunks)] for k in range(2)]
        silu = [sb(f"{name}_silu{k}", [P, COLS]) for k in range(2)]
        gate_ps = [pb(f"{name}_gate{k}", [P, COLS]) for k in range(2)]
        up_ps = [pb(f"{name}_up{k}", [P, COLS]) for k in range(2)]
        down_ps = [pb(f"{name}_down{k}", [P, TPB, P]) for k in range(2)]
        s_proj, s_gate_free, s_up_free, s_down, s_down_free = (
            sem(f"{name}_{w}") for w in ("proj", "gatefree", "upfree", "down", "downfree"))
        block = ctx.enter_context(nc.Block())

        def unit(i, k, c):
            return i * chunks + c, (k * chunks + c) % 2

        @block.tensor
        def _(pe):
            pe.sem_inc(s_down, 2)

            def project(i, k):
                cols = on.xnT[:, bass.ts(i, COLS)]
                for c in range(chunks):
                    n, b = unit(i, k, c)
                    pe.wait_ge(s_gate_free, n + 1)
                    nc.tensor.matmul(gate_ps[b][:, :], w_sb["gate"][:, c, :], cols, start=True, stop=True)
                    pe.wait_ge(s_up_free, n + 1)
                    nc.tensor.matmul(up_ps[b][:, :], w_sb["up"][:, c, :], cols, start=True, stop=True)\
                        .then_inc(s_proj, 1)

            def down(i, k):
                pe.wait_ge(s_up_free, i * chunks + (chunks + 2))
                pe.wait_ge(s_down_free, i + 1)
                for t in range(TPB):
                    for c in range(chunks):
                        ins = nc.tensor.matmul(down_ps[k][:, t, :], h[k][c][:, t * P:(t + 1) * P],
                                               w_sb["down"][:, c, :], start=(c == 0), stop=(c == chunks - 1))
                ins.then_inc(s_down, 1)

            software_pipeline(nc.tensor.Fori, [(project, 0), (down, 1)], BLOCKS)

        @block.scalar
        def _(act):
            act.sem_inc(s_gate_free, 2)

            def silus(i, k):
                for c in range(chunks):
                    n, b = unit(i, k, c)
                    act.wait_ge(s_proj, n + 1)
                    act.wait_ge(s_up_free, n + 1)
                    nc.scalar.activation(silu[b][:, :], gate_ps[b][:, :], ACT.Silu).then_inc(s_gate_free, 1)

            software_pipeline(nc.scalar.Fori, [(silus, 0)], BLOCKS)

        @block.vector
        def _(dve):
            dve.sem_inc(s_up_free, 2)
            dve.sem_inc(s_down_free, 2)

            def hidden(i, k):
                dve.wait_ge(s_down, i + 1)
                for c in range(chunks):
                    n, b = unit(i, k, c)
                    dve.wait_ge(s_gate_free, n + 3)
                    nc.vector.tensor_tensor(h[k][c][:, :], up_ps[b][:, :], silu[b][:, :], ALU.mult)\
                        .then_inc(s_up_free, 1)

            def take(i, k):
                dve.wait_ge(s_down, i + 3)
                nc.vector.tensor_copy(on.g[:, bass.ts(i, TPB), :], down_ps[k][:, :, :]).then_inc(s_down_free, 1)

            software_pipeline(nc.vector.Fori, [(hidden, 0), (take, 1)], BLOCKS)


def upto(value, limit):
    return min(value, limit) if isinstance(value, int) else value


def project_stage(nc, on, name, dram, heads, finish):
    hd = D // heads
    GROUPS = TILES // 2
    ctx, sb, pb, sem = scope(nc)
    with ctx:
        w = dram["w_sb"] if finish == "latent" else sb(f"{name}_w", [P, 3 * D])
        prod = [pb(f"{name}_prod{k}", [P, 2, COLS // D, D]) for k in range(2)]
        loaded, s_prod, s_taken, s_chain, s_act = (
            sem(f"{name}_{n}") for n in ("loaded", "prod", "taken", "chain", "act"))
        loads = [] if finish == "latent" else [(w[:, :], dram["w"])]
        if finish == "latent":
            pass
        elif finish == "softplus":
            bias = sb(f"{name}_bias", [P, 3, D])
            loads.append((bias[:, :, :], dram["bias"]))
            terms = [sb(f"{name}_terms{j}", [P, TILES, D]) for j in range(2)]
        else:
            cos_sin = sb(f"{name}_cos_sin", [P, 2, QT, hd])
            gamma_beta = sb(f"{name}_gamma_beta", [P, 2, 2, hd])
            loads += [(cos_sin[:, :, :, :], dram["cos_sin"]), (gamma_beta[:, :, :, :], dram["gamma_beta"])]
            mean_w = sb(f"{name}_mean_w", [P, 2 * heads])
            var, square, turned = ([sb(f"{name}_{n}{j}", [P, TILES, w]) for j in range(2)] for n, w in (
                ("var", heads), ("square", D), ("turned", D)))
            rot_gb = sb(f"{name}_rot_gb", [P, 2, 2, hd])
            tables = sb(f"{name}_tables", [P, 2, 3, QT, hd])
            beta_cos = sb(f"{name}_beta_cos", [P, 2, QT, hd])
            s_centred, s_tables, s_square = (sem(f"{name}_{n}") for n in ("centred", "tables", "square"))
        block = ctx.enter_context(nc.Block())

        @block.sync
        def _(sp):
            for dst, src in loads:
                sp.dma_start(dst, src).then_inc(loaded, 16)

        @block.tensor
        def _(pe):
            pe.wait_ge(loaded, 16 * len(loads))
            if finish == "rope":
                pe.wait_ge(s_centred, 3)

            for i in range(GROUPS):
                if i >= 2:
                    pe.wait_ge(s_taken, i - 1)
                for t in range(2):
                    tile = 2 * i + t
                    ins = nc.tensor.matmul(prod[i % 2][:, t, 0:3, :].rearrange("p j d -> p (j d)"),
                                           on.xnT[:, tile * P:(tile + 1) * P], w[:, :], start=True, stop=True)
                ins.then_inc(s_prod, 1)

        @block.vector
        def _(dve):
            dve.wait_ge(loaded, 16 * len(loads))
            if finish == "rope":
                w_heads = w[:, 0:2 * D].rearrange("p (h d) -> p h d", d=hd)
                nc.vector.tensor_reduce(mean_w[:, :], w_heads, AX.X, ALU.add).then_inc(s_centred, 1)
                dve.wait_ge(s_centred, 1)
                nc.vector.tensor_scalar(mean_w[:, :], mean_w[:, :], 1.0 / hd, None, ALU.mult).then_inc(s_centred, 1)
                dve.wait_ge(s_centred, 2)
                nc.vector.tensor_tensor(w_heads, w_heads, mean_w[:, :].unsqueeze(2).broadcast_to([P, 2 * heads, hd]),
                                        ALU.subtract).then_inc(s_centred, 1)
                half = hd // 2
                nc.vector.tensor_scalar(rot_gb[:, :, :, 0:half], gamma_beta[:, :, :, 1:hd:2], -1.0, None, ALU.mult)
                nc.vector.tensor_copy(rot_gb[:, :, :, half:hd], gamma_beta[:, :, :, 0:hd:2]).then_inc(s_tables, 1)
                dve.wait_ge(s_tables, 1)
                for j in range(2):
                    for out, gb, row, trig in ((tables[:, j, 0], gamma_beta, 0, 0), (tables[:, j, 1], rot_gb, 0, 1),
                                               (beta_cos[:, j], gamma_beta, 1, 0), (tables[:, j, 2], rot_gb, 1, 1)):
                        ins = nc.vector.tensor_tensor(out, cos_sin[:, trig, :, :],
                                                      gb[:, row, j, :].unsqueeze(1).broadcast_to([P, QT, hd]), ALU.mult)
                ins.then_inc(s_tables, 1)
                dve.wait_ge(s_tables, 2)
                nc.vector.tensor_tensor(tables[:, :, 2], tables[:, :, 2], beta_cos[:, :, :, :], ALU.add)\
                    .then_inc(s_tables, 1)

            def take(i, k):
                dve.wait_ge(s_prod, i + 1)
                tiles = bass.ds(i * 2, 2)
                if finish == "latent":
                    nc.vector.tensor_copy(on.q2[:, tiles, :], prod[k][:, :, 0:2, :].rearrange("p t j d -> p t (j d)"))
                    ins = nc.vector.tensor_copy(on.kv[:, tiles, :], prod[k][:, :, 2, :])
                else:
                    for j, dst in enumerate((on.q, on.k, on.v)):
                        if finish == "softplus":
                            ins = nc.vector.tensor_tensor(dst[:, tiles, :], prod[k][:, :, j, :],
                                                          bias[:, j:j + 1, :].broadcast_to([P, 2, D]), ALU.add)
                        else:
                            ins = nc.vector.tensor_copy(dst[:, tiles, :], prod[k][:, :, j, :])
                ins.then_inc(s_taken, 1)

            software_pipeline(nc.vector.Fori, [(take, 0)], GROUPS)
            done = [0]

            def link(ins):
                done[0] += 1
                ins.then_inc(s_chain, 1)
                dve.wait_ge(s_chain, done[0])

            dve.wait_ge(s_taken, GROUPS)
            if finish == "latent":
                return
            if finish == "softplus":
                for j, z in enumerate((on.q, on.k)):
                    dve.wait_ge(s_act, 5 + j)
                    nc.vector.scalar_tensor_tensor(z[:, :, :], z[:, :, :], 0.0, terms[j][:, :, :], ALU.max, ALU.add)\
                        .then_inc(s_chain, 1)
                dve.wait_ge(s_chain, 2)
                return
            flats = [z[:, :, :].rearrange("p t (h d) -> p (t h) d", d=hd) for z in (on.q, on.k)]

            def with_table(j, n, out, src, cols, op):
                for t in range(QT):
                    table = tables[:, j, n, t, cols].unsqueeze(1).unsqueeze(1)
                    table = table.broadcast_to([P, TILES // QT, heads, cols.stop - cols.start])
                    ins = nc.vector.tensor_tensor(out[:, t:TILES:QT], src[:, t:TILES:QT], table, op)
                return ins

            def heads_of(z):
                return z[:, :, :].rearrange("p t (h d) -> p t h d", d=hd)

            dve.wait_ge(s_tables, 3)
            for j, z in enumerate((on.q, on.k)):
                src, out = heads_of(z), heads_of(turned[j])
                with_table(j, 1, out[:, :, :, 0:half], src[:, :, :, 1:hd:2], slice(0, half), ALU.mult)
                ins = with_table(j, 1, out[:, :, :, half:hd], src[:, :, :, 0:hd:2], slice(half, hd), ALU.mult)
            link(ins)
            for j, z in enumerate((on.q, on.k)):
                dve.wait_ge(s_square, j + 1)
                v = var[j][:, :, :].rearrange("p t h -> p (t h)")
                link(nc.vector.tensor_reduce(v, square[j][:, :, :].rearrange("p t (h d) -> p (t h) d", d=hd), AX.X,
                                             ALU.add))
                link(nc.vector.tensor_scalar(v, v, 1.0 / hd, LN_EPS, ALU.mult, ALU.add))
            for j, z in enumerate((on.q, on.k)):
                link(with_table(j, 0, heads_of(z), heads_of(z), slice(0, hd), ALU.mult))
                link(nc.vector.tensor_tensor(z[:, :, :], z[:, :, :], turned[j][:, :, :], ALU.add))
                v = var[j][:, :, :].rearrange("p t h -> p (t h)")
                dve.wait_ge(s_act, j + 1)
                link(nc.vector.reciprocal(v, v))
                link(nc.vector.tensor_tensor(flats[j], flats[j], v.unsqueeze(2).broadcast_to([P, TILES * heads, hd]),
                                             ALU.mult))
                link(with_table(j, 2, heads_of(z), heads_of(z), slice(0, hd), ALU.add))

        @block.scalar
        def _(act):
            if finish == "softplus":
                act.wait_ge(s_taken, GROUPS)
                terms_of = ((ACT.Abs, 1.0, 0.0), (ACT.Exp, -1.0, 0.0), (ACT.Ln, 1.0, 1.0))
                for n, (func, scale, plus) in enumerate(terms_of):
                    for j, z in enumerate((on.q, on.k)):
                        if n:
                            act.wait_ge(s_act, 2 * (n - 1) + j + 1)
                        nc.scalar.activation(terms[j][:, :, :], (terms[j] if n else z)[:, :, :], func, scale=scale,
                                             bias=plus).then_inc(s_act, 1)
            elif finish == "rope":
                act.wait_ge(s_taken, GROUPS)
                for j, z in enumerate((on.q, on.k)):
                    nc.scalar.activation(square[j][:, :, :], z[:, :, :], ACT.Square).then_inc(s_square, 1)
                for j in range(2):
                    act.wait_ge(s_chain, 2 * j + 3)
                    nc.scalar.activation(var[j][:, :, :], var[j][:, :, :], ACT.Sqrt).then_inc(s_act, 1)


def latent_fold_stage(nc, name, dram, w_sb, wo_sb, heads, kvh):
    lat = 32
    ctx, sb, pb, sem = scope(nc)
    with ctx:
        wqT, wo = sb(f"{name}_wqT", [P, heads, D]), sb(f"{name}_wo", [P, heads, D])
        up = sb(f"{name}_up", [P, 2, lat])
        q_ps, o_ps = pb(f"{name}_qps", [P, heads * lat]), pb(f"{name}_ops", [P, kvh, D])
        loaded, folded, copied = (sem(f"{name}_{w}") for w in ("loaded", "folded", "copied"))
        loads = [(wqT[:, :, :], dram["wqT"]), (wo[:, :, :], dram["wo"]), (up[:, :, :], dram["up"]),
                 (w_sb[:, heads * lat:], dram["w_down"])]
        block = ctx.enter_context(nc.Block())

        @block.sync
        def _(sp):
            for dst, src in loads:
                sp.dma_start(dst, src).then_inc(loaded, 16)
            sp.wait_ge(loaded, 16 * len(loads))

        @block.tensor
        def _(pe):
            pe.wait_ge(loaded, 16 * len(loads))
            for h in range(heads):
                ins = nc.tensor.matmul(q_ps[:, h * lat:(h + 1) * lat], wqT[:, h, :], up[:, 0, :], start=True, stop=True)
            ins.then_inc(folded, 1)
            hpg = heads // kvh
            for h in range(heads):
                r = lat * (h % hpg)
                ins = nc.tensor.matmul(o_ps[r:r + lat, h // hpg, :], up[:, 1, :], wo[:, h, :], start=True, stop=True)
            ins.then_inc(folded, 1)

        @block.scalar
        def _(act):
            act.wait_ge(folded, 1)
            nc.scalar.activation(w_sb[:, 0:heads * lat], q_ps[:, :], ACT.Copy).then_inc(copied, 1)
            act.wait_ge(folded, 2)
            nc.scalar.activation(wo_sb[:, :, :], o_ps[:, :, :], ACT.Copy).then_inc(copied, 1)
            act.wait_ge(copied, 2)


def latent_attention(nc, on, name, dram, heads, kvh):
    with nc.sbuf_tensor(f"{name}_q2", [P, TILES, heads * 32], F32) as q2, \
            nc.sbuf_tensor(f"{name}_w", [P, 3 * D], F32) as w_sb, \
            nc.sbuf_tensor(f"{name}_wo_sb", [P, kvh, D], F32) as wo_sb:
        on.q2, on.kv = q2, on.v
        latent_fold_stage(nc, f"{name}f", dram, w_sb, wo_sb, heads, kvh)
        project_stage(nc, on, f"{name}p", {"w_sb": w_sb}, heads, "latent")
        attention_stage(nc, on, f"{name}a", {**dram, "wo_sb": wo_sb}, heads, float(D) ** -0.5, kvh)


def attention_stage(nc, on, name, dram, heads, softmax_scale, kv_heads=None):
    latent = kv_heads is not None
    hd = 32 if latent else D // heads
    kvh = kv_heads or heads
    SLOT = 64
    CW = 3 * P
    HALF = heads // 2
    QB = 12 if latent else 8
    KB = 4 if latent else 8
    STRIPS = 3 if latent else 4
    OB = heads * hd // P
    softmax = softmax_scale is not None
    FILL = 1
    TOP = FILL + 1
    LAG = FILL + (2 if softmax else 1)
    ROUNDS = heads // 2
    FILLS = ((0, 0), (0, 4), (0, 8), (1, 0)) if latent else ((0, 0), (1, 0), (0, 4), (1, 4))
    ctx, sb, pb, sem = scope(nc)
    with ctx:
        wo = dram["wo_sb"] if latent else sb(f"{name}_wo", [P, 1, D])
        bo = None if latent else sb(f"{name}_bo", [P, D])
        sel = sb(f"{name}_sel", [P, heads, P], BF16) if softmax else None
        widths = (heads * hd, kvh * hd)
        parts = [sb(f"{name}_parts{j}", [P, 3, QT, w], BF16) for j, w in enumerate(widths)]
        rest = [sb(f"{name}_rest{j}", [P, QT, w]) for j, w in enumerate(widths)]
        stack = [[sb(f"{name}_stack{k}{j}", [P, QT, n, P], BF16) for j, n in enumerate((QB, KB))]
                 for k in range(2)]
        opT = [[sb(f"{name}_opT{k}{j}", [P, n, SEQ], BF16) for j, n in enumerate((QB, KB))] for k in range(2)]
        v1 = [sb(f"{name}_v1{k}", [P, QT, kvh, 32]) for k in range(2)]
        probs = [sb(f"{name}_probs{k}", [P, heads, CW]) for k in range(2)]
        den_cols = sb(f"{name}_dencols", [P, kvh, 32]) if latent else None
        pv_sb = sb(f"{name}_pvsb", [P, 4, SEQ])
        rden = sb(f"{name}_rden", [P, heads])
        o_sb = sb(f"{name}_o", [P, QT, heads, hd])
        oT = sb(f"{name}_oT", [P, QT, OB, P])
        score_ps = [pb(f"{name}_score{k}", [P, COLS]) for k in range(2)]
        top_ps = [pb(f"{name}_top{k}", [P, COLS]) for k in range(2)] if softmax else None
        pv_ps = [pb(f"{name}_pv{k}", [P, 2, SEQ]) for k in range(2)]
        opT_ps = pb(f"{name}_opTp", [P, 4, SEQ], BF16)
        desk = pb(f"{name}_desk", [P, 4, D])
        out_ps = desk[:, 0:QT, :]
        if softmax:
            tops = sb(f"{name}_tops", [P, QT, heads])
            ntop = sb(f"{name}_ntop", [P, QT, P], BF16)
            ntopT = [sb(f"{name}_ntopT{k}", [P, SEQ], BF16) for k in range(2)]
            ntopT_ps = desk[:, 0, :].bitcast(BF16)
        else:
            causal3 = sb(f"{name}_causal3", [P, CW])
        S = {w: sem(f"{name}_{w}") for w in (
            "w", "init", "sel", "part1", "rest1", "part2", "part3", "stack0", "stack1", "v1", "turned", "opT", "top",
            "topout", "neg", "ntop", "ntopTp", "ntopT", "score", "probs", "pv", "pvout", "tokmaj", "rden",
            "o", "oturned", "oT", "out", "s")}
        block = ctx.enter_context(nc.Block())
        loads = [] if latent else [(wo[:, 0, :], dram["wo"]), (bo[:, :], dram["bo"])]
        if latent:
            loads.append((den_cols[:, :, :], dram["den_cols"]))

        @block.sync
        def _(sp):
            for dst, src in loads:
                sp.dma_start(dst, src).then_inc(S["w"], 16)

        def q_of(t):
            return on.q2[:, t, :] if latent else on.q[:, t, :]

        def k_of(t):
            return on.kv[:, t, 0:kvh * hd] if latent else on.k[:, t, :]

        def slots(k, j, lo, n):
            a = stack[k][j][:, :, :, :].rearrange("p t b (h s) -> p (t b h) s", s=SLOT)
            return a[:, :, lo * hd:(lo + n) * hd].rearrange("p g (n d) -> p g n d", d=hd)

        def wide_slots(k, j, t, lo, n):
            hs = (heads, kvh)[j]
            if lo < 4:
                return stack[k][j][:, t, 0:hs, lo * hd:(lo + n) * hd].rearrange("p h (n d) -> p h n d", d=hd)
            a = stack[k][j][:, t, hs:, :].rearrange("p b (h s) -> p (b h) s", s=2 * hd)
            return a[:, :, (lo - 4) * hd:(lo - 4 + n) * hd].rearrange("p g (n d) -> p g n d", d=hd)

        def part(m, j, n):
            a = parts[j][:, m, :, :].rearrange("p t (h d) -> p (t h) d", d=hd).unsqueeze(2)
            return a.broadcast_to([P, QT * heads, n, hd])

        def wide_part(m, j, t, n, twice=False):
            hs = (heads, kvh)[j]
            a = parts[j][:, m, t, :].rearrange("p (h d) -> p h d", d=hd).unsqueeze(2)
            return a.broadcast_to([P, hs, 2 if twice else n, hd])

        def step(fn, *args):
            return lambda i, k: fn(*args, i, k)

        def two_heads(r):
            return range(2 * r, 2 * r + 2)

        def by_head(bank):
            return bank[:, :, :].rearrange("p s (j r) -> p (s j) r", r=32)

        @block.gpsimd
        def _(pool):
            for k in range(2):
                if not latent:
                    for j in range(2):
                        heads_of = stack[k][j][:, :, :, :].rearrange("p t b (h s) -> p (t b h) s", s=SLOT)
                        nc.gpsimd.memset(heads_of[:, :, 6 * hd:], 0.0)
                if not latent:
                    nc.gpsimd.memset(v1[k][:, :, :, hd + 1:], 0.0)
                    ins = nc.gpsimd.memset(v1[k][:, :, :, hd:hd + 1], 1.0)
            if softmax:
                nc.gpsimd.memset(sel[:, :, :], 0.0)
                ins = nc.gpsimd.memset(ntop[:, :, :], 0.0)
            ins.then_inc(S["init"], 1)
            pool.wait_ge(S["init"], 1)
            if softmax:
                nc.gpsimd.affine_select(out=sel[:, :, :], in_=sel[:, :, :], compare_op=ALU.not_equal, fill=1.0,
                                        base=0, pattern=[[-1, heads], [0, P]], channel_multiplier=1)\
                    .then_inc(S["sel"], 1)
                pool.wait_ge(S["sel"], 1)
                nc.gpsimd.affine_select(out=sel[:, :, :], in_=sel[:, :, :], compare_op=ALU.not_equal, fill=1.0,
                                        base=-heads, pattern=[[-1, heads], [0, P]], channel_multiplier=1)\
                    .then_inc(S["sel"], 1)

            def values_in(i, k):
                pool.wait_ge(S["pv"], i * 2)
                t = bass.ds(i * QT, QT)
                v = on.kv[:, t, kvh * hd:] if latent else on.v[:, t, :]
                nc.gpsimd.tensor_copy(v1[k][:, :, :, 0:hd], v.rearrange("p t (h d) -> p t h d", d=hd))\
                    .then_inc(S["v1"], 1)

            def stack_q(i, k):
                pool.wait_ge(S["part3"], i + 1)
                pool.wait_ge(S["turned"], i * 4 + 3)
                if latent:
                    for t in range(QT):
                        q = on.q2[:, bass.ds(i * QT + t, 1), :].rearrange("p t (h d) -> p (t h) d", d=hd)
                        nc.gpsimd.tensor_copy(wide_slots(k, 0, t, 0, 3),
                                              q.unsqueeze(2).broadcast_to([P, heads, 3, hd]))
                        for m, lo, n in ((1, 3, 1), (1, 4, 1), (2, 5, 1)):
                            ins = nc.gpsimd.tensor_copy(wide_slots(k, 0, t, lo, n), wide_part(m, 0, t, n))
                    ins.then_inc(S["stack0"], 1)
                    return
                q = on.q[:, bass.ds(i * QT, QT), :].rearrange("p t (h d) -> p (t h) d", d=hd).unsqueeze(2)
                nc.gpsimd.tensor_copy(slots(k, 0, 0, 3), q.broadcast_to([P, QT * heads, 3, hd]))
                for m, lo, n in ((1, 3, 2), (2, 5, 1)):
                    ins = nc.gpsimd.tensor_copy(slots(k, 0, lo, n), part(m, 0, n))
                ins.then_inc(S["stack0"], 1)

            software_pipeline(nc.gpsimd.Fori, [(values_in, LAG), (stack_q, 0)], BATCH)

        @block.vector
        def _(dve):
            dve.sem_inc(S["topout" if softmax else "probs"], 2)
            dve.wait_ge(S["w"], 16 * len(loads))
            dve.wait_ge(S["init"], 1)
            if not softmax:
                nc.vector.memset(causal3[:, P:2 * P], 1.0)
                nc.vector.tensor_copy(causal3[:, 0:P], on.causal[:, :])
                nc.vector.tensor_copy(causal3[:, 2 * P:], on.causal[:, :]).then_inc(S["neg"], 1)
                dve.wait_ge(S["neg"], 1)

            def split(stage, i, k):
                t = bass.ds(i * QT, QT)
                src = (q_of(t), k_of(t))
                if stage == 0:
                    dve.wait_ge(S["stack0"], i)
                    dve.wait_ge(S["stack1"], i)
                    for j in range(2):
                        ins = nc.vector.tensor_copy(parts[j][:, 0, :, :], src[j])
                    ins.then_inc(S["part1"], 1)
                elif stage == 1:
                    dve.wait_ge(S["part1"], i + 1)
                    for j in range(2):
                        ins = nc.vector.tensor_tensor(rest[j][:, :, :], src[j], parts[j][:, 0, :, :], ALU.subtract)
                    ins.then_inc(S["rest1"], 1)
                elif stage == 2:
                    dve.wait_ge(S["rest1"], i + 1)
                    for j in range(2):
                        ins = nc.vector.tensor_copy(parts[j][:, 1, :, :], rest[j][:, :, :])
                    ins.then_inc(S["part2"], 1)
                elif stage == 3:
                    dve.wait_ge(S["part2"], i + 1)
                    for j in range(2):
                        ins = nc.vector.tensor_tensor(parts[j][:, 2, :, :], rest[j][:, :, :], parts[j][:, 1, :, :],
                                                      ALU.subtract)
                    ins.then_inc(S["part3"], 1)
                else:
                    dve.wait_ge(S["part3"], i + 1)
                    dve.wait_ge(S["turned"], i * 4 + 4)
                    stack_k(i, k)

            def stack_k(i, k):
                if latent:
                    for t in range(QT):
                        for m, lo in ((0, 0), (1, 1), (2, 2), (0, 3)):
                            nc.vector.tensor_copy(wide_slots(k, 1, t, lo, 1), wide_part(m, 1, t, 1))
                        for m, lo in ((1, 4), (0, 5)):
                            out = stack[k][1][:, t, kvh:, :].rearrange("p b (e s) -> p b e s", s=2 * hd)
                            ins = nc.vector.tensor_copy(out[:, :, :, (lo - 4) * hd:(lo - 3) * hd],
                                                        wide_part(m, 1, t, 1, twice=True))
                    ins.then_inc(S["stack1"], 1)
                    return
                for m, lo in ((0, 0), (1, 1), (2, 2), (0, 3), (1, 4), (0, 5)):
                    ins = nc.vector.tensor_copy(slots(k, 1, lo, 1), part(m, 1, 1))
                ins.then_inc(S["stack1"], 1)

            def top(r, i, k):
                for h in two_heads(r):
                    dve.wait_ge(S["top"], i * heads + h + 1)
                    nc.vector.reduce_max(tops[:, 0, h:h + 1], top_ps[h % 2][:, 0:P], AX.X)
                    nc.vector.reduce_max(tops[:, 1, h:h + 1], top_ps[h % 2][:, P:CW], AX.X).then_inc(S["topout"], 1)

            def negate_tops(i, k):
                dve.wait_ge(S["topout"], (i + 1) * heads + 2)
                dve.wait_ge(S["ntopTp"], i)
                nc.vector.tensor_scalar(ntop[:, :, 0:heads], tops[:, :, :], -1.0, None, ALU.mult).then_inc(S["neg"], 1)
                dve.wait_ge(S["neg"], i + 1)
                nc.vector.scalar_tensor_tensor(ntop[:, :, heads:2 * heads], tops[:, :, :], -1.0, ntop[:, :, 0:heads],
                                               ALU.mult, ALU.subtract).then_inc(S["ntop"], 1)
                dve.wait_ge(S["ntop"], i + 1)

            def masked(r, i, k):
                for h in two_heads(r):
                    dve.wait_ge(S["score"], i * heads + h + 1)
                    nc.vector.tensor_tensor(probs[k][:, h, :], score_ps[h % 2][:, 0:CW], causal3[:, :], ALU.mult)\
                        .then_inc(S["probs"], 1)

            def normalise(t):
                def fn(i, k):
                    n = i * QT + t
                    dve.wait_ge(S["tokmaj"], n + 1)
                    if latent:
                        den = desk[:, 2, :].rearrange("p (j r) -> p r j", r=32)[:, 0:kvh, :]
                        sums = desk[:, 0:2, :].rearrange("p g (j d) -> p (g j) d", d=hd)
                        nc.vector.reciprocal(rden[:, :].rearrange("p (g j) -> p g j", g=kvh), den)\
                            .then_inc(S["rden"], 1)
                    else:
                        sums = by_head(desk)[:, :, 0:hd]
                        nc.vector.reciprocal(rden[:, :], by_head(desk)[:, :, hd]).then_inc(S["rden"], 1)
                    dve.wait_ge(S["rden"], n + 1)
                    nc.vector.tensor_tensor(o_sb[:, t, :, :], sums,
                                            rden[:, :].unsqueeze(2).broadcast_to([P, heads, hd]), ALU.mult)\
                        .then_inc(S["o"], 1)
                    dve.wait_ge(S["o"], n + 1)
                return fn

            def store(i, k):
                dve.wait_ge(S["out"], i + 1)
                if latent:
                    nc.vector.tensor_copy(on.s[:, bass.ds(i * QT, QT), :], out_ps).then_inc(S["s"], 1)
                    return
                nc.vector.tensor_tensor(on.s[:, bass.ds(i * QT, QT), :], out_ps,
                                        bo[:, :].unsqueeze(1).broadcast_to([P, QT, D]), ALU.add).then_inc(S["s"], 1)

            steps = []
            for r in range(ROUNDS):
                if r < 4:
                    steps.append((step(split, r), 0))
                if r == 4 or ROUNDS == 4 and r == 3:
                    steps.append((step(split, 4), 0))
                steps.append((step(top, r), TOP) if softmax else (step(masked, r), LAG))
                if r == ROUNDS // 4:
                    steps.append((normalise(0), LAG + 2))
                elif r == ROUNDS // 2:
                    steps.append((normalise(1), LAG + 2))
            steps += [(negate_tops, TOP)] * softmax + [(store, LAG + 2)]
            software_pipeline(nc.vector.Fori, steps, BATCH)

        @block.tensor
        def _(pe):
            pe.sem_inc(S["turned"], 8)
            pe.sem_inc(S["pv"], 2)
            pe.wait_ge(S["w"], 16 * len(loads))
            if softmax:
                pe.wait_ge(S["sel"], 2)

            def turn(n, i, k):
                j, block = FILLS[n]
                pe.wait_ge(S[f"stack{j}"], i + 1)
                pe.wait_ge(S["opT"], i * 4 + n)
                for p in range(4):
                    for t in range(QT):
                        ins = nc.tensor.transpose(opT_ps[:, p, t * P:(t + 1) * P],
                                                  stack[k][j][:, t, block + p, :], on.ident_bf[:, :])
                ins.then_inc(S["turned"], 1)

            def operands_ready(r, i):
                if r == 0:
                    pe.wait_ge(S["opT"], i * 4 + (4 if latent else 2))
                elif r == ROUNDS // 2:
                    pe.wait_ge(S["opT"], i * 4 + 4)

            def operands(k, h, q0, q1, k0, k1):
                q, key = (slice(q0 * P, q1 * P), slice(k0 * P, k1 * P))
                r = slice(SLOT * (h % 2), SLOT * (h % 2) + SLOT)
                if not latent:
                    return [(opT[k][0][r, h // 2, q], opT[k][1][r, h // 2, key])]
                g = h // (heads // kvh)
                return [(opT[k][0][:, h, q], opT[k][1][:, g, key]),
                        (opT[k][0][r, heads + h // 2, q], opT[k][1][r, kvh + g, key])]

            def tops_(r, i, k):
                operands_ready(r, i)
                for h in two_heads(r):
                    pe.wait_ge(S["topout"], i * heads + h + 1)
                    bank = top_ps[h % 2]
                    for qt, lo, hi, m0 in ((0, 0, P, 0), (1, P, CW, 2 * P)):
                        for n, (q, key) in enumerate(operands(k, h, qt, qt + 1, 0, qt + 1)):
                            nc.tensor.matmul(bank[:, lo:hi], q, key, start=(n == 0), stop=True,
                                             skip_group_check=(n > 0))
                        ins = nc.tensor.matmul(bank[:, m0:m0 + P], on.ident_bf[:, :], on.mask_qk[:, :],
                                               start=False, stop=True, skip_group_check=True)
                    ins.then_inc(S["top"], 1)

            def turn_tops(i, k):
                pe.wait_ge(S["ntop"], i + 1)
                if not isinstance(i, int) or i >= 3:
                    pe.wait_ge(S["s"], i - 2)
                for t in range(QT):
                    ins = nc.tensor.transpose(ntopT_ps[:, t * P:(t + 1) * P], ntop[:, t, :], on.ident_bf[:, :])
                ins.then_inc(S["ntopTp"], 1)

            def scores(r, i, k):
                if softmax:
                    pe.wait_ge(S["ntopT"], i + 1)
                else:
                    operands_ready(r, i)
                for h in two_heads(r):
                    pe.wait_ge(S["probs"], i * heads + h + 1)
                    bank = score_ps[h % 2]
                    for kt, lo, hi, m0 in ((0, 0, 2 * P, 0), (1, 2 * P, CW, 2 * P)):
                        for n, (q, key) in enumerate(operands(k, h, kt, QT, kt, kt + 1)):
                            ins = nc.tensor.matmul(bank[:, lo:hi], key, q, start=(n == 0), stop=True,
                                                   skip_group_check=(n > 0))
                        if softmax:
                            nc.tensor.matmul(bank[:, lo:hi], sel[:, h, :], ntopT[k][:, kt * P:], start=False,
                                             stop=True, skip_group_check=True)
                            ins = nc.tensor.matmul(bank[:, m0:m0 + P], on.ident_bf[:, :], on.mask_kq[:, :],
                                                   start=False, stop=True, skip_group_check=True)
                    ins.then_inc(S["score"], 1)

            def values(half):
                def fn(i, k):
                    if half == 0:
                        pe.wait_ge(S["v1"], i + 1)
                    pe.wait_ge(S["probs"], i * heads + ((heads if half or latent else HALF) + 2))
                    pe.wait_ge(S["pvout"], i * 2)
                    if latent and half:
                        for kt, lo in ((0, 0), (1, 2 * P)):
                            for g in range(kvh):
                                for j in range(4):
                                    ins = nc.tensor.matmul(
                                        pv_ps[1][32 * j:32 * j + 32, 0, kt * P:SEQ], den_cols[:, g, :],
                                        probs[k][:, 4 * g + j, lo:lo + (QT - kt) * P],
                                        start=(kt == 0 and g == 0), stop=True, skip_group_check=True)
                        ins.then_inc(S["pv"], 1)
                        return
                    for strip in range(2):
                        for kt, lo in ((0, 0), (1, 2 * P)):
                            for j in range(4):
                                h = (0 if latent else half * HALF) + strip * 4 + j
                                ins = nc.tensor.matmul(
                                    pv_ps[half][32 * j:32 * j + 32, strip, kt * P:SEQ],
                                    v1[k][:, kt, strip if latent else h, :],
                                    probs[k][:, h, lo:lo + (QT - kt) * P],
                                    start=(kt == 0), stop=(kt == 1), skip_group_check=True)
                    ins.then_inc(S["pv"], 1)
                return fn

            def token_major(t):
                def fn(i, k):
                    if t == 0:
                        pe.wait_ge(S["pvout"], (i + 1) * 2)
                        pe.wait_ge(S["s"], i)
                        if softmax:
                            pe.wait_ge(S["ntopT"], upto(i + 3, BATCH))
                    else:
                        pe.wait_ge(S["o"], i * QT + t)
                    for strip in range(STRIPS):
                        ins = nc.tensor.transpose(desk[:, strip, :], pv_sb[:, strip, t * P:(t + 1) * P], on.ident[:, :])
                    ins.then_inc(S["tokmaj"], 1)
                return fn

            def turn_output(i, k):
                pe.wait_ge(S["o"], (i + 1) * QT)
                for t in range(QT):
                    for c in range(OB):
                        o = o_sb[:, t, :, :].rearrange("p h d -> p (h d)")[:, c * P:(c + 1) * P]
                        ins = nc.tensor.transpose(desk[:, t * OB + c, :], o, on.ident[:, :])
                ins.then_inc(S["oturned"], 1)

            def output(i, k):
                pe.wait_ge(S["oT"], i + 1)
                for t in range(QT):
                    for c in range(OB):
                        ins = nc.tensor.matmul(desk[:, t, :], oT[:, t, c, :], wo[:, c, :], start=(c == 0),
                                               stop=(c == OB - 1))
                ins.then_inc(S["out"], 1)

            after = {r: [] for r in range(ROUNDS)}
            after[0] = [(token_major(0), LAG + 2)]
            after[ROUNDS // 4 + 1] += [(values(1), LAG + 1)]
            after[ROUNDS // 2 - 1] += [(token_major(1), LAG + 2)]
            after[ROUNDS // 2 + 1] += [(turn_output, LAG + 2)]
            if latent:
                after[2] += [(step(turn, 0), FILL)]
                after[3] += [(step(turn, 1), FILL), (step(turn, 2), FILL), (output, LAG + 2), (step(turn, 3), FILL)]
            else:
                after[0] += [(step(turn, 2), FILL + 1)]
                after[2] += [(step(turn, 3), FILL + 1)]
                after[4] += [(step(turn, 0), FILL)]
                after[6] += [(step(turn, 1), FILL)]
                after[7] += [(output, LAG + 2)]
            steps = [(values(0), LAG + 1)] + [(turn_tops, LAG)] * softmax
            for r in range(ROUNDS):
                steps += [(step(tops_, r), TOP)] * softmax + [(step(scores, r), LAG)] + after[r]
            software_pipeline(nc.tensor.Fori, steps, BATCH)

        @block.scalar
        def _(act):
            if softmax:
                act.sem_inc(S["probs"], 2)

            def exps(r, i, k):
                for h in two_heads(r):
                    act.wait_ge(S["score"], i * heads + h + 1)
                    nc.scalar.activation(probs[k][:, h, :], score_ps[h % 2][:, 0:CW], ACT.Exp, scale=softmax_scale)\
                        .then_inc(S["probs"], 1)

            def copy_tops(i, k):
                act.wait_ge(S["ntopTp"], i + 1)
                nc.scalar.activation(ntopT[k][:, :], ntopT_ps, ACT.Copy).then_inc(S["ntopT"], 1)

            def copy_operands(n, i, k):
                act.wait_ge(S["turned"], i * 4 + n + 1 + 8)
                j, block = FILLS[n]
                nc.scalar.activation(opT[k][j][:, block:block + 4, :], opT_ps[:, :, :], ACT.Copy)\
                    .then_inc(S["opT"], 1)

            def take_values(half):
                def fn(i, k):
                    act.wait_ge(S["pv"], i * 2 + half + 3)
                    act.wait_ge(S["tokmaj"], i * QT)
                    n = 1 if latent and half else 2
                    nc.scalar.activation(pv_sb[:, 2 * half:2 * half + n, :], pv_ps[half][:, 0:n, :], ACT.Copy)\
                        .then_inc(S["pvout"], 1)
                return fn

            def copy_output(i, k):
                act.wait_ge(S["oturned"], i + 1)
                act.wait_ge(S["out"], i)
                nc.scalar.activation(oT[:, :, :, :].rearrange("p t c d -> p (t c) d"), desk[:, 0:QT * OB, :], ACT.Copy)\
                    .then_inc(S["oT"], 1)

            after = {r: [] for r in range(ROUNDS)}
            after[ROUNDS // 2] += [(take_values(0), LAG + 1), (take_values(1), LAG + 1)]
            if latent:
                after[3] += [(step(copy_operands, 0), FILL), (copy_output, LAG + 2), (step(copy_operands, 1), FILL),
                             (step(copy_operands, 2), FILL), (step(copy_operands, 3), FILL)]
            else:
                after[0] += [(step(copy_operands, 2), FILL + 1)]
                after[2] += [(step(copy_operands, 3), FILL + 1)]
                after[4] += [(step(copy_operands, 0), FILL)]
                after[6] += [(copy_output, LAG + 2), (step(copy_operands, 1), FILL)]
            steps = [(copy_tops, LAG)] * softmax
            for r in range(ROUNDS):
                steps += [(step(exps, r), LAG)] * softmax + after[r]
            software_pipeline(nc.scalar.Fori, steps, BATCH)


def channel_attention_stage(nc, on, name, dram, heads, hd):
    PAIRS = heads // 2
    assert 2 * hd == P and PAIRS * P == 2 * COLS
    ctx, sb, pb, sem = scope(nc)
    with ctx:
        w_q, w_k = sb(f"{name}_wq", [P, PAIRS, P]), sb(f"{name}_wk", [P, PAIRS, P])
        w_vT, w_out = sb(f"{name}_wvT", [P, PAIRS, P]), sb(f"{name}_wout", [P, PAIRS, P])
        temp, gamma = sb(f"{name}_temp", [P, PAIRS]), sb(f"{name}_gamma", [P, D])
        square = sb(f"{name}_square", [P, TILES, D])
        norm2, norm = sb(f"{name}_norm2", [P, TILES]), sb(f"{name}_norm", [P, TILES])
        x_b = [sb(f"{name}_x{k}", [P, QT, D]) for k in range(2)]
        xT = sb(f"{name}_xT", [P, TOKENS])
        xT_b = sb(f"{name}_xTb", [P, SEQ])
        gram = [sb(f"{name}_gram{k}", [P, P]) for k in range(2)]
        tk = [sb(f"{name}_tk{k}", [P, PAIRS, P]) for k in range(2)]
        sq_k, sq_q = sb(f"{name}_sqk", [P, PAIRS, P]), sb(f"{name}_sqq", [P, PAIRS, P])
        rk, rq = sb(f"{name}_rk", [P, PAIRS, hd]), sb(f"{name}_rq", [P, PAIRS])
        rk_root, rq_root = sb(f"{name}_rkroot", [P, PAIRS, hd]), sb(f"{name}_rqroot", [P, PAIRS])
        logit = sb(f"{name}_logit", [P, PAIRS, hd])
        top, total = sb(f"{name}_top", [P, PAIRS]), sb(f"{name}_total", [P, PAIRS])
        attn = [sb(f"{name}_attn{k}", [P, PAIRS, P]) for k in range(2)]
        u_sb, m_sb = sb(f"{name}_u", [P, PAIRS, P]), sb(f"{name}_m", [P, P])
        tk_ps, tq_ps = pb(f"{name}_tkp", [P, 2, COLS]), pb(f"{name}_tqp", [P, 2, COLS])
        pair_ps = pb(f"{name}_pairp", [P, PAIRS, P])
        rk_ps = pb(f"{name}_rkp", [P, PAIRS, hd])
        gram_ps = pb(f"{name}_gramp", [P, 4, P])
        S = {w: sem(f"{name}_{w}") for w in (
            "w", "zero", "pre", "preroot", "temp", "x", "gramp", "gram", "tkq", "tk", "sq", "norms", "roots", "clip",
            "inv", "r", "simp", "logit", "chain", "exp", "sum", "attn", "up", "u", "mp", "m", "xTb", "out", "s")}
        block = ctx.enter_context(nc.Block())
        loads = [(w_q[:, :, :], dram["w_q"]), (w_k[:, :, :], dram["w_k"]), (w_vT[:, :, :], dram["w_vT"]),
                 (w_out[:, :, :], dram["w_out"]), (temp[:, :], dram["temp"]), (gamma[:, :], dram["gamma"])]
        halves = (slice(0, hd), slice(hd, P))

        @block.sync
        def _(sp):
            for dst, src in loads:
                sp.dma_start(dst, src).then_inc(S["w"], 16)

        @block.gpsimd
        def _(pool):
            for k in range(2):
                ins = nc.gpsimd.memset(attn[k][:, :, :], 0.0)
            ins.then_inc(S["zero"], 1)

            def copy_x(i, k):
                pool.wait_ge(S["out"], i)
                pool.wait_ge(S["gram"], i * 2 + 2)
                nc.gpsimd.tensor_copy(xT_b[:, :], xT[:, bass.ts(i, SEQ)]).then_inc(S["xTb"], 1)

            software_pipeline(nc.gpsimd.Fori, [(copy_x, 0)], BATCH)

        @block.vector
        def _(dve):
            dve.wait_ge(S["w"], 16 * len(loads))
            dve.wait_ge(S["zero"], 1)
            dve.sem_inc(S["s"], 3)
            nc.vector.tensor_tensor(square[:, :, :], on.xn[:, :, :], on.xn[:, :, :], ALU.mult).then_inc(S["pre"], 1)
            dve.wait_ge(S["pre"], 1)
            nc.vector.tensor_reduce(norm2[:, :], square[:, :, :], AX.X, ALU.add).then_inc(S["pre"], 1)
            dve.wait_ge(S["pre"], 2)
            nc.vector.tensor_scalar(norm2[:, :], norm2[:, :], 1e-24, 1.0 / D, ALU.max, ALU.mult).then_inc(S["pre"], 1)
            dve.wait_ge(S["preroot"], 1)
            nc.vector.reciprocal(norm[:, :], norm[:, :]).then_inc(S["pre"], 1)
            dve.wait_ge(S["temp"], 1)
            nc.vector.tensor_scalar(temp[:, :], temp[:, :], 8.0, None, ALU.mult).then_inc(S["pre"], 1)
            dve.wait_ge(S["pre"], 5)

            def x_in(i, k):
                dve.wait_ge(S["gramp"], i + 1)
                for t in range(QT):
                    ins = nc.vector.scalar_tensor_tensor(
                        x_b[k][:, t, :], on.xn[:, bass.ds(i * QT + t, 1), :], norm[:, bass.ds(i * QT + t, 1)],
                        gamma[:, :], ALU.mult, ALU.mult)
                ins.then_inc(S["x"], 1)

            def scores(i, k):
                dve.wait_ge(S["simp"], i + 1)
                dve.wait_ge(S["r"], i + 1)
                for r in halves:
                    ins = nc.vector.tensor_tensor(logit[r, :, :], pair_ps[r, :, r], rk[r, :, :], ALU.mult)
                ins.then_inc(S["logit"], 1)
                dve.wait_ge(S["logit"], i + 1)

                def wide(a):
                    return a[:, :].unsqueeze(2).broadcast_to([P, PAIRS, hd])

                nc.vector.tensor_tensor(logit[:, :, :], logit[:, :, :], wide(rq), ALU.mult).then_inc(S["chain"], 1)
                dve.wait_ge(S["chain"], i * 3 + 1)
                nc.vector.tensor_reduce(top[:, :], logit[:, :, :], AX.X, ALU.max).then_inc(S["chain"], 1)
                dve.wait_ge(S["chain"], i * 3 + 2)
                nc.vector.tensor_tensor(logit[:, :, :], logit[:, :, :], wide(top), ALU.subtract).then_inc(S["chain"], 1)

            def squares(i, k):
                dve.wait_ge(S["tkq"], i + 1)
                dve.wait_ge(S["norms"], i)
                nc.vector.tensor_tensor(sq_q[:, :, :].rearrange("p a b -> p (a b)"),
                                        tq_ps[:, :, :].rearrange("p a b -> p (a b)"),
                                        w_q[:, :, :].rearrange("p a b -> p (a b)"), ALU.mult)
                dve.wait_ge(S["tk"], i + 1)
                ins = nc.vector.tensor_tensor(sq_k[:, :, :], tk[k][:, :, :], w_k[:, :, :], ALU.mult)
                ins.then_inc(S["sq"], 1)

            def weights(i, k):
                dve.wait_ge(S["exp"], i + 1)
                nc.vector.tensor_reduce(total[:, :], logit[:, :, :], AX.X, ALU.add).then_inc(S["sum"], 1)
                dve.wait_ge(S["sum"], i * 2 + 1)
                nc.vector.reciprocal(total[:, :], total[:, :]).then_inc(S["sum"], 1)
                dve.wait_ge(S["sum"], i * 2 + 2)
                dve.wait_ge(S["up"], i + 1)
                for r in halves:
                    ins = nc.vector.tensor_tensor(attn[k][r, :, r], logit[r, :, :],
                                                  total[r, :].unsqueeze(2).broadcast_to([hd, PAIRS, hd]), ALU.mult)
                ins.then_inc(S["attn"], 1)
                dve.wait_ge(S["attn"], i + 1)

            def inverse_norms(i, k):
                dve.wait_ge(S["roots"], i + 1)
                nc.vector.tensor_scalar(rk_root[:, :, :], rk_root[:, :, :], 1e-12, None, ALU.max)
                nc.vector.tensor_scalar(rq_root[:, :], rq_root[:, :], 1e-12, None, ALU.max).then_inc(S["clip"], 1)
                dve.wait_ge(S["clip"], i + 1)
                nc.vector.reciprocal(rk[:, :, :], rk_root[:, :, :])
                nc.vector.reciprocal(rq[:, :], rq_root[:, :]).then_inc(S["inv"], 1)
                dve.wait_ge(S["inv"], i + 1)
                nc.vector.tensor_tensor(rq[:, :], rq[:, :], temp[:, :], ALU.mult).then_inc(S["r"], 1)

            def store(i, k):
                dve.wait_ge(S["out"], i + 1)
                nc.vector.tensor_copy(on.s[:, bass.ds(i * QT, QT), :],
                                      tk_ps[:, 1, 0:SEQ].rearrange("p (t d) -> p t d", t=QT)).then_inc(S["s"], 1)

            software_pipeline(nc.vector.Fori, [(x_in, 0), (weights, 4), (scores, 3), (inverse_norms, 2), (squares, 1),
                                               (store, 4)], BATCH)

        @block.tensor
        def _(pe):
            pe.sem_inc(S["gramp"], 2)
            pe.sem_inc(S["up"], 2)
            pe.wait_ge(S["w"], 16 * len(loads))

            def gram_of(i, k):
                pe.wait_ge(S["x"], i + 1)
                pe.wait_ge(S["gram"], i * 2)
                for t in range(QT):
                    nc.tensor.matmul(gram_ps[:, 0, :], x_b[k][:, t, :], x_b[k][:, t, :], start=(t == 0),
                                     stop=(t == QT - 1))
                for t in range(QT):
                    ins = nc.tensor.transpose(gram_ps[:, 1 + t, :], x_b[k][:, t, :], on.ident[:, :])
                ins.then_inc(S["gramp"], 1)

            def sims(i, k):
                pe.wait_ge(S["tk"], i + 1)
                pe.wait_ge(S["u"], i)
                pe.wait_ge(S["logit"], i)
                for p in range(PAIRS):
                    ins = nc.tensor.matmul(pair_ps[:, p, :], w_q[:, p, :], tk[k][:, p, :], start=True, stop=True)
                ins.then_inc(S["simp"], 1)

            def gram_w(i, k):
                pe.wait_ge(S["gram"], i * 2 + 2)
                pe.wait_ge(S["s"], i)
                pe.wait_ge(S["roots"], i)
                for w, ps in ((w_k, tk_ps), (w_q, tq_ps)):
                    for c in range(2):
                        ins = nc.tensor.matmul(ps[:, c, :], gram[k][:, :],
                                               w[:, 4 * c:4 * c + 4, :].rearrange("p a b -> p (a b)"),
                                               start=True, stop=True)
                ins.then_inc(S["tkq"], 1)

            def mix(i, k):
                pe.wait_ge(S["attn"], i + 1)
                pe.wait_ge(S["logit"], upto(i + 2, BATCH))
                for p in range(PAIRS):
                    ins = nc.tensor.matmul(pair_ps[:, p, :], attn[k][:, p, :], w_out[:, p, :], start=True, stop=True)
                ins.then_inc(S["up"], 1)

            def norms(i, k):
                pe.wait_ge(S["sq"], i + 1)
                pe.wait_ge(S["roots"], i)
                for half, r in enumerate(halves):
                    nc.tensor.matmul(rk_ps[r, :, :], on.ones[:, 0:hd], sq_k[:, :, r], start=True, stop=True)
                for p in range(PAIRS):
                    ins = nc.tensor.matmul(tq_ps[:, 0, p:p + 1], sq_q[:, p, :], on.ones[:, 0:1], start=True, stop=True)
                ins.then_inc(S["norms"], 1)

            def fold(i, k):
                pe.wait_ge(S["u"], i + 2)
                pe.wait_ge(S["tk"], upto(i + 4, BATCH))
                for p in range(PAIRS):
                    ins = nc.tensor.matmul(tk_ps[:, 0, 0:P], w_vT[:, p, :], u_sb[:, p, :], start=(p == 0),
                                           stop=(p == PAIRS - 1))
                ins.then_inc(S["mp"], 1)

            def output(i, k):
                pe.wait_ge(S["m"], i + 1)
                pe.wait_ge(S["xTb"], i + 1)
                pe.wait_ge(S["s"], i + 3)
                for t in range(QT):
                    ins = nc.tensor.matmul(tk_ps[:, 1, t * P:(t + 1) * P], xT_b[:, t * P:(t + 1) * P], m_sb[:, :],
                                           start=True, stop=True)
                ins.then_inc(S["out"], 1)

            software_pipeline(nc.tensor.Fori, [(sims, 3), (norms, 2), (mix, 4), (gram_w, 1), (gram_of, 0), (fold, 4),
                                               (output, 4)], BATCH)

        @block.scalar
        def _(act):
            act.sem_inc(S["u"], 1)
            act.wait_ge(S["w"], 16 * len(loads))
            act.wait_ge(S["pre"], 3)
            nc.scalar.activation(norm[:, :], norm2[:, :], ACT.Sqrt).then_inc(S["preroot"], 1)
            nc.scalar.activation(temp[:, :], temp[:, :], ACT.Exp).then_inc(S["temp"], 1)

            def copy_gram(i, k):
                act.wait_ge(S["gramp"], i + 3)
                nc.scalar.activation(gram[k][:, :], gram_ps[:, 0, :], ACT.Copy).then_inc(S["gram"], 1)
                nc.scalar.activation(xT[:, bass.ts(i, SEQ)], gram_ps[:, 1:3, :].rearrange("p t d -> p (t d)"), ACT.Copy)\
                    .then_inc(S["gram"], 1)

            def exps(i, k):
                act.wait_ge(S["chain"], i * 3 + 3)
                nc.scalar.activation(logit[:, :, :], logit[:, :, :], ACT.Exp).then_inc(S["exp"], 1)

            def copy_tk(i, k):
                act.wait_ge(S["tkq"], i + 1)
                if not isinstance(i, int) or i >= 2:
                    act.wait_ge(S["simp"], i - 1)
                nc.scalar.activation(tk[k][:, :, :].rearrange("p a b -> p (a b)"),
                                     tk_ps[:, :, :].rearrange("p a b -> p (a b)"), ACT.Copy).then_inc(S["tk"], 1)

            def copy_u(i, k):
                act.wait_ge(S["up"], i + 3)
                act.wait_ge(S["mp"], i)
                nc.scalar.activation(u_sb[:, :, :], pair_ps[:, :, :], ACT.Copy).then_inc(S["u"], 1)

            def roots(i, k):
                act.wait_ge(S["norms"], i + 1)
                act.wait_ge(S["r"], i)
                nc.scalar.activation(rk_root[:, :, :], rk_ps[:, :, :], ACT.Sqrt)
                nc.scalar.activation(rq_root[:, :], tq_ps[:, 0, 0:PAIRS], ACT.Sqrt).then_inc(S["roots"], 1)

            def copy_m(i, k):
                act.wait_ge(S["mp"], i + 1)
                act.wait_ge(S["out"], i)
                nc.scalar.activation(m_sb[:, :], tk_ps[:, 0, 0:P], ACT.Copy).then_inc(S["m"], 1)

            software_pipeline(nc.scalar.Fori, [(roots, 2), (exps, 3), (copy_u, 4), (copy_tk, 1), (copy_gram, 0),
                                               (copy_m, 4)], BATCH)


def centroid_route_stage(nc, on, name, dram, experts, chunks, alpha, slot, w_row, w1, b1, rows1, sorted_x, block_rows,
                         filled, rows_written):
    n_blocks = w_row.shape[1]
    ctx, sb, pb, sem = scope(nc)
    with ctx:
        centT, b2 = sb(f"{name}_centT", [P, experts]), sb(f"{name}_b2", [experts, D])
        ln_g, ln_b = sb(f"{name}_lng", [P, experts]), sb(f"{name}_lnb", [P, experts])
        rank_w = sb(f"{name}_rankw", [P, experts])
        aff, pick = sb(f"{name}_aff", [P, TILES, experts]), sb(f"{name}_pick", [P, TILES, experts])
        best, first = (sb(f"{name}_{w}", [P, TILES]) for w in ("best", "first"))
        combine = sb(f"{name}_combine", [P, TILES, experts])
        rank, order = (sb(f"{name}_{w}", [P, experts, TILES]) for w in ("rank", "order"))
        count, start, opened, one = (sb(f"{name}_{w}", [P, experts]) for w in ("count", "start", "opened", "one"))
        blocks_i = sb(f"{name}_blocks_i", [P, experts], I32)
        number = sb(f"{name}_number", [P, P + 1])
        reached = sb(f"{name}_reached", [P, n_blocks, experts])
        owner = sb(f"{name}_owner", [P, n_blocks])
        count_ps = pb(f"{name}_countp", [P, 2, experts, TILES])
        combT = [sb(f"{name}_combT{k}", [experts, COLS]) for k in range(2)]
        aff_ps = pb(f"{name}_affp", [P, COLS])
        bias_ps = pb(f"{name}_biasp", [P, COLS])
        turn_ps = [pb(f"{name}_turnp{k}", [P, COLS]) for k in range(2)]
        init_ps = [pb(f"{name}_initp{k}", [P, TPB, D]) for k in range(2)]
        S = {w: sem(f"{name}_{w}") for w in ("w", "experts", "aff", "bias", "chain", "alpha", "scaled", "turned",
                                             "combT", "init", "g", "pick", "count")}
        loads = [(centT[:, :], dram["centT"]), (b2[:, :], dram["b2"]), (ln_g[:, :], dram["ln_g"]),
                 (ln_b[:, :], dram["ln_b"]), (rank_w[:, :], dram["rank_w"]), (number[:, :], dram["number"])]
        expert_loads = [(w1[:, :, :], dram["w1"]), (b1[:, :, :].rearrange("p e c -> p (e c)"), dram["b1"])]
        block = ctx.enter_context(nc.Block())

        @block.sync
        def _(sp):
            for dst, src in loads:
                sp.dma_start(dst, src).then_inc(S["w"], 16)
            for dst, src in expert_loads:
                sp.dma_start(dst, src).then_inc(S["experts"], 16)
            more = sorted_x.shape[0] // P - TILES
            sp.dma_start(sorted_x[0:TOKENS, :].rearrange("(t p) d -> p t d", p=P), on.xn[:, :, :])\
                .then_inc(filled, 16)
            sp.dma_start(sorted_x[TOKENS:, :].rearrange("(t p) d -> p t d", p=P), on.xn[:, 0:more, :])\
                .then_inc(filled, 16)
            rows = rows1.rearrange("(e p) f -> p e f", p=P)
            sp.wait_ge(S["scaled"], 1)
            sp.dma_start(rows[:, :, 0:chunks * P], w1[:, :, :]).then_inc(rows_written, 16)
            sp.dma_start(rows[:, :, chunks * P:], b1[:, :, :]).then_inc(rows_written, 16)

        @block.tensor
        def _(pe):
            pe.wait_ge(S["w"], 16 * len(loads))
            for t in range(TILES):
                ins = nc.tensor.matmul(aff_ps[:, t * experts:(t + 1) * experts], on.xnT[:, t * P:(t + 1) * P],
                                       centT[:, :], start=True, stop=True)
            ins.then_inc(S["aff"], 1)
            pe.wait_ge(S["pick"], 1)
            picked = pick[:, :, :].rearrange("p t e -> p e t")
            nc.tensor.matmul(count_ps[:, 0, :, :], on.causal[:, :], picked, start=True, stop=True)
            nc.tensor.matmul(count_ps[:, 1, :, :], on.ones[:, :], picked, start=True, stop=True)\
                .then_inc(S["count"], 1)
            pe.wait_ge(S["experts"], 16 * len(expert_loads))
            for e in range(experts):
                for c in range(chunks):
                    n = e * chunks + c
                    ins = nc.tensor.matmul(bias_ps[:, n:n + 1], w1[:, e, c * P:(c + 1) * P], ln_b[:, e:e + 1],
                                           start=True, stop=True)
            ins.then_inc(S["bias"], 1)
            pe.wait_ge(S["chain"], 6)
            for i in range(BLOCKS + 1):
                if i < BLOCKS:
                    if i >= 2:
                        pe.wait_ge(S["combT"], i - 1)
                    for t in range(TPB):
                        ins = nc.tensor.transpose(turn_ps[i % 2][0:experts, t * P:(t + 1) * P],
                                                  combine[:, i * TPB + t, :], on.ident[:, :])
                    ins.then_inc(S["turned"], 1)
                if i:
                    pe.wait_ge(S["combT"], i)
                    if i >= 3:
                        pe.wait_ge(S["g"], i - 2)
                    for t in range(TPB):
                        ins = nc.tensor.matmul(init_ps[(i - 1) % 2][:, t, :], combT[(i - 1) % 2][:, t * P:(t + 1) * P],
                                               b2[:, :], start=True, stop=True)
                    ins.then_inc(S["init"], 1)

        @block.scalar
        def _(act):
            act.wait_ge(S["chain"], 2)
            nc.scalar.activation(alpha[:, :], best[:, :], ACT.Sigmoid).then_inc(S["alpha"], 1)
            for i in range(BLOCKS):
                act.wait_ge(S["turned"], i + 1)
                if i >= 2:
                    act.wait_ge(S["init"], i - 1)
                nc.scalar.activation(combT[i % 2][:, :], turn_ps[i % 2][0:experts, :], ACT.Copy)\
                    .then_inc(S["combT"], 1)

        @block.vector
        def _(dve):
            done = [0]

            def link(ins):
                done[0] += 1
                ins.then_inc(S["chain"], 1)
                dve.wait_ge(S["chain"], done[0])

            def wide(a):
                return a[:, :].unsqueeze(2).broadcast_to([P, TILES, experts])

            dve.wait_ge(S["w"], 16 * len(loads))
            dve.wait_ge(S["aff"], 1)
            link(nc.vector.tensor_copy(aff[:, :, :].rearrange("p t e -> p (t e)"), aff_ps[:, 0:TILES * experts]))
            link(nc.vector.tensor_reduce(best[:, :], aff[:, :, :], AX.X, ALU.max))
            link(nc.vector.tensor_tensor(pick[:, :, :], aff[:, :, :], wide(best), ALU.is_equal))
            link(nc.vector.tensor_tensor(pick[:, :, :], pick[:, :, :],
                                         rank_w[:, :].unsqueeze(1).broadcast_to([P, TILES, experts]), ALU.mult))
            link(nc.vector.tensor_reduce(first[:, :], pick[:, :, :], AX.X, ALU.max))
            nc.vector.tensor_tensor(pick[:, :, :], pick[:, :, :], wide(first), ALU.is_equal).then_inc(S["pick"], 1)
            dve.wait_ge(S["pick"], 1)
            dve.wait_ge(S["alpha"], 1)
            link(nc.vector.tensor_tensor(combine[:, :, :], pick[:, :, :], wide(alpha), ALU.mult))
            nc.vector.memset(order[:, :, :], 1.0)
            link(nc.vector.memset(one[:, :], 1.0))
            dve.wait_ge(S["count"], 1)
            before_tiles(nc, link, order, rank, count_ps[:, 1], count_ps[:, 0])
            link(nc.vector.tensor_reduce(count[:, :], count_ps[:, 1], AX.X, ALU.add))
            link(nc.vector.tensor_scalar(blocks_i[:, :], count[:, :], block_rows - 1.0, None, ALU.add))
            link(nc.vector.tensor_scalar(blocks_i[:, :], blocks_i[:, :], block_rows.bit_length() - 1, None,
                                         ALU.arith_shift_right))
            link(nc.vector.tensor_copy(count[:, :], blocks_i[:, :]))
            link(nc.vector.tensor_tensor_scan(start[:, :], one[:, :], count[:, :], 0.0, ALU.mult, ALU.add))
            link(nc.vector.tensor_tensor(start[:, :], start[:, :], count[:, :], ALU.subtract))
            link(nc.vector.tensor_scalar(opened[:, :], start[:, :], float(block_rows), -1.0, ALU.mult, ALU.add))
            link(nc.vector.tensor_tensor(rank[:, :, :], rank[:, :, :],
                                         opened[:, :].unsqueeze(2).broadcast_to([P, experts, TILES]), ALU.add))
            link(nc.vector.tensor_tensor(rank[:, :, :], rank[:, :, :], pick[:, :, :].rearrange("p t e -> p e t"),
                                         ALU.mult))
            link(nc.vector.tensor_reduce(first[:, :], rank[:, :, :].rearrange("p e t -> p t e"), AX.X, ALU.add))
            link(nc.vector.tensor_copy(slot[:, :], first[:, :]))
            link(nc.vector.tensor_tensor(reached[:, :, :],
                                         number[:, 0:n_blocks].unsqueeze(2).broadcast_to([P, n_blocks, experts]),
                                         start[:, :].unsqueeze(1).broadcast_to([P, n_blocks, experts]), ALU.is_ge))
            link(nc.vector.tensor_reduce(owner[:, :], reached[:, :, :], AX.X, ALU.add))
            link(nc.vector.tensor_scalar(owner[:, :], owner[:, :], -1.0, float(P), ALU.add, ALU.mult))
            link(nc.vector.tensor_scalar(w_row[:, :], owner[:, :], number[:, P:P + 1], None, ALU.add))
            dve.wait_ge(S["bias"], 1)
            flat = b1[:, :, :].rearrange("p e c -> p (e c)")
            nc.vector.tensor_tensor(flat, flat, bias_ps[:, 0:experts * chunks], ALU.add)
            for e in range(experts):
                ins = nc.vector.tensor_scalar(w1[:, e, :], w1[:, e, :], ln_g[:, e:e + 1], None, ALU.mult)
            ins.then_inc(S["scaled"], 1)
            for i in range(BLOCKS):
                dve.wait_ge(S["init"], i + 1)
                t = slice(i * TPB, (i + 1) * TPB)
                nc.vector.tensor_tensor(on.g[:, t, :], init_ps[i % 2][:, :, :], on.xn[:, t, :], ALU.add)\
                    .then_inc(S["g"], 1)


def sorted_experts_stage(nc, on, name, chunks, slot, w_row, alpha, rows1, rows2, sorted_x, sorted_y, block_rows,
                         filled, rows_written):
    RT = block_rows // P
    W1 = chunks * P + chunks
    n_blocks = w_row.shape[1]
    ctx, sb, pb, sem = scope(nc)
    with ctx:
        row_of = [sb(f"{name}_row_of{k}", [P, 1], U32) for k in range(2)]
        w1 = [sb(f"{name}_w1{k}", [P, W1]) for k in range(2)]
        w2 = [sb(f"{name}_w2{k}", [P, chunks * D]) for k in range(2)]
        x_b = [sb(f"{name}_x{k}", [P, RT, D]) for k in range(2)]
        xT = [sb(f"{name}_xT{k}", [P, block_rows]) for k in range(2)]
        h = [sb(f"{name}_h{k}", [P, chunks, block_rows]) for k in range(2)]
        y = [sb(f"{name}_y{k}", [P, RT, D]) for k in range(2)]
        turn_ps = pb(f"{name}_turnp", [P, block_rows])
        hidden_ps = [pb(f"{name}_hiddenp{b}", [P, chunks // 2, block_rows]) for b in range(2)]
        down_ps = [pb(f"{name}_downp{k}", [P, RT, D]) for k in range(2)]
        S = {w: sem(f"{name}_{w}") for w in ("row_of", "placed", "going", "turned", "xT", "proj", "h", "down", "y",
                                             "back")}
        w_in, x_in, stored = ([sem(f"{name}_{w}{k}") for k in range(2)] for w in ("w_in", "x_in", "stored"))
        block = ctx.enter_context(nc.Block())

        def pipeline(fori, *steps):
            software_pipeline(fori, list(steps), n_blocks)

        def landed(j, k, each):
            return (j // 2 + 1) * each if isinstance(j, int) else (j - k) * (each // 2) + each

        def block_of(rows, j):
            return rows[bass.ts(j, block_rows), :].rearrange("(t p) d -> p t d", p=P)

        @block.gpsimd
        def _(pool):
            pool.wait_ge(filled, 32)
            for t in range(TILES):
                nc.gpsimd.indirect_dma_start(
                    out=sorted_x, out_offset=bass.IndirectOffsetOnAxis(ap=slot[:, t:t + 1], axis=0),
                    in_=on.v[:, t, :], in_offset=None).then_inc(S["placed"], 16)

            def gather(j, k):
                pool.wait_ge(S["down"], j + 1)
                pool.wait_ge(S["row_of"], j + 1)
                pool.sem_inc(S["going"], 1)
                for w, rows in ((w1, rows1), (w2, rows2)):
                    nc.gpsimd.indirect_dma_start(
                        out=w[k][:, :], out_offset=None, in_=rows,
                        in_offset=bass.IndirectOffsetOnAxis(ap=row_of[k][:, :], axis=0)).then_inc(w_in[k], 16)

            pool.wait_ge(rows_written, 32)
            pipeline(nc.gpsimd.Fori, (gather, 0))
            for k in range(2):
                pool.wait_ge(stored[k], 8 * n_blocks)
            for t in range(TILES):
                nc.gpsimd.indirect_dma_start(
                    out=on.v[:, t, :], out_offset=None, in_=sorted_y,
                    in_offset=bass.IndirectOffsetOnAxis(ap=slot[:, t:t + 1], axis=0)).then_inc(S["back"], 16)

        @block.sync
        def _(sp):
            sp.wait_ge(S["placed"], 16 * TILES)

            def load(j, k):
                sp.wait_ge(S["turned"], j + 1)
                sp.dma_start(x_b[k][:, :, :], block_of(sorted_x, j)).then_inc(x_in[k], 16)

            def store(j, k):
                sp.wait_ge(S["y"], j + 3)
                sp.dma_start(block_of(sorted_y, j), y[k][:, :, :]).then_inc(stored[k], 16)

            pipeline(nc.sync.Fori, (load, 0), (store, 4))

        @block.tensor
        def _(pe):
            pe.sem_inc(S["turned"], 2)
            pe.sem_inc(S["down"], 2)

            def turn(j, k):
                pe.wait_ge(x_in[k], landed(j, k, 16))
                pe.wait_ge(S["xT"], j + 1)
                for t in range(RT):
                    ins = nc.tensor.transpose(turn_ps[:, t * P:(t + 1) * P], x_b[k][:, t, :], on.ident[:, :])
                ins.then_inc(S["turned"], 1)

            def project(j, k):
                pe.wait_ge(w_in[k], landed(j, k, 32))
                pe.wait_ge(S["xT"], j + 2)
                for b in range(2):
                    pe.wait_ge(S["h"], j * 2 + b + 1)
                    for c in range(chunks // 2):
                        n = b * (chunks // 2) + c
                        ins = nc.tensor.matmul(hidden_ps[b][:, c, :], w1[k][:, n * P:(n + 1) * P], xT[k][:, :],
                                               start=True, stop=True)
                    ins.then_inc(S["proj"], 1)

            def down(j, k):
                pe.wait_ge(S["h"], j * 2 + 4)
                pe.wait_ge(S["y"], j + 1)
                for t in range(RT):
                    for c in range(chunks):
                        ins = nc.tensor.matmul(down_ps[k][:, t, :], h[k][:, c, t * P:(t + 1) * P],
                                               w2[k][:, c * D:(c + 1) * D], start=(c == 0), stop=(c == chunks - 1))
                ins.then_inc(S["down"], 1)

            pipeline(nc.tensor.Fori, (down, 3), (project, 2), (turn, 1))

        @block.scalar
        def _(act):
            act.sem_inc(S["xT"], 1)
            act.sem_inc(S["h"], 2)

            def copy_x(j, k):
                act.wait_ge(S["turned"], j + 3)
                act.wait_ge(S["proj"], max(j * 2 - 2, 0) if isinstance(j, int) else j * 2 - 2)
                nc.scalar.activation(xT[k][:, :], turn_ps[:, :], ACT.Copy).then_inc(S["xT"], 1)

            def hidden(j, k):
                act.wait_ge(S["down"], j + 1)
                for b in range(2):
                    act.wait_ge(S["proj"], j * 2 + b + 1)
                    for c in range(chunks // 2):
                        n = b * (chunks // 2) + c
                        ins = nc.scalar.activation(h[k][:, n, :], hidden_ps[b][:, c, :], ACT.Relu,
                                                   bias=w1[k][:, chunks * P + n:chunks * P + n + 1])
                    ins.then_inc(S["h"], 1)

            pipeline(nc.scalar.Fori, (hidden, 2), (copy_x, 1))

        @block.vector
        def _(dve):
            dve.sem_inc(S["y"], 2)

            def rows_in(j, k):
                if not isinstance(j, int) or j >= 2:
                    dve.wait_ge(w_in[k], landed(j, k, 32) - 32)
                nc.vector.tensor_copy(row_of[k][:, :], w_row[:, bass.ds(j, 1)]).then_inc(S["row_of"], 1)

            def take(j, k):
                dve.wait_ge(S["down"], j + 3)
                if not isinstance(j, int) or j >= 2:
                    dve.wait_ge(stored[k], landed(j, k, 16) - 16)
                nc.vector.tensor_copy(y[k][:, :, :], down_ps[k][:, :, :]).then_inc(S["y"], 1)

            pipeline(nc.vector.Fori, (rows_in, 0), (take, 3))
            dve.wait_ge(S["back"], 16 * TILES)
            for t in range(TILES):
                nc.vector.scalar_tensor_tensor(on.g[:, t, :], on.v[:, t, :], alpha[:, t:t + 1], on.g[:, t, :], ALU.mult,
                                               ALU.add)


def centroid_experts(nc, on, name, dram, experts, chunks):
    block_rows = 2 * P
    n_blocks = TOKENS // block_rows + experts
    rows1 = nc.dram_tensor(f"{name}_rows1", (experts * P, chunks * P + chunks), F32, kind="Internal").ap()
    sorted_x, sorted_y = (nc.dram_tensor(f"{name}_sorted_{w}", (n_blocks * block_rows, D), F32, kind="Internal").ap()
                          for w in ("x", "y"))
    ctx, sb, pb, sem = scope(nc)
    with ctx:
        alpha = sb(f"{name}_alpha", [P, TILES])
        slot, w_row = sb(f"{name}_slot", [P, TILES], U32), sb(f"{name}_w_row", [P, n_blocks], U32)
        w1, b1 = sb(f"{name}_w1", [P, experts, chunks * P]), sb(f"{name}_b1", [P, experts, chunks])
        filled, rows_written = sem(f"{name}_filled"), sem(f"{name}_rows_written")
        centroid_route_stage(nc, on, f"{name}r", dram, experts, chunks, alpha, slot, w_row, w1, b1, rows1, sorted_x,
                             block_rows, filled, rows_written)
        layernorm_stage(nc, on, f"{name}n", on.xn, on.v, None, False)
        sorted_experts_stage(nc, on, f"{name}e", chunks, slot, w_row, alpha, rows1,
                             dram["w2"].rearrange("e p f -> (e p) f"), sorted_x, sorted_y, block_rows,
                             filled, rows_written)


def top_route_stage(nc, on, name, dram, experts, top_k, combT, spread, weights):
    ctx, sb, pb, sem = scope(nc)
    with ctx:
        routerT, bias = sb(f"{name}_routerT", [P, experts]), sb(f"{name}_bias", [P, experts])
        prob, fixed, mask, equal, order, keep = (sb(f"{name}_{w}", [P, TILES, experts]) for w in (
            "prob", "fixed", "mask", "equal", "order", "keep"))
        parts = sb(f"{name}_parts", [P, TILES, 3, experts], BF16)
        turned_ps = [pb(f"{name}_turnedp{k}", [P, COLS], BF16) for k in range(2)]
        most = sb(f"{name}_most", [P, TILES, 8])
        col = [sb(f"{name}_col{k}", [P, TILES]) for k in range(2)]
        logit_ps = [pb(f"{name}_logitp{k}", [P, TILES // 2, experts]) for k in range(2)]
        S = {w: sem(f"{name}_{w}") for w in ("w", "logit", "chain", "exp", "parts", "turned",
                                             "copied", "experts", "spread")}
        loads = [(routerT[:, :], dram["routerT"]), (bias[:, :], dram["bias"])]
        block = ctx.enter_context(nc.Block())

        @block.sync
        def _(sp):
            for dst, src in loads:
                sp.dma_start(dst, src).then_inc(S["w"], 16)
            for dst, src in weights:
                sp.dma_start(dst, src).then_inc(S["experts"], 16)
            sp.wait_ge(S["experts"], 16 * len(weights))

        @block.gpsimd
        def _(pool):
            nc.gpsimd.memset(spread[:, :, :, :], 0.0).then_inc(S["spread"], 1)
            for m in range(3):
                pool.wait_ge(S["spread"], m + 1)
                nc.gpsimd.affine_select(out=spread[:, :, :, :], in_=spread[:, :, :, :], compare_op=ALU.not_equal,
                                        fill=1.0, base=-m * experts, pattern=[[-2, experts // 2], [-1, 2], [0, P // 2]],
                                        channel_multiplier=1).then_inc(S["spread"], 1)
            pool.wait_ge(S["spread"], 4)

        @block.tensor
        def _(pe):
            pe.wait_ge(S["w"], 16 * len(loads))
            for t in range(TILES):
                ins = nc.tensor.matmul(logit_ps[t // (TILES // 2)][:, t % (TILES // 2), :],
                                       on.xnT[:, t * P:(t + 1) * P], routerT[:, :], start=True, stop=True)
            ins.then_inc(S["logit"], 1)
            pe.wait_ge(S["parts"], 4)
            for i in range(BLOCKS):
                if i >= 2:
                    pe.wait_ge(S["copied"], i - 1)
                for t in range(TPB):
                    ins = nc.tensor.transpose(turned_ps[i % 2][0:3 * experts, t * P:(t + 1) * P],
                                              parts[:, i * TPB + t, :, :].rearrange("p m e -> p (m e)"),
                                              on.ident_bf[:, :])
                ins.then_inc(S["turned"], 1)

        @block.scalar
        def _(act):
            act.wait_ge(S["chain"], 4)
            nc.scalar.activation(prob[:, :, :], prob[:, :, :], ACT.Exp).then_inc(S["exp"], 1)
            for i in range(BLOCKS):
                act.wait_ge(S["turned"], i + 1)
                nc.scalar.activation(combT[:, i * COLS:(i + 1) * COLS], turned_ps[i % 2][0:3 * experts, :], ACT.Copy)\
                    .then_inc(S["copied"], 1)

        @block.vector
        def _(dve):
            done = {w: 0 for w in ("chain", "parts")}

            def link(ins, w="chain"):
                done[w] += 1
                ins.then_inc(S[w], 1)
                dve.wait_ge(S[w], done[w])

            def wide(a):
                return a.unsqueeze(2).broadcast_to([P, TILES, experts])

            def each(out, a, b, op):
                link(nc.vector.tensor_tensor(out[:, :, :], a[:, :, :], b, op))

            nc.vector.memset(order[:, :, :], 1.0)
            dve.wait_ge(S["w"], 16 * len(loads))
            dve.wait_ge(S["logit"], 1)
            half = TILES // 2
            link(nc.vector.tensor_copy(prob[:, 0:half, :], logit_ps[0][:, :, :]))
            link(nc.vector.tensor_copy(prob[:, half:, :], logit_ps[1][:, :, :]))
            link(nc.vector.tensor_reduce(col[0][:, :], prob[:, :, :], AX.X, ALU.max))
            each(prob, prob, wide(col[0][:, :]), ALU.subtract)
            dve.wait_ge(S["exp"], 1)
            link(nc.vector.tensor_reduce(col[0][:, :], prob[:, :, :], AX.X, ALU.add))
            link(nc.vector.reciprocal(col[1][:, :], col[0][:, :]))
            each(prob, prob, wide(col[1][:, :]), ALU.mult)
            each(fixed, prob, bias[:, :].unsqueeze(1).broadcast_to([P, TILES, experts]), ALU.add)
            for t in range(TILES):
                ins = nc.vector.max(most[:, t, :], fixed[:, t, :])
            link(ins)
            last = wide(most[:, :, top_k - 1])
            each(keep, fixed, last, ALU.is_gt)
            each(equal, fixed, last, ALU.is_equal)
            link(nc.vector.tensor_reduce(col[0][:, :], keep[:, :, :], AX.X, ALU.add))
            link(nc.vector.tensor_scalar(col[0][:, :], col[0][:, :], -1.0, float(top_k), ALU.mult, ALU.add))
            link(nc.vector.memset(order[:, :, 0:1], 0.0))
            link(nc.vector.tensor_tensor_scan(mask[:, :, :].rearrange("p t e -> p (t e)"),
                                              order[:, :, :].rearrange("p t e -> p (t e)"),
                                              equal[:, :, :].rearrange("p t e -> p (t e)"), 0.0, ALU.mult, ALU.add))
            each(mask, mask, wide(col[0][:, :]), ALU.is_le)
            each(equal, equal, mask[:, :, :], ALU.mult)
            each(keep, keep, equal[:, :, :], ALU.add)
            each(keep, keep, prob[:, :, :], ALU.mult)
            link(nc.vector.tensor_reduce(col[0][:, :], keep[:, :, :], AX.X, ALU.add))
            link(nc.vector.tensor_scalar(col[0][:, :], col[0][:, :], 1e-12, None, ALU.max))
            link(nc.vector.reciprocal(col[1][:, :], col[0][:, :]))
            each(keep, keep, wide(col[1][:, :]), ALU.mult)
            link(nc.vector.tensor_copy(parts[:, :, 0, :], keep[:, :, :]), "parts")
            link(nc.vector.tensor_tensor(fixed[:, :, :], keep[:, :, :], parts[:, :, 0, :], ALU.subtract), "parts")
            link(nc.vector.tensor_copy(parts[:, :, 1, :], fixed[:, :, :]), "parts")
            link(nc.vector.tensor_tensor(parts[:, :, 2, :], fixed[:, :, :], parts[:, :, 1, :], ALU.subtract), "parts")


def summed_experts_stage(nc, on, name, experts, w_sb, combT, spread):
    UNITS = experts // 2 + 1
    ctx, sb, pb, sem = scope(nc)
    with ctx:
        silu, prod, h = ([sb(f"{name}_{w}{k}", [P, COLS]) for k in range(2)] for w in ("silu", "prod", "h"))
        gate_ps, up_ps, weight_ps = ([pb(f"{name}_{w}{k}", [P, COLS]) for k in range(2)] for w in (
            "gatep", "upp", "weightp"))
        down_ps = [pb(f"{name}_downp{k}", [P, TPB, D]) for k in range(2)]
        S = {w: sem(f"{name}_{w}") for w in ("gate", "up", "silu", "prod", "h", "down", "taken")}
        block = ctx.enter_context(nc.Block())

        def unit(i, k, q):
            return i * UNITS + q, (k * UNITS + q) % 2

        @block.tensor
        def _(pe):
            pe.sem_inc(S["down"], 2)

            def project(q, i, k):
                n, b = unit(i, k, q)
                cols = bass.ts(i, COLS)
                pe.wait_ge(S["silu"], n + 1)
                nc.tensor.matmul(gate_ps[b][:, :], w_sb["gate"][:, q, :], on.xnT[:, cols], start=True, stop=True)\
                    .then_inc(S["gate"], 1)
                pe.wait_ge(S["prod"], n + 1)
                ins = nc.tensor.matmul(up_ps[b][:, :], w_sb["up"][:, q, :], on.xnT[:, cols], start=True, stop=True)
                if q:
                    pe.wait_ge(S["h"], n + 1)
                    ins = nc.tensor.matmul(weight_ps[b][:, :], spread[:, q - 1, :, :].rearrange("p a b -> p (a b)"),
                                           combT[:, cols], start=True, stop=True)
                ins.then_inc(S["up"], 1)

            def down(q, i, k):
                n, b = unit(i, k, q)
                pe.wait_ge(S["h"], n + 3)
                if q == 0:
                    pe.wait_ge(S["taken"], i + 1)
                for t in range(TPB):
                    ins = nc.tensor.matmul(down_ps[k][:, t, :], h[b][:, t * P:(t + 1) * P], w_sb["down"][:, q, :],
                                           start=(q == 0 and t == 0), stop=(q == UNITS - 1), skip_group_check=True)
                ins.then_inc(S["down"], 1)

            def others(i, k):
                for q in range(2, UNITS):
                    project(q, i, k)
                    down(q - 2, i, k)

            software_pipeline(nc.tensor.Fori, [(lambda i, k: project(0, i, k), 0),
                                               (lambda i, k: down(UNITS - 2, i, k), 1),
                                               (lambda i, k: project(1, i, k), 0),
                                               (lambda i, k: down(UNITS - 1, i, k), 1), (others, 0)], BLOCKS)

        @block.scalar
        def _(act):
            act.sem_inc(S["silu"], 2)

            def silus(i, k):
                for q in range(UNITS):
                    n, b = unit(i, k, q)
                    act.wait_ge(S["gate"], n + 1)
                    act.wait_ge(S["prod"], n + 1)
                    nc.scalar.activation(silu[b][:, :], gate_ps[b][:, :], ACT.Silu).then_inc(S["silu"], 1)

            software_pipeline(nc.scalar.Fori, [(silus, 0)], BLOCKS)

        @block.vector
        def _(dve):
            for w in ("prod", "h", "taken"):
                dve.sem_inc(S[w], 2)

            def product(q, i, k):
                n, b = unit(i, k, q)
                dve.wait_ge(S["silu"], n + 3)
                dve.wait_ge(S["up"], n + 1)
                dve.wait_ge(S["h"], n + 1)
                nc.vector.tensor_tensor(prod[b][:, :], up_ps[b][:, :], silu[b][:, :], ALU.mult).then_inc(S["prod"], 1)

            def weigh(q, i, k):
                n, b = unit(i, k, q)
                dve.wait_ge(S["prod"], n + 3)
                dve.wait_ge(S["down"], n + 1)
                if q:
                    nc.vector.tensor_tensor(h[b][:, :], prod[b][:, :], weight_ps[b][:, :], ALU.mult)\
                        .then_inc(S["h"], 1)
                else:
                    nc.vector.tensor_copy(h[b][:, :], prod[b][:, :]).then_inc(S["h"], 1)

            def others(lo, hi):
                def fn(i, k):
                    for q in range(lo, hi):
                        product(q, i, k)
                        weigh(q - 1, i, k)
                return fn

            def take(i, k):
                dve.wait_ge(S["down"], i * UNITS + (UNITS + 2))
                nc.vector.tensor_copy(on.g[:, bass.ts(i, TPB), :], down_ps[k][:, :, :]).then_inc(S["taken"], 1)

            software_pipeline(nc.vector.Fori, [(lambda i, k: product(0, i, k), 0),
                                               (lambda i, k: weigh(UNITS - 1, i, k), 1), (others(1, 4), 0), (take, 1),
                                               (others(4, UNITS), 0)], BLOCKS)


def top_experts(nc, on, name, dram, experts, top_k):
    ctx, sb, pb, sem = scope(nc)
    with ctx:
        units = experts // 2 + 1
        combT = sb(f"{name}_combT", [3 * experts, TOKENS], BF16)
        spread = sb(f"{name}_spread", [3 * experts, experts // 2, 2, P // 2], BF16)
        w_sb = {w: sb(f"{name}_{w}", [P, units, P]) for w in ("gate", "up", "down")}
        loads = []
        for w in w_sb:
            loads.append((w_sb[w][:, 0, :], dram[f"shared_{w}"]))
            loads.append((w_sb[w][:, 1:, :], dram[f"pair_{w}"].rearrange("e p f -> p e f")))
        top_route_stage(nc, on, f"{name}r", dram, experts, top_k, combT, spread, loads)
        summed_experts_stage(nc, on, f"{name}e", experts, w_sb, combT, spread)


def unpack_weights_stage(nc, name, dram, scale, w_sb):
    ctx, sb, pb, sem = scope(nc)
    with ctx:
        kinds = list(w_sb)
        whole = {w: sb(f"{name}_{w}", [P, w_sb[w].shape[1], P], I32) for w in kinds}
        loaded, scaled = sem(f"{name}_loaded"), sem(f"{name}_scaled")
        block = ctx.enter_context(nc.Block())

        @block.sync
        def _(sp):
            for w in kinds:
                sp.dma_start(whole[w][:, :, :], dram[w]).then_inc(loaded, 16)

        @block.vector
        def _(dve):
            for w in kinds:
                dve.wait_ge(loaded, 16 * len(kinds))
                nc.vector.tensor_scalar(w_sb[w][:, :, :], whole[w][:, :, :], scale, None, ALU.mult).then_inc(scaled, 1)
            dve.wait_ge(scaled, len(kinds))


def integer_ffn(nc, on, name, dram, hidden):
    chunks = hidden // P
    ctx, sb, pb, sem = scope(nc)
    with ctx:
        w_sb = {w: sb(f"{name}_{w}", [P, chunks, P]) for w in ("gate", "up", "down")}
        unpack_weights_stage(nc, f"{name}u", dram, 1.0 / 127.0, w_sb)
        ffn_stage(nc, on, f"{name}e", chunks, w_sb)


def choice_route_stage(nc, on, name, dram, experts, capacity, combine, place, values):
    ctx, sb, pb, sem = scope(nc)
    with ctx:
        gateT = sb(f"{name}_gateT", [P, experts])
        score, mask, equal, rank, order = (sb(f"{name}_{w}", [P, experts, TILES]) for w in (
            "score", "mask", "equal", "rank", "order"))
        count, need = sb(f"{name}_count", [P, experts]), sb(f"{name}_need", [P, experts])
        slot, part = (sb(f"{name}_{w}", [P, experts, TILES], I32) for w in ("slot", "part"))
        number = sb(f"{name}_number", [P, P + 1])
        bit, step, least, trial = (sb(f"{name}_{w}", [P, experts], I32) for w in ("bit", "step", "least", "trial"))
        logit_ps = pb(f"{name}_logitp", [P, TILES, experts])
        total_ps = pb(f"{name}_totalp", [P, experts])
        within_ps, tiles_ps = (pb(f"{name}_{w}", [P, experts, TILES]) for w in ("withinp", "tilesp"))
        S = {w: sem(f"{name}_{w}") for w in ("w", "logit", "exp", "chain", "search", "halved", "counted", "rest", "final")}
        BITS, AT_ONCE = 30, 5
        block = ctx.enter_context(nc.Block())

        loads = [(gateT[:, :], dram["gateT"]), (number[:, :], dram["number"])]

        def each_bit(fori, body):
            with fori(0, BITS // AT_ONCE) as r:
                for n in range(AT_ONCE):
                    body(r * AT_ONCE + n)

        @block.sync
        def _(sp):
            for dst, src in loads:
                sp.dma_start(dst, src).then_inc(S["w"], 16)

        @block.tensor
        def _(pe):
            pe.wait_ge(S["w"], 16 * len(loads))
            for t in range(TILES):
                ins = nc.tensor.matmul(logit_ps[:, t, :], on.xnT[:, t * P:(t + 1) * P], gateT[:, :], start=True,
                                       stop=True)
            ins.then_inc(S["logit"], 1)

            def count_all(i):
                pe.wait_ge(S["search"], i * 4 + 3)
                nc.tensor.matmul(total_ps[:, :], on.ones[:, :], count[:, :], start=True, stop=True)\
                    .then_inc(S["counted"], 1)

            each_bit(nc.tensor.Fori, count_all)
            pe.wait_ge(S["rest"], 3)
            nc.tensor.matmul(total_ps[:, :], on.ones[:, :], count[:, :], start=True, stop=True)
            nc.tensor.matmul(within_ps[:, :, :], on.causal[:, :], equal[:, :, :], start=True, stop=True)
            nc.tensor.matmul(tiles_ps[:, :, :], on.ones[:, :], equal[:, :, :], start=True, stop=True)\
                .then_inc(S["final"], 1)
            pe.wait_ge(S["rest"], 4)
            nc.tensor.matmul(within_ps[:, :, :], on.causal[:, :], equal[:, :, :], start=True, stop=True)
            nc.tensor.matmul(tiles_ps[:, :, :], on.ones[:, :], equal[:, :, :], start=True, stop=True)\
                .then_inc(S["final"], 1)

        @block.scalar
        def _(act):
            act.wait_ge(S["logit"], 1)
            nc.scalar.activation(score[:, :, :], logit_ps[:, :, :].rearrange("p t e -> p e t"), ACT.Exp, scale=-1.0)\
                .then_inc(S["exp"], 1)

        @block.vector
        def _(dve):
            done = {w: 0 for w in ("chain", "rest")}

            def link(ins, w="chain"):
                done[w] += 1
                ins.then_inc(S[w], 1)
                dve.wait_ge(S[w], done[w])

            def wide(a):
                return a.unsqueeze(2).broadcast_to([P, experts, TILES])

            nc.vector.memset(order[:, :, :], 1.0)
            nc.vector.memset(bit[:, :], 1 << (BITS - 1))
            link(nc.vector.memset(least[:, :], 0))
            dve.wait_ge(S["exp"], 1)
            link(nc.vector.tensor_scalar(mask[:, :, :], score[:, :, :], 1.0, None, ALU.add))
            link(nc.vector.reciprocal(score[:, :, :], mask[:, :, :]))
            def try_bit(i):
                nc.vector.tensor_tensor(trial[:, :], least[:, :], bit[:, :], ALU.bitwise_or).then_inc(S["search"], 1)
                dve.wait_ge(S["search"], i * 4 + 1)
                nc.vector.tensor_tensor(mask[:, :, :], score[:, :, :], wide(trial[:, :].bitcast(F32)), ALU.is_ge)\
                    .then_inc(S["search"], 1)
                dve.wait_ge(S["search"], i * 4 + 2)
                nc.vector.tensor_reduce(count[:, :], mask[:, :, :], AX.X, ALU.add).then_inc(S["search"], 1)
                dve.wait_ge(S["counted"], i + 1)
                nc.vector.scalar_tensor_tensor(step[:, :], total_ps[:, :], float(capacity), bit[:, :], ALU.is_ge,
                                               ALU.mult).then_inc(S["search"], 1)
                dve.wait_ge(S["search"], i * 4 + 4)
                nc.vector.tensor_tensor(least[:, :], least[:, :], step[:, :], ALU.bitwise_or)
                nc.vector.tensor_scalar(bit[:, :], bit[:, :], 1, None, ALU.logical_shift_right)\
                    .then_inc(S["halved"], 1)
                dve.wait_ge(S["halved"], i + 1)

            each_bit(nc.vector.Fori, try_bit)
            last = wide(least[:, :].bitcast(F32))
            link(nc.vector.tensor_tensor(mask[:, :, :], score[:, :, :], last, ALU.is_gt), "rest")
            link(nc.vector.tensor_tensor(equal[:, :, :], score[:, :, :], last, ALU.is_equal), "rest")
            link(nc.vector.tensor_reduce(count[:, :], mask[:, :, :], AX.X, ALU.add), "rest")
            dve.wait_ge(S["final"], 1)
            link(nc.vector.tensor_scalar(need[:, :], total_ps[:, :], -1.0, float(capacity), ALU.mult, ALU.add))
            before_tiles(nc, link, order, rank, tiles_ps, within_ps)
            link(nc.vector.tensor_tensor(rank[:, :, :], rank[:, :, :], wide(need[:, :]), ALU.is_le))
            link(nc.vector.tensor_tensor(equal[:, :, :], equal[:, :, :], rank[:, :, :], ALU.mult))
            link(nc.vector.tensor_tensor(equal[:, :, :], mask[:, :, :], equal[:, :, :], ALU.add), "rest")
            link(nc.vector.tensor_tensor(combine[:, :, :], equal[:, :, :], score[:, :, :], ALU.mult))
            dve.wait_ge(S["final"], 2)
            before_tiles(nc, link, order, rank, tiles_ps, within_ps)
            link(nc.vector.tensor_scalar(slot[:, :, :], rank[:, :, :], -1.0, None, ALU.add))
            link(nc.vector.tensor_scalar(part[:, :, :], slot[:, :, :], P - 1, None, ALU.bitwise_and))
            link(nc.vector.scalar_tensor_tensor(mask[:, :, :], part[:, :, :], 1.0, equal[:, :, :], ALU.add, ALU.mult))
            link(nc.vector.tensor_scalar(place[:, :, :], mask[:, :, :], -1.0, None, ALU.add))
            link(nc.vector.tensor_scalar(part[:, :, :], slot[:, :, :], 7, None, ALU.arith_shift_right))
            dve.wait_ge(S["w"], 16 * len(loads))
            for c in range(capacity // P):
                link(nc.vector.tensor_scalar(mask[:, :, :], part[:, :, :], float(c), None, ALU.is_equal))
                nc.vector.tensor_tensor(values[:, :, :, c, 0].rearrange("p t e -> p e t"), mask[:, :, :],
                                        number[:, 0:TILES].unsqueeze(1).broadcast_to([P, experts, TILES]), ALU.mult)
                link(nc.vector.tensor_scalar(values[:, :, :, c, 1].rearrange("p t e -> p e t"), mask[:, :, :],
                                             number[:, P:P + 1], None, ALU.mult))


def before_tiles(nc, link, order, rank, tiles_ps, within_ps):
    flat = "p e t -> p (e t)"
    link(nc.vector.memset(order[:, :, 0:1], 0.0))
    link(nc.vector.tensor_copy(rank[:, :, :], tiles_ps[:, :, :]))
    link(nc.vector.tensor_tensor_scan(rank[:, :, :].rearrange(flat), order[:, :, :].rearrange(flat),
                                      rank[:, :, :].rearrange(flat), 0.0, ALU.mult, ALU.add))
    link(nc.vector.tensor_tensor(rank[:, :, :], rank[:, :, :], tiles_ps[:, :, :], ALU.subtract))
    link(nc.vector.tensor_tensor(rank[:, :, :], rank[:, :, :], within_ps[:, :, :], ALU.add))


def shared_and_slots_stage(nc, on, name, dram, experts, slot_chunks, chunks, place, values, combine, token, table):
    ctx, sb, pb, sem = scope(nc)
    with ctx:
        number = sb(f"{name}_number", [P, P + 1])
        number_bf = sb(f"{name}_number_bf", [P, P], BF16)
        onehot = [sb(f"{name}_onehot{k}", [P, experts, P], BF16) for k in range(TPB)]
        tile_values = [sb(f"{name}_values{k}", [P, experts, slot_chunks * 2], BF16) for k in range(TPB)]
        whole = sb(f"{name}_whole", [P, experts, slot_chunks, 2])
        score = sb(f"{name}_score", [P, TILES, experts])
        w_sb = {w: sb(f"{name}_w_{w}", [P, chunks, P]) for w in ("gate", "up", "down")}
        silu, h = ([sb(f"{name}_{w}{c}", [P, COLS]) for c in range(chunks)] for w in ("silu", "h"))
        token_ps = pb(f"{name}_tokenp", [P, experts, slot_chunks * 2])
        gate_ps, up_ps = ([pb(f"{name}_{w}{c}", [P, COLS]) for c in range(chunks)] for w in ("gatep", "upp"))
        down_ps = pb(f"{name}_downp", [P, TPB, D])
        S = {w: sem(f"{name}_{w}") for w in ("loaded", "onehot", "values", "used", "chain", "score", "table", "gate",
                                             "silu", "h", "down", "taken")}
        loads = [(number[:, :], dram["number"])] + [(w_sb[w][:, :, :], dram[f"shared_{w}"]) for w in w_sb]
        block = ctx.enter_context(nc.Block())

        @block.sync
        def _(sp):
            for dst, src in loads:
                sp.dma_start(dst, src).then_inc(S["loaded"], 16)
            rows = table.rearrange("(t p) d -> p t d", p=P)
            sp.dma_start(rows[:, :, 0:D], on.xn[:, :, :]).then_inc(S["table"], 16)
            sp.wait_ge(S["score"], 1)
            sp.dma_start(rows[:, :, D:], score[:, :, :]).then_inc(S["table"], 16)
            sp.wait_ge(S["table"], 32)

        @block.gpsimd
        def _(pool):
            def copy_values(i, k):
                for c in range(TPB):
                    pool.wait_ge(S["used"], i * TPB + c + 1)
                    nc.gpsimd.tensor_copy(
                        tile_values[c][:, :, :],
                        values[:, bass.ds(i * TPB + c, 1), :, :, :].rearrange("p t e c v -> p (t e) (c v)"))\
                        .then_inc(S["values"], 1)

            software_pipeline(nc.gpsimd.Fori, [(copy_values, 0)], BLOCKS)

        @block.vector
        def _(dve):
            nc.vector.tensor_copy(score[:, :, :], combine[:, :, :].rearrange("p e t -> p t e")).then_inc(S["score"], 1)
            dve.wait_ge(S["loaded"], 16 * len(loads))
            nc.vector.tensor_copy(number_bf[:, :], number[:, 0:P]).then_inc(S["chain"], 1)
            dve.wait_ge(S["chain"], 1)

            def mark(t, k):
                dve.wait_ge(S["used"], t + 1)
                nc.vector.tensor_tensor(
                    onehot[k][:, :, :],
                    place[:, :, bass.ds(t, 1)].broadcast_to([P, experts, P]),
                    number_bf[:, :].unsqueeze(1).broadcast_to([P, experts, P]), ALU.is_equal).then_inc(S["onehot"], 1)

            def hidden(c, i, k):
                dve.wait_ge(S["silu"], i * chunks + c + 1)
                dve.wait_ge(S["down"], i)
                nc.vector.tensor_tensor(h[c][:, :], up_ps[c][:, :], silu[c][:, :], ALU.mult).then_inc(S["h"], 1)

            def take(i, k):
                dve.wait_ge(S["down"], i + 1)
                nc.vector.tensor_copy(on.g[:, bass.ts(i, TPB), :], down_ps[:, :, :]).then_inc(S["taken"], 1)

            def marks(lo, hi):
                def fn(i, k):
                    for c in range(lo, hi):
                        mark(i * TPB + c, c)
                        if 0 < c <= chunks:
                            hidden(c - 1, i, k)
                return fn

            software_pipeline(nc.vector.Fori, [(marks(0, 2), 1), (take, 2), (marks(2, TPB), 1)], BLOCKS)
            dve.wait_ge(S["used"], TILES + TPB)
            nc.vector.tensor_copy(whole[:, :, :, :].rearrange("p e c v -> p e (c v)"), token_ps[:, :, :])\
                .then_inc(S["chain"], 1)
            dve.wait_ge(S["chain"], 2)
            nc.vector.scalar_tensor_tensor(token[:, :, :], whole[:, :, :, 0], float(P), whole[:, :, :, 1],
                                           ALU.mult, ALU.add).then_inc(S["chain"], 1)
            dve.wait_ge(S["chain"], 3)

        @block.scalar
        def _(act):
            def silus(i, k):
                for c in range(chunks):
                    act.wait_ge(S["gate"], i * chunks + c + 1)
                    act.wait_ge(S["h"], i * chunks)
                    nc.scalar.activation(silu[c][:, :], gate_ps[c][:, :], ACT.Silu).then_inc(S["silu"], 1)

            software_pipeline(nc.scalar.Fori, [(silus, 1)], BLOCKS)

        @block.tensor
        def _(pe):
            pe.sem_inc(S["used"], TPB)
            pe.wait_ge(S["loaded"], 16 * len(loads))

            def project(c, i, k):
                pe.wait_ge(S["h"], i * chunks)
                cols = on.xnT[:, bass.ts(i, COLS)]
                nc.tensor.matmul(gate_ps[c][:, :], w_sb["gate"][:, c, :], cols, start=True, stop=True)
                nc.tensor.matmul(up_ps[c][:, :], w_sb["up"][:, c, :], cols, start=True, stop=True)\
                    .then_inc(S["gate"], 1)

            def gather(c, i, k):
                t = i * TPB + c
                pe.wait_ge(S["onehot"], t + 1)
                pe.wait_ge(S["values"], t + 1)
                for e in range(experts):
                    ins = nc.tensor.matmul(
                        token_ps[:, e, :], onehot[c][:, e, :], tile_values[c][:, e, :],
                        start=isinstance(t, int) and t == 0 and e == 0, stop=True, skip_group_check=True)
                ins.then_inc(S["used"], 1)

            def down(i, k):
                pe.wait_ge(S["h"], i * chunks + chunks)
                pe.wait_ge(S["taken"], i)
                for t in range(TPB):
                    for c in range(chunks):
                        ins = nc.tensor.matmul(down_ps[:, t, :], h[c][:, t * P:(t + 1) * P], w_sb["down"][:, c, :],
                                               start=(c == 0), stop=(c == chunks - 1))
                ins.then_inc(S["down"], 1)

            def block_of(i, k):
                for c in range(TPB):
                    if c < chunks:
                        project(c, i, k)
                    if c == chunks + 1:
                        down(i, k)
                    gather(c, i, k)

            software_pipeline(nc.tensor.Fori, [(block_of, 1)], BLOCKS)


def chosen_experts_stage(nc, on, name, dram, experts, chunks, token, rows, table, sums):
    ctx, sb, pb, sem = scope(nc)
    with ctx:
        RT = rows // P
        W = table.shape[1]
        kinds = ("gate", "up", "down", "bias", "down_b")
        widths = {"bias": [P, 1, 2 * chunks], "down_b": [P, 1, D]}
        w_sb = {w: [sb(f"{name}_w_{w}{k}", widths.get(w, [P, chunks, P])) for k in range(2)] for w in kinds}
        taken = [sb(f"{name}_taken{k}", [P, RT], U32) for k in range(2)]
        given = [sb(f"{name}_given{k}", [P, RT], U32) for k in range(2)]
        xg = [sb(f"{name}_xg{k}", [P, RT, W]) for k in range(2)]
        xinT = [sb(f"{name}_xinT{k}", [P, rows]) for k in range(2)]
        weight = [sb(f"{name}_weight{k}", [P, RT]) for k in range(2)]
        silu = [sb(f"{name}_silu{k}", [P, rows]) for k in range(2)]
        h = [[sb(f"{name}_h{k}_{c}", [P, rows]) for c in range(chunks)] for k in range(2)]
        scaled = [sb(f"{name}_scaled{k}", [P, RT, D]) for k in range(2)]
        turn_ps = pb(f"{name}_turnp", [P, rows])
        gate_ps = [pb(f"{name}_gatep{k}", [P, rows]) for k in range(2)]
        up_ps = [pb(f"{name}_upp{k}", [P, rows]) for k in range(2)]
        down_ps = [pb(f"{name}_downp{k}", [P, RT, D]) for k in range(2)]
        w_loaded = [sem(f"{name}_w_loaded{k}") for k in range(2)]
        S = {w: sem(f"{name}_{w}") for w in ("init", "taken", "going", "turned", "xinT", "weight", "proj", "silu",
                                             "h", "down", "scaled", "given", "added",
                                             "biased")}
        gathered = [sem(f"{name}_gathered{k}") for k in range(2)]
        block = ctx.enter_context(nc.Block())

        def gathers(e, k):
            return (e // 2 + 1) * (16 * RT) if isinstance(e, int) else (e - k) * (8 * RT) + 16 * RT

        def pipeline(fori, *steps):
            software_pipeline(fori, list(steps), experts)

        def row_of(kind, e):
            return dram[kind][bass.ds(e, 1), :, :]

        @block.sync
        def _(sp):
            sp.dma_start(sums.rearrange("(t p) d -> p t d", p=P), on.g[:, :, :]).then_inc(S["init"], 16)

            def load(e, k):
                sp.wait_ge(S["scaled"], e + 1)
                for w in ("gate", "up", "down"):
                    sp.dma_start(w_sb[w][k][:, :, :], row_of(w, e).rearrange("e p (c f) -> (e p) c f", f=P))\
                        .then_inc(w_loaded[k], 16)
                for w in ("bias", "down_b"):
                    sp.dma_start(w_sb[w][k][:, :, :], row_of(w, e).rearrange("e p b -> p e b"))\
                        .then_inc(w_loaded[k], 16)

            pipeline(nc.sync.Fori, (load, 0))
            sp.wait_ge(S["added"], 16 * RT * experts)

        @block.gpsimd
        def _(pool):
            def gather(e, k):
                pool.wait_ge(S["weight"], e + 1)
                pool.wait_ge(S["turned"], e + 1)
                pool.wait_ge(S["taken"], e + 1)
                pool.sem_inc(S["going"], 1)
                for c in range(RT):
                    nc.gpsimd.indirect_dma_start(
                        out=xg[k][:, c, :], out_offset=None, in_=table,
                        in_offset=bass.IndirectOffsetOnAxis(ap=taken[k][:, c:c + 1], axis=0))\
                        .then_inc(gathered[k], 16)

            def scatter(e, k):
                pool.wait_ge(S["init"], 16)
                pool.wait_ge(S["added"], e * (16 * RT))
                pool.wait_ge(S["given"], e + 1)
                pool.sem_inc(S["going"], 1)
                for c in range(RT):
                    nc.gpsimd.indirect_dma_start(
                        out=sums, out_offset=bass.IndirectOffsetOnAxis(ap=given[k][:, c:c + 1], axis=0),
                        in_=scaled[k][:, c, :], in_offset=None, compute_op=ALU.add).then_inc(S["added"], 16)

            pipeline(nc.gpsimd.Fori, (gather, 0), (scatter, 3))

        @block.tensor
        def _(pe):
            pe.sem_inc(S["turned"], 2)
            pe.sem_inc(S["down"], 2)

            def turn(e, k):
                pe.wait_ge(gathered[k], gathers(e, k))
                pe.wait_ge(S["xinT"], e + 1)
                for c in range(RT):
                    ins = nc.tensor.transpose(turn_ps[:, c * P:(c + 1) * P], xg[k][:, c, 0:D], on.ident[:, :])
                ins.then_inc(S["turned"], 1)

            def project(e, k):
                pe.wait_ge(w_loaded[k], (e // 2 + 1) * 80 if isinstance(e, int) else (e - k) * 40 + 80)
                pe.wait_ge(S["xinT"], e + 2)
                for c in range(chunks):
                    n, b = e * chunks + c, c % 2
                    pe.wait_ge(S["silu"], n + 1)
                    nc.tensor.matmul(gate_ps[b][:, :], w_sb["gate"][k][:, c, :], xinT[k][:, :], start=True, stop=True)
                    pe.wait_ge(S["h"], n + 1)
                    nc.tensor.matmul(up_ps[b][:, :], w_sb["up"][k][:, c, :], xinT[k][:, :], start=True, stop=True)\
                        .then_inc(S["proj"], 1)

            def down(e, k):
                pe.wait_ge(S["h"], e * chunks + (chunks + 2))
                pe.wait_ge(S["scaled"], e + 1)
                for t in range(RT):
                    for c in range(chunks):
                        ins = nc.tensor.matmul(down_ps[k][:, t, :], h[k][c][:, t * P:(t + 1) * P],
                                               w_sb["down"][k][:, c, :], start=(c == 0), stop=(c == chunks - 1))
                ins.then_inc(S["down"], 1)

            pipeline(nc.tensor.Fori, (down, 3), (project, 2), (turn, 1))

        @block.scalar
        def _(act):
            act.sem_inc(S["xinT"], 1)
            act.sem_inc(S["silu"], 2)

            def copy_x(e, k):
                act.wait_ge(S["turned"], e + 3)
                act.wait_ge(S["proj"], e * chunks - chunks if isinstance(e, int) and e > 0 or not isinstance(e, int)
                            else 0)
                nc.scalar.activation(xinT[k][:, :], turn_ps[:, :], ACT.Copy).then_inc(S["xinT"], 1)

            def silus(e, k):
                for c in range(chunks):
                    n, b = e * chunks + c, c % 2
                    act.wait_ge(S["proj"], n + 1)
                    act.wait_ge(S["h"], n + 1)
                    nc.scalar.activation(silu[b][:, :], gate_ps[b][:, :], ACT.Silu,
                                         bias=w_sb["bias"][k][:, 0, c:c + 1]).then_inc(S["silu"], 1)

            pipeline(nc.scalar.Fori, (silus, 2), (copy_x, 1))

        @block.vector
        def _(dve):
            dve.sem_inc(S["weight"], 2)
            dve.sem_inc(S["scaled"], 2)
            dve.sem_inc(S["h"], 2)

            def take(e, k):
                if not isinstance(e, int) or e >= 2:
                    dve.wait_ge(gathered[k], gathers(e, k) - 16 * RT)
                nc.vector.tensor_copy(taken[k][:, :], token[:, bass.ds(e, 1), :]).then_inc(S["taken"], 1)

            def weights_of(e, k):
                dve.wait_ge(gathered[k], gathers(e, k))
                dve.wait_ge(S["scaled"], e + 1)
                nc.vector.tensor_copy(weight[k][:, :], xg[k][:, :, bass.ds(e + D, 1)]).then_inc(S["weight"], 1)

            def hidden(e, k):
                dve.wait_ge(S["down"], e + 1)
                for c in range(chunks):
                    n, b = e * chunks + c, c % 2
                    dve.wait_ge(S["silu"], n + 3)
                    nc.vector.scalar_tensor_tensor(h[k][c][:, :], up_ps[b][:, :],
                                                   w_sb["bias"][k][:, 0, chunks + c:chunks + c + 1], silu[b][:, :],
                                                   ALU.add, ALU.mult).then_inc(S["h"], 1)

            def scale(e, k):
                dve.wait_ge(S["down"], e + 3)
                dve.wait_ge(S["weight"], e + 3)
                if not isinstance(e, int) or e >= 2:
                    dve.wait_ge(S["added"], e * (16 * RT) - 16 * RT)
                nc.vector.tensor_tensor(scaled[k][:, :, :], down_ps[k][:, :, :],
                                        w_sb["down_b"][k][:, :, :].broadcast_to([P, RT, D]), ALU.add)\
                    .then_inc(S["biased"], 1)
                dve.wait_ge(S["biased"], e + 1)
                for t in range(RT):
                    ins = nc.vector.tensor_scalar(scaled[k][:, t, :], scaled[k][:, t, :], weight[k][:, t:t + 1],
                                                  None, ALU.mult)
                ins.then_inc(S["scaled"], 1)
                nc.vector.tensor_copy(given[k][:, :], token[:, bass.ds(e, 1), :]).then_inc(S["given"], 1)

            pipeline(nc.vector.Fori, (take, 0), (scale, 3), (hidden, 2), (weights_of, 1))


def choice_experts(nc, on, name, dram, experts, capacity, chunks):
    RT = capacity // P
    table = nc.dram_tensor(f"{name}_table", (TOKENS, D + experts), F32, kind="Internal").ap()
    sums = nc.dram_tensor(f"{name}_sums", (TOKENS, D), F32, kind="Internal").ap()
    with nc.sbuf_tensor(f"{name}_combine", [P, experts, TILES], F32) as combine, \
            nc.sbuf_tensor(f"{name}_token", [P, experts, RT], U32) as token:
        with nc.sbuf_tensor(f"{name}_place", [P, experts, TILES], BF16) as place, \
                nc.sbuf_tensor(f"{name}_values", [P, TILES, experts, RT, 2], BF16) as values:
            choice_route_stage(nc, on, f"{name}r", dram, experts, capacity, combine, place, values)
            shared_and_slots_stage(nc, on, f"{name}t", dram, experts, RT, dram["shared_gate"].shape[1], place, values,
                                   combine, token, table)
        chosen_experts_stage(nc, on, f"{name}e", dram, experts, chunks, token, capacity, table, sums)
    return sums


class Chip:
    pass


def persistent(nc, ctx):
    def sb(name, shape, dt=F32):
        return ctx.enter_context(nc.sbuf_tensor(name, shape, dt))

    on = Chip()
    on.x = sb("x_sb", [P, TILES, D])
    on.xn = sb("xn_sb", [P, TILES, D])
    on.xnT = sb("xnT_sb", [P, TOKENS])
    on.s = sb("s_sb", [P, TILES, D])
    on.g = sb("g_sb", [P, TILES, D])
    on.q = on.g
    on.k = on.s
    on.v = sb("v_sb", [P, TILES, D])
    on.ident = sb("ident", [P, P])
    on.ident_bf = sb("ident_bf", [P, P], BF16)
    on.ones = sb("ones", [P, P])
    on.causal = sb("causal", [P, P])
    on.mask_kq = sb("mask_kq", [P, P], BF16)
    on.mask_qk = sb("mask_qk", [P, P], BF16)
    return on


def final_stage(nc, on, g, out):
    ctx, sb, pb, sem = scope(nc)
    with ctx:
        s_loaded = [sem(f"out_loaded{i}") for i in range(BLOCKS)]
        s_gate, s_prod, s_added, s_stored = (sem(f"out_{w}") for w in ("silu", "prod", "added", "stored"))
        block = ctx.enter_context(nc.Block())

        def block_of(t, i):
            return t[:, i * TPB:(i + 1) * TPB, :].rearrange("p t d -> p (t d)")

        @block.scalar
        def _(act):
            for i in range(BLOCKS):
                act.wait_ge(s_loaded[i], 16)
                nc.scalar.activation(block_of(on.g, i), block_of(on.g, i), ACT.Silu).then_inc(s_gate, 1)

        @block.vector
        def _(dve):
            for i in range(BLOCKS):
                dve.wait_ge(s_gate, i + 1)
                nc.vector.tensor_tensor(block_of(on.g, i), block_of(on.g, i), block_of(on.s, i), ALU.mult)\
                    .then_inc(s_prod, 1)
                dve.wait_ge(s_prod, i + 1)
                nc.vector.tensor_tensor(block_of(on.x, i), block_of(on.x, i), block_of(on.g, i), ALU.add)\
                    .then_inc(s_added, 1)

        @block.sync
        def _(sp):
            rows, g_rows = (a.rearrange("(t p) d -> p t d", p=P) for a in (out, g))
            for i in range(BLOCKS):
                t = slice(i * TPB, (i + 1) * TPB)
                sp.dma_start(on.g[:, t, :], g_rows[:, t, :]).then_inc(s_loaded[i], 16)
            for i in range(BLOCKS):
                sp.wait_ge(s_added, i + 1)
                t = slice(i * TPB, (i + 1) * TPB)
                sp.dma_start(rows[:, t, :], on.x[:, t, :]).then_inc(s_stored, 16)
            sp.wait_ge(s_stored, 16 * BLOCKS)


def gated_mixers_kernel(nc, dram, out):
    def of(layer):
        return {name[len(layer) + 1:]: dram[name] for name in dram if name.startswith(layer + "_")}

    with ExitStack() as ctx:
        on = persistent(nc, ctx)
        constants_stage(nc, on, dram)
        layernorm_stage(nc, on, "n0", on.x, on.xn, on.xnT, False)
        project_stage(nc, on, "p0", of("a0"), 16, "softplus")
        attention_stage(nc, on, "a0", of("a0"), 16, None)
        integer_ffn(nc, on, "f0", of("f0"), 384)
        layernorm_stage(nc, on, "n1", on.x, on.xn, on.xnT, True)
        project_stage(nc, on, "p1", of("a1"), 16, "rope")
        attention_stage(nc, on, "a1", of("a1"), 16, 8 ** -0.5)
        centroid_experts(nc, on, "f1", of("f1"), 8, 4)
        layernorm_stage(nc, on, "n2", on.x, on.xn, on.xnT, True)
        latent_attention(nc, on, "a2", of("a2"), 8, 2)
        top_experts(nc, on, "f2", of("f2"), 32, 6)
        layernorm_stage(nc, on, "n3", on.x, on.xn, on.xnT, True)
        channel_attention_stage(nc, on, "a3", of("a3"), 16, 64)
        sums = choice_experts(nc, on, "f3", of("f3"), 16, 512, 4)
        final_stage(nc, on, sums, out)


def rope_tables():
    pos = np.arange(SEQ, dtype=np.float32)[:, None]
    turn = np.arange(0, 8, 2, dtype=np.float32) / np.float32(8)
    theta = pos * np.exp(-turn * np.float32(np.log(10000.0)))
    tables = np.stack([np.repeat(np.cos(theta), 2, 1), np.repeat(np.sin(theta), 2, 1)]).astype(np.float32)
    return tables.reshape(2, QT, P, 8).transpose(2, 0, 1, 3)


def every_partition(a):
    return np.tile(a[None], (P,) + (1,) * a.ndim)


def row_chunks(w):
    return w.reshape(-1, P, w.shape[1]).transpose(1, 0, 2)


def layouts(i):
    d = {"x": i["L0_attn_x"].reshape(TOKENS, D)}
    for layer, mixer in (("a0", "L0_attn_"), ("a1", "L1_attn_")):
        d[f"{layer}_w"] = np.concatenate([i[mixer + w].T for w in ("Wq", "Wk", "Wv")], 1)
        d[f"{layer}_wo"] = i[mixer + "Wo"].T
        d[f"{layer}_bo"] = every_partition(i[mixer + "bo"])
    d["a0_bias"] = every_partition(np.stack([i["L0_attn_bq"], i["L0_attn_bk"], i["L0_attn_bv"]]))
    for w in ("gate", "up"):
        d[f"f0_{w}"] = i[f"L0_ffn_w_{w}"].T.reshape(P, 3, P)
    d["f0_down"] = row_chunks(i["L0_ffn_w_down"].T)

    d["a1_cos_sin"] = rope_tables()
    d["a1_gamma_beta"] = every_partition(np.stack([np.stack([i[f"L1_attn_{w}_{p}"] for w in "qk"])
                                                   for p in ("gamma", "beta")]))
    d["f1_centT"] = i["L1_ffn_centroids"].T
    d["f1_b2"] = i["L1_ffn_b2"]
    d["f1_ln_g"], d["f1_ln_b"] = i["L1_ffn_ln_g"].T, i["L1_ffn_ln_b"].T
    d["f1_rank_w"] = every_partition(8 - np.arange(8, dtype=np.float32))
    d["f1_w1"] = i["L1_ffn_w1"].transpose(1, 0, 2)
    d["f1_b1"] = i["L1_ffn_b1"].reshape(8, 4, P).transpose(2, 0, 1).reshape(P, 32)
    d["f1_w2"] = i["L1_ffn_w2"].reshape(8, 4, P, P).transpose(0, 2, 1, 3).reshape(8, P, 512)

    d["a2_wqT"] = i["L2_attn_wq"].reshape(P, 8, P).transpose(2, 1, 0)
    d["a2_wo"] = row_chunks(i["L2_attn_wo"])
    d["a2_up"] = np.stack([i["L2_attn_wk_up"].T, i["L2_attn_wv_up"].T], 1)
    d["a2_w_down"] = np.concatenate([i["L2_attn_wk_down"], i["L2_attn_wv_down"]], 1)
    den_cols = np.zeros((P, 2, 32), np.float32)
    den_cols[:, 0, 0] = 1
    den_cols[:, 1, 1] = 1
    d["a2_den_cols"] = den_cols
    gate_up = i["L2_ffn_gate_up_proj"]
    for w, half in (("gate", slice(0, 64)), ("up", slice(64, 128))):
        d[f"f2_pair_{w}"] = gate_up[:, half].reshape(16, P, P).transpose(0, 2, 1)
    d["f2_pair_down"] = i["L2_ffn_down_proj"].transpose(0, 2, 1).reshape(16, P, P)
    d["f2_routerT"] = i["L2_ffn_router_weight"].T
    d["f2_bias"] = every_partition(i["L2_ffn_e_score_bias"])
    for w in ("gate", "up", "down"):
        d[f"f2_shared_{w}"] = i[f"L2_ffn_shared_{w}_w"].T

    wq, wk, wv = (i["L3_attn_w_qkv"][:, j * 1024:(j + 1) * 1024] for j in range(3))
    d["a3_w_q"], d["a3_w_k"] = wq.reshape(P, 8, P), wk.reshape(P, 8, P)
    d["a3_w_vT"] = row_chunks(wv.T)
    d["a3_w_out"] = row_chunks(i["L3_attn_w_out"])
    d["a3_temp"] = np.repeat(i["L3_attn_temperature"].reshape(8, 2).T, 64, axis=0)
    d["a3_gamma"] = every_partition(i["L3_attn_gamma"])
    number = np.concatenate([np.tile(np.arange(P), (P, 1)), np.arange(P)[:, None]], 1).astype(np.float32)
    d["f1_number"] = d["f3_number"] = number
    d["f3_gateT"] = i["L3_ffn_gate_w"].T
    for w in ("gate", "up"):
        d[f"f3_shared_{w}"] = i[f"L3_ffn_sh_{w}_w"].T.reshape(P, 2, P)
    d["f3_shared_down"] = row_chunks(i["L3_ffn_sh_down_w"].T)
    d["f3_gate"], d["f3_up"] = i["L3_ffn_gw"].transpose(0, 2, 1), i["L3_ffn_up_w"].transpose(0, 2, 1)
    d["f3_down"] = i["L3_ffn_down_w"].transpose(0, 2, 1).reshape(16, 4, P, P).transpose(0, 2, 1, 3).reshape(16, P, 512)
    d["f3_bias"] = np.concatenate([i["L3_ffn_gb"].reshape(16, 4, P), i["L3_ffn_up_b"].reshape(16, 4, P)], 1)\
        .transpose(0, 2, 1)
    d["f3_down_b"] = every_partition(i["L3_ffn_down_b"]).transpose(1, 0, 2)
    return d


def kernel(**inputs):
    import concourse.bacc as _bacc
    from concourse.bass_utils import run_bass_kernel_spmd as _run

    arrays = {f"in_{n}": np.ascontiguousarray(a) for n, a in
              layouts({n: np.asarray(a) for n, a in inputs.items()}).items()}
    nc = _bacc.Bacc("TRN2", target_bir_lowering=False, num_devices=1)
    dram = {n[3:]: nc.dram_tensor(n, a.shape, mybir.dt.from_np(a.dtype), kind="ExternalInput").ap()
            for n, a in arrays.items()}
    out = nc.dram_tensor("out", (TOKENS, D), F32, kind="ExternalOutput").ap()
    gated_mixers_kernel(nc, dram, out)
    r = _run(nc, [arrays], core_ids=[0])
    return r.results[0]["out"].reshape(BATCH, SEQ, D)
```
